# Optimizing a Trainium2 kernel written in Bass

```python
import numpy as np
import jax
import jax.numpy as jnp

def _softmax(x, axis=-1):
    return jax.nn.softmax(x, axis=axis)

def _gelu(x):
    return jax.nn.gelu(x, approximate=True)

def _silu(x):
    return jax.nn.silu(x)

def _sigmoid(x):
    return jax.nn.sigmoid(x)

def _layernorm(x, axis=-1, eps=1e-05):
    m = jnp.mean(x, axis=axis, keepdims=True)
    v = jnp.var(x, axis=axis, keepdims=True)
    return (x - m) / jnp.sqrt(v + eps)

def _scatter_add(tgt, idx, src, axis=0):
    return tgt.at[idx].add(src)

def _segment_sum(src, seg, n):
    return jax.ops.segment_sum(src, seg, n)
kernel_name = 'mk_xattn_ffn_d4_seqx_r8_df6a52'

def setup_inputs(seed: int=0):
    np.random.seed(seed)
    _w = jnp.asarray

    def _rec_inputs():
        import jax
        import jax.numpy as jnp
        _rk = jax.random.key(seed)
        x = -0.0003929 + 0.9999 * jax.random.normal(jax.random.fold_in(_rk, 1), (8, 56, 256), jnp.float32)
        _lenS = 56 - jax.random.randint(jax.random.fold_in(_rk, 7), (8,), 0, max(1, 56 // 4) + 1, jnp.int32)
        _lenS2 = 1500 - jax.random.randint(jax.random.fold_in(_rk, 8), (8,), 0, max(1, 1500 // 4) + 1, jnp.int32)
        _ctx_2048P = jax.random.normal(jax.random.fold_in(_rk, 11), (8, 16, 256), jnp.float32)
        _ctx_2048c = jax.random.dirichlet(jax.random.fold_in(_rk, 511), 0.3 * jnp.ones((16,), jnp.float32), (8, 1500))
        _ctx_2048t = jnp.einsum('bsk,bkd->bsd', _ctx_2048c, _ctx_2048P)
        _ctx_2048t = _ctx_2048t * jax.lax.rsqrt(jnp.mean(jnp.square(_ctx_2048t)) + 1e-12) * 0.953939
        ctx_2048 = -1.39393e-06 + 0.999914 * (_ctx_2048t + 0.3 * jax.random.normal(jax.random.fold_in(_rk, 611), (8, 1500, 256), jnp.float32))
        itok_BxS_0_1023 = jax.random.randint(jax.random.fold_in(_rk, 12), (8, 56), 0, 128, jnp.int32)
        _validS = jnp.arange(56)[None, :] < _lenS[:, None]
        _validS2 = jnp.arange(1500)[None, :] < _lenS2[:, None]
        _causal = jnp.tril(jnp.ones((56, 56), dtype=bool))
        mask_BxS2_bk0 = jnp.logical_not(jnp.broadcast_to(_validS2[:, :], (8, 1500)))
        mask_BxS2_ff1 = jnp.where(jnp.ones((8, 1500), dtype=bool), 1.0, 0.0).astype(jnp.float32)
        return (x, ctx_2048, itok_BxS_0_1023, mask_BxS2_bk0, mask_BxS2_ff1)
    x, ctx_2048, itok_BxS_0_1023, mask_BxS2_bk0, mask_BxS2_ff1 = _rec_inputs()

    def _L0_xattn_setup():
        import jax, jax.numpy as jnp
        import numpy as np
        B, Lq, Lk = (2, 512, 128)
        Q_DIM, KV_DIM = (256, 256)
        H, HD = (16, 128)
        KVC, QC, R = (64, 96, 64)
        LOOKBACK = 8
        NEG = -1e+30

        def _rope(x, L):
            half = x.shape[-1] // 2
            inv_freq = 1.0 / 10000.0 ** (jnp.arange(half, dtype=jnp.float32) / half)
            ang = jnp.arange(L, dtype=jnp.float32)[:, None] * inv_freq
            cos, sin = (jnp.cos(ang), jnp.sin(ang))
            x1, x2 = (x[..., :half], x[..., half:])
            return jnp.concatenate([x1 * cos - x2 * sin, x1 * sin + x2 * cos], axis=-1)
        key = jax.random.key(seed)
        ks = jax.random.split(key, 11)

        def w(k, shape, fan_in):
            return jax.random.normal(k, shape, jnp.float32) / np.sqrt(fan_in).astype(np.float32)
        return {'q': jax.random.normal(ks[0], (B, Lq, Q_DIM), jnp.float32), 'kv': jax.random.normal(ks[1], (B, Lk, KV_DIM), jnp.float32), 'seg_id': jnp.sort(jax.random.randint(ks[2], (B, Lq), 0, Lk), axis=-1), 'W_kvc': w(ks[3], (KV_DIM, KVC), KV_DIM), 'W_dq': w(ks[4], (Q_DIM, QC), Q_DIM), 'W_uq': w(ks[5], (QC, H * HD), QC), 'W_qr': w(ks[6], (QC, H * R), QC), 'W_uk': w(ks[7], (KVC, H * HD), KVC), 'W_kr': w(ks[8], (KVC, R), KVC), 'W_uv': w(ks[9], (KVC, H * HD), KVC), 'W_o': w(ks[10], (H * HD, Q_DIM), H * HD)}
    _L0_xattn_all = _L0_xattn_setup()
    _L0_xattn_in = {k: v for k, v in _L0_xattn_all.items() if k in ('W_kvc', 'W_dq', 'W_uq', 'W_qr', 'W_uk', 'W_kr', 'W_uv', 'W_o')}
    del _L0_xattn_all

    def _L0_ffn_setup():
        import jax, jax.numpy as jnp
        import numpy as np
        D_MODEL = 256
        D_FF = 1024
        BATCH = 4
        SEQ = 256
        MAX_EXP = 4
        NUM_BITS = 8
        C_CHUNKS = 2
        SCALE = 0.1

        def _pow2_ternary(key, out_dim, in_dim, max_exp):
            k1, k2 = jax.random.split(key)
            t = jax.random.randint(k1, (out_dim, in_dim), -1, 2).astype(jnp.float32)
            e = jax.random.randint(k2, (out_dim, in_dim), 0, max_exp + 1).astype(jnp.float32)
            return t * jnp.exp2(-e)

        def _lookup_act(h):
            total_bits = NUM_BITS * C_CHUNKS
            qmax = 2 ** (total_bits - 1) - 1
            qmin = -2 ** (total_bits - 1)
            q = jnp.clip(jnp.round(h / SCALE), qmin, qmax)
            return jax.nn.gelu(q * SCALE)
        key = jax.random.key(seed)
        kx, k1, k2 = jax.random.split(key, 3)
        x = jax.random.normal(kx, (BATCH, SEQ, D_MODEL), dtype=jnp.float32)
        W1 = _pow2_ternary(k1, D_FF, D_MODEL, MAX_EXP)
        W2 = _pow2_ternary(k2, D_MODEL, D_FF, MAX_EXP)
        return {'x': x, 'W1': W1, 'W2': W2}
    _L0_ffn_all = _L0_ffn_setup()
    _L0_ffn_in = {k: v for k, v in _L0_ffn_all.items() if k in ('W1', 'W2')}
    del _L0_ffn_all

    def _L1_xattn_setup():
        import jax, jax.numpy as jnp
        import numpy as np
        key = jax.random.key(seed)
        k1, k2, k3 = jax.random.split(key, 3)
        B, S, D, M = (8, 256, 256, 128)
        hidden_states = jax.random.normal(k1, (B, S, D), dtype=jnp.float32)
        memory_tokens = jax.random.normal(k2, (B, M, D), dtype=jnp.float32)
        memory_mask = jax.random.randint(k3, (B, M), 0, 2).astype(jnp.bool_)
        return {'hidden_states': hidden_states, 'memory_tokens': memory_tokens, 'memory_mask': memory_mask}
    _L1_xattn_all = _L1_xattn_setup()
    _L1_xattn_in = {k: v for k, v in _L1_xattn_all.items() if k in ()}
    del _L1_xattn_all

    def _L1_ffn_setup():
        import jax, jax.numpy as jnp
        import numpy as np
        B, S, H = (4, 128, 256)
        E, K, I, SI = (16, 4, 176, 704)

        def _silu_mul(gu, inter):
            return jax.nn.silu(gu[:, :inter]) * gu[:, inter:]
        key = jax.random.key(seed)
        ks = jax.random.split(key, 7)
        s = 0.02
        return {'hidden_states': jax.random.normal(ks[0], (B, S, H), jnp.float32), 'gate_w': jax.random.normal(ks[1], (E, H), jnp.float32) * s, 'expert_gate_up': jax.random.normal(ks[2], (E, 2 * I, H), jnp.float32) * s, 'expert_down': jax.random.normal(ks[3], (E, H, I), jnp.float32) * s, 'shared_gate_up': jax.random.normal(ks[4], (2 * SI, H), jnp.float32) * s, 'shared_down': jax.random.normal(ks[5], (H, SI), jnp.float32) * s, 'shared_gate_vec': jax.random.normal(ks[6], (1, H), jnp.float32) * s}
    _L1_ffn_all = _L1_ffn_setup()
    _L1_ffn_in = {k: v for k, v in _L1_ffn_all.items() if k in ('gate_w', 'expert_gate_up', 'expert_down', 'shared_gate_up', 'shared_down', 'shared_gate_vec')}
    del _L1_ffn_all

    def _L2_xattn_setup():
        import jax, jax.numpy as jnp
        import numpy as np
        H = 256
        NH = 16
        HD = H // NH
        FD = 64
        key = jax.random.key(seed)
        ks = jax.random.split(key, 12)
        B, S = (4, 512)
        s = 1.0 / np.sqrt(H)
        sf = 1.0 / np.sqrt(HD)
        return {'query': jax.random.normal(ks[0], (B, S, H), jnp.float32), 'key': jax.random.normal(ks[1], (B, S, H), jnp.float32), 'value': jax.random.normal(ks[2], (B, S, H), jnp.float32), 'attention_mask': jnp.ones((B, S), jnp.float32), 'Wq': jax.random.normal(ks[3], (H, H), jnp.float32) * s, 'bq': jnp.zeros((H,), jnp.float32), 'Wk': jax.random.normal(ks[4], (H, H), jnp.float32) * s, 'bk': jnp.zeros((H,), jnp.float32), 'Wv': jax.random.normal(ks[5], (H, H), jnp.float32) * s, 'bv': jnp.zeros((H,), jnp.float32), 'Wqf': jax.random.normal(ks[6], (FD, HD), jnp.float32) * sf, 'Wkf': jax.random.normal(ks[7], (FD, HD), jnp.float32) * sf, 'Wo': jax.random.normal(ks[8], (H, H), jnp.float32) * s, 'bo': jnp.zeros((H,), jnp.float32)}
    _L2_xattn_all = _L2_xattn_setup()
    _L2_xattn_in = {k: v for k, v in _L2_xattn_all.items() if k in ('Wq', 'bq', 'Wk', 'bk', 'Wv', 'bv', 'Wqf', 'Wkf', 'Wo', 'bo')}
    del _L2_xattn_all

    def _L2_ffn_setup():
        import jax, jax.numpy as jnp
        import numpy as np
        FP8_MAX = 448.0
        GLOBAL_DIV = 448.0 * 6.0

        def _fp8(x):
            return x.astype(jnp.float8_e4m3fn).astype(jnp.float32)

        def _reorder_quantize_x(x, idx):
            scale = jnp.max(jnp.abs(x)) / GLOBAL_DIV
            xr = (x / scale)[:, idx]
            scale_x = jnp.max(jnp.abs(xr), axis=1, keepdims=True) / FP8_MAX
            qx = _fp8(xr / scale_x)
            return (qx, scale_x, scale)

        def _qlinear(qx, scale_x, scale, W, idx, out_idx=None):
            Wr = W[:, idx]
            w_scale = jnp.max(jnp.abs(Wr), axis=1, keepdims=True) / FP8_MAX
            qw = _fp8(Wr / w_scale)
            y = qx * scale_x @ (qw * w_scale).T * scale
            if out_idx is not None:
                y = y[:, out_idx]
            return y
        key = jax.random.key(seed)
        ks = jax.random.split(key, 6)
        B, S, H, I = (2, 128, 256, 704)
        return {'x': jax.random.normal(ks[0], (B, S, H), jnp.float32), 'w_gate': jax.random.normal(ks[1], (I, H), jnp.float32) * 0.02, 'w_up': jax.random.normal(ks[2], (I, H), jnp.float32) * 0.02, 'w_down': jax.random.normal(ks[3], (H, I), jnp.float32) * 0.02, 'up_reorder_index': jax.random.permutation(ks[4], jnp.arange(H, dtype=jnp.int64)), 'down_reorder_index': jax.random.permutation(ks[5], jnp.arange(I, dtype=jnp.int64))}
    _L2_ffn_all = _L2_ffn_setup()
    _L2_ffn_in = {k: v for k, v in _L2_ffn_all.items() if k in ('w_gate', 'w_up', 'w_down', 'up_reorder_index', 'down_reorder_index')}
    del _L2_ffn_all

    def _L3_xattn_setup():
        import jax, jax.numpy as jnp
        import numpy as np
        B, S, D = (8, 128, 256)
        H, HD = (16, 128)
        key = jax.random.key(seed)
        ks = jax.random.split(key, 6)
        fan_in = 1.0 / np.sqrt(D)
        return {'inputs_q': jax.random.normal(ks[0], (B, S, D), jnp.float32), 'inputs_kv': jax.random.normal(ks[1], (B, S, D), jnp.float32), 'Wq': jax.random.normal(ks[2], (D, H * HD), jnp.float32) * fan_in, 'Wk': jax.random.normal(ks[3], (D, H * HD), jnp.float32) * fan_in, 'Wv': jax.random.normal(ks[4], (D, H * HD), jnp.float32) * fan_in, 'Wo': jax.random.normal(ks[5], (H * HD, D), jnp.float32) * (1.0 / np.sqrt(H * HD))}
    _L3_xattn_all = _L3_xattn_setup()
    _L3_xattn_in = {k: v for k, v in _L3_xattn_all.items() if k in ('Wq', 'Wk', 'Wv', 'Wo')}
    del _L3_xattn_all

    def _L3_ffn_setup():
        import jax, jax.numpy as jnp
        import numpy as np
        from jax import lax
        E = 8
        K = 2
        H = 256
        I = 512
        B, S = (2, 256)
        SCALE = 0.02

        def _silu_and_mul(gu):
            g, u = jnp.split(gu, 2, axis=-1)
            return jax.nn.silu(g) * u
        key = jax.random.key(seed)
        ks = jax.random.split(key, 6)
        return {'hidden_states': jax.random.normal(ks[0], (B, S, H), dtype=jnp.float32), 'gate_w': jax.random.normal(ks[1], (H, E), dtype=jnp.float32) * SCALE, 'w_gate_up': jax.random.normal(ks[2], (E, H, 2 * I), dtype=jnp.float32) * SCALE, 'w_down': jax.random.normal(ks[3], (E, I, H), dtype=jnp.float32) * SCALE, 'shared_gate_up': jax.random.normal(ks[4], (H, 2 * I), dtype=jnp.float32) * SCALE, 'shared_down': jax.random.normal(ks[5], (I, H), dtype=jnp.float32) * SCALE}
    _L3_ffn_all = _L3_ffn_setup()
    _L3_ffn_in = {k: v for k, v in _L3_ffn_all.items() if k in ('gate_w', 'w_gate_up', 'w_down', 'shared_gate_up', 'shared_down')}
    del _L3_ffn_all
    return {'x': x, 'ctx_2048': ctx_2048, 'itok_BxS_0_1023': itok_BxS_0_1023, 'mask_BxS2_bk0': mask_BxS2_bk0, 'mask_BxS2_ff1': mask_BxS2_ff1, 'L0_xattn_W_kvc': _L0_xattn_in['W_kvc'], 'L0_xattn_W_dq': _L0_xattn_in['W_dq'], 'L0_xattn_W_uq': _L0_xattn_in['W_uq'], 'L0_xattn_W_qr': _L0_xattn_in['W_qr'], 'L0_xattn_W_uk': _L0_xattn_in['W_uk'], 'L0_xattn_W_kr': _L0_xattn_in['W_kr'], 'L0_xattn_W_uv': _L0_xattn_in['W_uv'], 'L0_xattn_W_o': _L0_xattn_in['W_o'], 'L0_ffn_W1': _L0_ffn_in['W1'], 'L0_ffn_W2': _L0_ffn_in['W2'], 'L1_ffn_gate_w': _L1_ffn_in['gate_w'], 'L1_ffn_expert_gate_up': _L1_ffn_in['expert_gate_up'], 'L1_ffn_expert_down': _L1_ffn_in['expert_down'], 'L1_ffn_shared_gate_up': _L1_ffn_in['shared_gate_up'], 'L1_ffn_shared_down': _L1_ffn_in['shared_down'], 'L1_ffn_shared_gate_vec': _L1_ffn_in['shared_gate_vec'], 'L2_xattn_Wq': _L2_xattn_in['Wq'], 'L2_xattn_bq': _L2_xattn_in['bq'], 'L2_xattn_Wk': _L2_xattn_in['Wk'], 'L2_xattn_bk': _L2_xattn_in['bk'], 'L2_xattn_Wv': _L2_xattn_in['Wv'], 'L2_xattn_bv': _L2_xattn_in['bv'], 'L2_xattn_Wqf': _L2_xattn_in['Wqf'], 'L2_xattn_Wkf': _L2_xattn_in['Wkf'], 'L2_xattn_Wo': _L2_xattn_in['Wo'], 'L2_xattn_bo': _L2_xattn_in['bo'], 'L2_ffn_w_gate': _L2_ffn_in['w_gate'], 'L2_ffn_w_up': _L2_ffn_in['w_up'], 'L2_ffn_w_down': _L2_ffn_in['w_down'], 'L2_ffn_up_reorder_index': _L2_ffn_in['up_reorder_index'], 'L2_ffn_down_reorder_index': _L2_ffn_in['down_reorder_index'], 'L3_xattn_Wq': _L3_xattn_in['Wq'], 'L3_xattn_Wk': _L3_xattn_in['Wk'], 'L3_xattn_Wv': _L3_xattn_in['Wv'], 'L3_xattn_Wo': _L3_xattn_in['Wo'], 'L3_ffn_gate_w': _L3_ffn_in['gate_w'], 'L3_ffn_w_gate_up': _L3_ffn_in['w_gate_up'], 'L3_ffn_w_down': _L3_ffn_in['w_down'], 'L3_ffn_shared_gate_up': _L3_ffn_in['shared_gate_up'], 'L3_ffn_shared_down': _L3_ffn_in['shared_down']}

def reference(x, ctx_2048, itok_BxS_0_1023, mask_BxS2_bk0, mask_BxS2_ff1, L0_xattn_W_kvc, L0_xattn_W_dq, L0_xattn_W_uq, L0_xattn_W_qr, L0_xattn_W_uk, L0_xattn_W_kr, L0_xattn_W_uv, L0_xattn_W_o, L0_ffn_W1, L0_ffn_W2, L1_ffn_gate_w, L1_ffn_expert_gate_up, L1_ffn_expert_down, L1_ffn_shared_gate_up, L1_ffn_shared_down, L1_ffn_shared_gate_vec, L2_xattn_Wq, L2_xattn_bq, L2_xattn_Wk, L2_xattn_bk, L2_xattn_Wv, L2_xattn_bv, L2_xattn_Wqf, L2_xattn_Wkf, L2_xattn_Wo, L2_xattn_bo, L2_ffn_w_gate, L2_ffn_w_up, L2_ffn_w_down, L2_ffn_up_reorder_index, L2_ffn_down_reorder_index, L3_xattn_Wq, L3_xattn_Wk, L3_xattn_Wv, L3_xattn_Wo, L3_ffn_gate_w, L3_ffn_w_gate_up, L3_ffn_w_down, L3_ffn_shared_gate_up, L3_ffn_shared_down):
    import jax
    import jax.numpy as jnp

    def _L0_xattn_ref(q, kv, seg_id, W_kvc, W_dq, W_uq, W_qr, W_uk, W_kr, W_uv, W_o):
        import jax, jax.numpy as jnp
        import numpy as np
        B, Lq, Lk = (2, 512, 128)
        Q_DIM, KV_DIM = (256, 256)
        H, HD = (16, 128)
        KVC, QC, R = (64, 96, 64)
        LOOKBACK = 8
        NEG = -1e+30

        def _rope(x, L):
            half = x.shape[-1] // 2
            inv_freq = 1.0 / 10000.0 ** (jnp.arange(half, dtype=jnp.float32) / half)
            ang = jnp.arange(L, dtype=jnp.float32)[:, None] * inv_freq
            cos, sin = (jnp.cos(ang), jnp.sin(ang))
            x1, x2 = (x[..., :half], x[..., half:])
            return jnp.concatenate([x1 * cos - x2 * sin, x1 * sin + x2 * cos], axis=-1)
        b, lq, _ = q.shape
        lk = kv.shape[1]
        kv_c = kv @ W_kvc
        q_c = q @ W_dq
        q_nope = (q_c @ W_uq).reshape(b, lq, H, HD).transpose(0, 2, 1, 3)
        q_rope = (q_c @ W_qr).reshape(b, lq, H, R).transpose(0, 2, 1, 3)
        k_nope = (kv_c @ W_uk).reshape(b, lk, H, HD)
        v = (kv_c @ W_uv).reshape(b, lk, H, HD)
        k_rope = kv_c @ W_kr
        q_rope = _rope(q_rope, lq)
        k_rope = _rope(k_rope, lk)
        scale = 1.0 / np.sqrt(HD + R).astype(np.float32)
        scores = (jnp.einsum('bhqd,bkhd->bhqk', q_nope, k_nope) + jnp.einsum('bhqr,bkr->bhqk', q_rope, k_rope)) * scale
        k_ids = jnp.arange(lk)[None, None, :]
        qs = seg_id[:, :, None]
        good = (k_ids <= qs) & (k_ids >= qs - LOOKBACK)
        scores = jnp.where(good[:, None, :, :], scores, NEG)
        attn = jax.nn.softmax(scores, axis=-1)
        out = jnp.einsum('bhqk,bkhd->bqhd', attn, v).reshape(b, lq, H * HD)
        return out @ W_o

    def _L0_ffn_ref(x, W1, W2):
        import jax, jax.numpy as jnp
        import numpy as np
        D_MODEL = 256
        D_FF = 1024
        BATCH = 4
        SEQ = 256
        MAX_EXP = 4
        NUM_BITS = 8
        C_CHUNKS = 2
        SCALE = 0.1

        def _pow2_ternary(key, out_dim, in_dim, max_exp):
            k1, k2 = jax.random.split(key)
            t = jax.random.randint(k1, (out_dim, in_dim), -1, 2).astype(jnp.float32)
            e = jax.random.randint(k2, (out_dim, in_dim), 0, max_exp + 1).astype(jnp.float32)
            return t * jnp.exp2(-e)

        def _lookup_act(h):
            total_bits = NUM_BITS * C_CHUNKS
            qmax = 2 ** (total_bits - 1) - 1
            qmin = -2 ** (total_bits - 1)
            q = jnp.clip(jnp.round(h / SCALE), qmin, qmax)
            return jax.nn.gelu(q * SCALE)
        h = jnp.einsum('bsd,fd->bsf', x, W1)
        a = _lookup_act(h)
        return jnp.einsum('bsf,df->bsd', a, W2)

    def _L1_xattn_ref(hidden_states, memory_tokens, memory_mask):
        import jax, jax.numpy as jnp
        import numpy as np
        B, S, D = hidden_states.shape
        scale = 1.0 / jnp.sqrt(jnp.asarray(D, hidden_states.dtype))
        scores = jnp.einsum('bsd,bmd->bsm', hidden_states, memory_tokens) * scale
        neg_inf = jnp.asarray(-1e+30, scores.dtype)
        scores = jnp.where(memory_mask[:, None, :], scores, neg_inf)
        attn = jax.nn.softmax(scores, axis=-1)
        readout = jnp.einsum('bsm,bmd->bsd', attn, memory_tokens)
        valid_b = jnp.any(memory_mask, axis=-1)
        out = jnp.where(valid_b[:, None, None], readout, jnp.zeros_like(readout))
        return out

    def _L1_ffn_ref(hidden_states, gate_w, expert_gate_up, expert_down, shared_gate_up, shared_down, shared_gate_vec):
        import jax, jax.numpy as jnp
        import numpy as np
        B, S, H = (4, 128, 256)
        E, K, I, SI = (16, 4, 176, 704)

        def _silu_mul(gu, inter):
            return jax.nn.silu(gu[:, :inter]) * gu[:, inter:]
        orig_shape = hidden_states.shape
        x = hidden_states.reshape(-1, H)
        router_logits = x @ gate_w.T
        routing_probs = jax.nn.softmax(router_logits.astype(jnp.float32), axis=-1)
        topk_w, topk_idx = jax.lax.top_k(routing_probs, K)
        topk_w = topk_w / topk_w.sum(axis=-1, keepdims=True)
        topk_w = topk_w.astype(x.dtype)
        combine = (jax.nn.one_hot(topk_idx, E, dtype=x.dtype) * topk_w[..., None]).sum(1)
        shared = _silu_mul(x @ shared_gate_up.T, SI) @ shared_down.T
        shared = shared * jax.nn.sigmoid(x @ shared_gate_vec.T)

        def step(acc, ew):
            w_gu, w_d, cw = ew
            h = _silu_mul(x @ w_gu.T, I)
            return (acc + h @ w_d.T * cw[:, None], None)
        acc0 = jnp.zeros_like(x)
        sparse, _ = jax.lax.scan(step, acc0, (expert_gate_up, expert_down, combine.T))
        return (shared + sparse).reshape(orig_shape)

    def _L2_xattn_ref(query, key, value, attention_mask, Wq, bq, Wk, bk, Wv, bv, Wqf, Wkf, Wo, bo):
        import jax, jax.numpy as jnp
        import numpy as np
        H = 256
        NH = 16
        HD = H // NH
        FD = 64
        B, Sq, _ = query.shape
        Sk = key.shape[1]

        def heads(x, W, b, S):
            return (x @ W.T + b).reshape(B, S, NH, HD).transpose(0, 2, 1, 3)
        q = heads(query, Wq, bq, Sq)
        k = heads(key, Wk, bk, Sk)
        v = heads(value, Wv, bv, Sk)
        q_prime = jax.nn.relu(jnp.einsum('bhnd,fd->bhnf', q, Wqf))
        k_prime = jax.nn.relu(jnp.einsum('bhnd,fd->bhnf', k, Wkf))
        k_prime = k_prime * attention_mask[:, None, :, None]
        kv = jnp.einsum('bhnf,bhne->bhfe', k_prime, v)
        qkv = jnp.einsum('bhmf,bhfe->bhme', q_prime, kv)
        k_sum = jnp.sum(k_prime, axis=2)
        qk_sum = jnp.einsum('bhmf,bhf->bhm', q_prime, k_sum)[..., None]
        out = qkv / (qk_sum + 1e-08)
        out = out.transpose(0, 2, 1, 3).reshape(B, Sq, H)
        return out @ Wo.T + bo

    def _L2_ffn_ref(x, w_gate, w_up, w_down, up_reorder_index, down_reorder_index):
        import jax, jax.numpy as jnp
        import numpy as np
        FP8_MAX = 448.0
        GLOBAL_DIV = 448.0 * 6.0

        def _fp8(x):
            return x.astype(jnp.float8_e4m3fn).astype(jnp.float32)

        def _reorder_quantize_x(x, idx):
            scale = jnp.max(jnp.abs(x)) / GLOBAL_DIV
            xr = (x / scale)[:, idx]
            scale_x = jnp.max(jnp.abs(xr), axis=1, keepdims=True) / FP8_MAX
            qx = _fp8(xr / scale_x)
            return (qx, scale_x, scale)

        def _qlinear(qx, scale_x, scale, W, idx, out_idx=None):
            Wr = W[:, idx]
            w_scale = jnp.max(jnp.abs(Wr), axis=1, keepdims=True) / FP8_MAX
            qw = _fp8(Wr / w_scale)
            y = qx * scale_x @ (qw * w_scale).T * scale
            if out_idx is not None:
                y = y[:, out_idx]
            return y
        B, S, H = x.shape
        xf = x.reshape(B * S, H)
        qx, sx, sc = _reorder_quantize_x(xf, up_reorder_index)
        g = _qlinear(qx, sx, sc, w_gate, up_reorder_index, out_idx=down_reorder_index)
        u = _qlinear(qx, sx, sc, w_up, up_reorder_index, out_idx=down_reorder_index)
        t = jax.nn.silu(g) * u
        qt, st, sct = _reorder_quantize_x(t, down_reorder_index)
        y = _qlinear(qt, st, sct, w_down, down_reorder_index)
        return y.reshape(B, S, H)

    def _L3_xattn_ref(inputs_q, inputs_kv, Wq, Wk, Wv, Wo):
        import jax, jax.numpy as jnp
        import numpy as np
        B, S, D = (8, 128, 256)
        H, HD = (16, 128)
        b, sq, _ = inputs_q.shape
        skv = inputs_kv.shape[1]
        q = (inputs_q @ Wq).reshape(b, sq, H, HD) * (1.0 / np.sqrt(HD))
        k = (inputs_kv @ Wk).reshape(b, skv, H, HD)
        v = (inputs_kv @ Wv).reshape(b, skv, H, HD)
        scores = jnp.einsum('bqhd,bkhd->bhqk', q, k)
        attn = jax.nn.softmax(scores, axis=-1)
        ctx = jnp.einsum('bhqk,bkhd->bqhd', attn, v).reshape(b, sq, H * HD)
        return ctx @ Wo

    def _L3_ffn_ref(hidden_states, gate_w, w_gate_up, w_down, shared_gate_up, shared_down):
        import jax, jax.numpy as jnp
        import numpy as np
        from jax import lax
        E = 8
        K = 2
        H = 256
        I = 512
        B, S = (2, 256)
        SCALE = 0.02

        def _silu_and_mul(gu):
            g, u = jnp.split(gu, 2, axis=-1)
            return jax.nn.silu(g) * u
        orig_shape = hidden_states.shape
        x = hidden_states.reshape(-1, orig_shape[-1])
        shared_out = _silu_and_mul(x @ shared_gate_up) @ shared_down
        router_logits = x @ gate_w
        probs = jax.nn.softmax(router_logits, axis=-1)
        topk_w, topk_i = lax.top_k(probs, K)
        topk_w = topk_w / jnp.sum(topk_w, axis=-1, keepdims=True)
        combine = jnp.sum(jax.nn.one_hot(topk_i, E, dtype=x.dtype) * topk_w[..., None], axis=1)

        def body(acc, we):
            wg, wd, cw = we
            h = _silu_and_mul(x @ wg) @ wd
            return (acc + cw[:, None] * h, None)
        moe_out, _ = lax.scan(body, jnp.zeros_like(x), (w_gate_up, w_down, combine.T))
        return (moe_out + shared_out).reshape(orig_shape)
    x = x + _L0_xattn_ref(_layernorm(x, axis=-1), ctx_2048, itok_BxS_0_1023, L0_xattn_W_kvc, L0_xattn_W_dq, L0_xattn_W_uq, L0_xattn_W_qr, L0_xattn_W_uk, L0_xattn_W_kr, L0_xattn_W_uv, L0_xattn_W_o)
    x = x + _L0_ffn_ref(_layernorm(x, axis=-1), L0_ffn_W1, L0_ffn_W2)
    x = x + _L1_xattn_ref(_layernorm(x, axis=-1), ctx_2048, mask_BxS2_bk0)
    x = x + _L1_ffn_ref(_layernorm(x, axis=-1), L1_ffn_gate_w, L1_ffn_expert_gate_up, L1_ffn_expert_down, L1_ffn_shared_gate_up, L1_ffn_shared_down, L1_ffn_shared_gate_vec)
    x = x + _L2_xattn_ref(_layernorm(x, axis=-1), ctx_2048, ctx_2048, mask_BxS2_ff1, L2_xattn_Wq, L2_xattn_bq, L2_xattn_Wk, L2_xattn_bk, L2_xattn_Wv, L2_xattn_bv, L2_xattn_Wqf, L2_xattn_Wkf, L2_xattn_Wo, L2_xattn_bo)
    x = x + _L2_ffn_ref(_layernorm(x, axis=-1), L2_ffn_w_gate, L2_ffn_w_up, L2_ffn_w_down, L2_ffn_up_reorder_index, L2_ffn_down_reorder_index)
    x = x + _L3_xattn_ref(_layernorm(x, axis=-1), ctx_2048, L3_xattn_Wq, L3_xattn_Wk, L3_xattn_Wv, L3_xattn_Wo)
    x = x + _L3_ffn_ref(_layernorm(x, axis=-1), L3_ffn_gate_w, L3_ffn_w_gate_up, L3_ffn_w_down, L3_ffn_shared_gate_up, L3_ffn_shared_down)
    return x

_drawn_inputs = setup_inputs


def setup_inputs(seed=0):
    import zlib

    import numpy as np

    out = dict(_drawn_inputs(seed))
    spreads = {'L2_xattn_bq': (0.0, 0.8),
     'L2_xattn_bk': (0.0, 0.8),
     'L2_xattn_bv': (0.0, 0.8),
     'L2_xattn_bo': (0.0, 0.8)}
    factors = {'L1_ffn_gate_w': 8.0,
     'L1_ffn_expert_gate_up': 8.0,
     'L1_ffn_expert_down': 8.0,
     'L1_ffn_shared_gate_up': 8.0,
     'L1_ffn_shared_down': 8.0,
     'L1_ffn_shared_gate_vec': 8.0,
     'L2_xattn_Wq': 8.0,
     'L2_xattn_Wk': 8.0,
     'L2_xattn_Wv': 7.433,
     'L2_xattn_Wqf': 8.0,
     'L2_xattn_Wkf': 8.0,
     'L2_xattn_Wo': 7.174,
     'L2_ffn_w_gate': 8.0,
     'L2_ffn_w_up': 8.0,
     'L2_ffn_w_down': 8.0,
     'L3_xattn_Wq': 8.0,
     'L3_xattn_Wk': 8.0,
     'L3_xattn_Wv': 6.639,
     'L3_xattn_Wo': 6.763,
     'L3_ffn_gate_w': 8.0,
     'L3_ffn_w_gate_up': 8.0,
     'L3_ffn_w_down': 8.0,
     'L3_ffn_shared_gate_up': 8.0,
     'L3_ffn_shared_down': 8.0}
    for name, (base, spread) in spreads.items():
        noise = np.random.default_rng([zlib.crc32(name.encode()), seed]).standard_normal(out[name].shape)
        drawn = base * np.exp(spread * noise) if base else spread * noise
        out[name] = jnp.asarray(drawn.astype(out[name].dtype))
    for name, factor in factors.items():
        out[name] = (out[name] * factor).astype(out[name].dtype)
    return out
```

```python
from contextlib import ExitStack

import numpy as np

import concourse.bass as bass
from concourse import mybir

F32 = mybir.dt.float32
BF16 = mybir.dt.bfloat16
I32 = mybir.dt.int32
U32 = mybir.dt.uint32
U8 = mybir.dt.uint8
ACT = mybir.ActivationFunctionType
ALU = mybir.AluOpType
AXIS = mybir.AxisListType
REDUCE = bass.bass_isa.ReduceOp

P = 128
B, S, D = 8, 56, 256
SP = 64
PAIRS = B // 2
T = B * SP
TOK = B * S
DC = D // P
LK = 1500
KT, KP = 12, 125
KN = 500
EPS = 1e-5
NEG = -1e30
DMA = 16


class InOrder:

    def __init__(self, eng, sem, n=0):
        self.eng, self.sem, self.n, self.base = eng, sem, n, 0

    def __call__(self, ins):
        ins.then_inc(self.sem, 1)
        self.n += 1
        self.eng.wait_ge(self.sem, self.base + self.n)

    def loop(self, i, first, per_turn):
        self.base, self.n = first + i * per_turn, 0

    def end(self, first, per_turn, turns):
        assert self.n == per_turn, (self.n, per_turn)
        self.base, self.n = 0, first + per_turn * turns


class Core:

    def __init__(self, nc, ctx, dram):
        self.nc, self.dram = nc, dram

        def sb(name, shape, dt=F32):
            return ctx.enter_context(nc.sbuf_tensor(name, shape, dt))

        self.x_rows = sb("x_rows", [P, PAIRS, D])
        self.xn_rows = sb("xn_rows", [P, PAIRS, D])
        self.xn_cols = sb("xn_cols", [P, DC, T])
        self.ident = sb("ident", [P, P])
        self.bn = sb("bn", [P, PAIRS, 6])
        self.mean_var = sb("mean_var", [P, PAIRS, 2])
        self.var_eps = sb("var_eps", [P, PAIRS])
        self.rstd = sb("rstd", [P, PAIRS])
        self.minus_half = sb("minus_half", [P, PAIRS])
        self.psum = ctx.enter_context(nc.psum_tensor("psum", [P, 8, 512], F32))

        self.stage_sems = []
        self.const_ready = self.sem("const_ready")
        self.dve_step = self.sem("dve_step")
        self.act_step = self.sem("act_step")
        self.pool_step = self.sem("pool_step")
        self.ln_stats = self.sem("ln_stats")
        self.ln_rstd = self.sem("ln_rstd")
        self.ln_rows = self.sem("ln_rows")
        self.ln_turned = self.sem("ln_turned")
        self.ln_cols = self.sem("ln_cols")
        self.keep_sems()
        self.norms = 0
        self.turn_of = {}
        self.dve_n = self.act_n = self.pool_n = 0

    def sem(self, name):
        self.stage_sems.append(self.nc.alloc_semaphore(name=name))
        return self.stage_sems[-1]

    def keep_sems(self):
        self.stage_sems = []

    def retire_sems(self):
        self.nc.clear_and_free_semaphores(self.stage_sems)
        self.nc.all_engine_barrier()
        self.stage_sems = []

    def open_kv_sums(self, ctx):
        self.kv_sums = ctx.enter_context(self.nc.sbuf_tensor("kv_sums", [P, B, 8, 34], F32))

    def new_norm(self, turned=True):
        k = self.norms
        self.norms += 1
        if turned:
            self.turn_of[k] = len(self.turn_of)
        return k

    def cols_ready(self, k):
        return DC * (self.turn_of[k] + 1)

    def ln_vector(self, dve, link, k):
        for i in range(PAIRS):
            ins = dve.bn_stats(self.bn[:, i, :], self.x_rows[:, i, :])
            link(ins)
        for i in range(PAIRS):
            ins = dve.bn_aggr(self.mean_var[:, i, :], self.bn[:, i, :])
            link(ins)
        dve.tensor_scalar(self.var_eps[:, :], self.mean_var[:, :, 1], EPS, None,
                          ALU.add).then_inc(self.ln_stats, 1)
        dve.wait_ge(self.ln_rstd, k + 1)
        for i in range(PAIRS):
            dve.tensor_scalar(self.xn_rows[:, i, :], self.x_rows[:, i, :], self.mean_var[:, i, 0:1],
                              self.rstd[:, i:i + 1], ALU.subtract, ALU.mult).then_inc(self.ln_rows, 1)

    def ln_pool(self, pool, k):
        pool.wait_ge(self.ln_stats, k + 1)
        pool.tensor_tensor(self.rstd[:, :], self.var_eps[:, :], self.minus_half[:, :],
                           ALU.pow).then_inc(self.ln_rstd, 1)

    def ln_tensor(self, pe, k):
        for i in range(PAIRS):
            pe.wait_ge(self.ln_rows, PAIRS * k + i + 1)
            for c in range(DC):
                ins = pe.transpose(self.psum[:, c, i * P:(i + 1) * P],
                                   self.xn_rows[:, i, c * P:(c + 1) * P], self.ident[:, :])
        ins.then_inc(self.ln_turned, 1)

    def ln_scalar(self, act, k):
        act.wait_ge(self.ln_turned, self.turn_of[k] + 1)
        for c in range(DC):
            act.copy(self.xn_cols[:, c, :], self.psum[:, c, :]).then_inc(self.ln_cols, 1)

    def tok(self, c):
        return self.xn_cols[:, c, :].rearrange("p (b s) -> p b s", b=B)[:, :, 0:S]


def unpad(cols):
    return cols.rearrange("p (b s) -> p b s", b=B)[:, :, 0:S]


def packed(cols):
    return cols.rearrange("p (b s) -> p b s", b=B)


def setup(core):
    nc, dram = core.nc, core.dram
    x_loaded, zeroed = core.sem("x_loaded"), core.sem("zeroed")
    core.x_loaded = x_loaded
    with nc.Block() as block:
        @block.vector
        def _(dve):
            dve.memset(core.x_rows[:, :, :], 0.0).then_inc(zeroed, 1)
            dve.memset(core.minus_half[:, :], -0.5).then_inc(zeroed, 1)

        @block.sync
        def _(sp):
            sp.dma_start(core.ident[:, :], dram["c_ident"]).then_inc(core.const_ready, DMA)
            sp.wait_ge(zeroed, 1)
            for b in range(B):
                r = (b % 2) * SP
                sp.dma_start(core.x_rows[r:r + S, b // 2, :], dram["x"][b]).then_inc(x_loaded, DMA)
            sp.wait_ge(x_loaded, DMA * B)
            sp.wait_ge(core.const_ready, DMA)


def store(core):
    dram = core.dram
    stored = core.sem("stored")
    with core.nc.Block() as block:
        @block.sync
        def _(sp):
            for b in range(B):
                r = (b % 2) * SP
                sp.dma_start(dram["out"][b], core.x_rows[r:r + S, b // 2, :]).then_inc(stored, DMA)
            sp.wait_ge(stored, DMA * B)


H, HD = 16, 128
KVC, QC, R = 64, 96, 64
WIN = 9
GQ = 14
GROUPS = S // GQ
GR = GQ * WIN
HH = H // 2
ROW0 = GQ * HH


def window_attention(core):
    nc, dram, ps = core.nc, core.dram, core.psum
    k_ln = core.new_norm()
    dve0, act0 = core.dve_n, core.act_n
    scale = 1.0 / float(np.sqrt(np.float32(HD + R)))
    ctx = ExitStack()
    with ctx:
        def sb(name, shape, dt=F32):
            return ctx.enter_context(nc.sbuf_tensor(name, shape, dt))
        w_dq = sb("w_dq", [P, DC, QC])
        w_kvc_t = sb("w_kvc_t", [KVC, D])
        w_kr2 = sb("w_kr2", [KVC, 2 * R])
        w_key = sb("w_key", [P, DC, P])
        w_key_sw = sb("w_key_sw", [P, DC, R])
        w_uq_t = sb("w_uq_t", [P, H, QC])
        w_uk_t = sb("w_uk_t", [P, H, KVC])
        w_qr = sb("w_qr", [QC, 2, H * R])
        w_abs = sb("w_abs", [QC, H * KVC])
        w_uv_t = sb("w_uv_t", [P, H, KVC])
        w_o = sb("w_o", [P, H, D])
        w_vo = sb("w_vo", [P, HH, D])
        q_lat = sb("q_lat", [QC, T])
        rope_q = sb("rope_q", [P, 2, S])
        rope_a = sb("rope_a", [P, TOK])
        rope_b = sb("rope_b", [P, TOK])
        q_cat = sb("q_cat", [P, B * GROUPS, H, GQ])
        q_now = sb("q_now", [P, 2, GROUPS, H, GQ])
        seg_k = sb("seg_k", [GR, B * GROUPS], I32)
        seg_r = sb("seg_r", [ROW0, B * GROUPS], I32)
        win_k = sb("win_k", [GR, 1])
        seq_row = sb("seq_row", [GR, B * GROUPS])
        win_r = sb("win_r", [ROW0, WIN])
        diag = sb("diag", [ROW0, GR])
        row_f = sb("row_f", [GR, B * GROUPS])
        row_c = sb("row_c", [GR, B * GROUPS])
        rows_at = sb("rows_at", [GR, B * GROUPS], I32)
        kid = sb("kid", [ROW0, B * GROUPS, WIN])
        kid_c = sb("kid_c", [ROW0, B * GROUPS, WIN])
        outside = sb("outside", [ROW0, B * GROUPS, WIN])
        mask = sb("mask", [ROW0, B * GROUPS, GR])
        got = sb("got", [GR, 2, GROUPS, 3 * P])
        got_t = sb("got_t", [P, 2, 3, GROUPS * GR])
        key_sin = sb("key_sin", [P, GROUPS * GR])
        keys = sb("keys", [P, 2, GROUPS * GR])
        vals = sb("vals", [GR, 2, GROUPS, KVC])
        s_sb = sb("s_sb", [ROW0, 2, 2, GR])
        neg_max = sb("neg_max", [ROW0, 2, 2])
        sums = sb("sums", [ROW0, 2, 2])
        inv = sb("inv", [ROW0, 2, 2])
        prob = sb("prob", [ROW0, 2, 2, GR])
        prob_t = sb("prob_t", [GR, 2, 2, ROW0])
        lat = sb("lat", [P, HH, T])

        sem = core.sem
        idx_in = sem("w_idx_in")
        w_in = sem("w_weights_in")
        rows_known = sem("w_rows_known")
        got_in = [sem("w_got_in0"), sem("w_got_in1")]
        got_turned = sem("w_got_turned")
        got_t_ready = sem("w_got_t_ready")
        key_mm = sem("w_key_mm")
        key_latent = sem("w_key_latent")
        key_ready = sem("w_key_ready")
        val_mm = sem("w_val_mm")
        val_ready = sem("w_val_ready")
        comp_mm = sem("w_comp_mm")
        comp_ready = sem("w_comp_ready")
        q_mm = sem("w_q_mm")
        q_rot = sem("w_q_rot")
        q_abs = sem("w_q_abs")
        q_staged = sem("w_q_staged")
        score_mm = sem("w_score_mm")
        score_sb = sem("w_score_sb")
        maxed = sem("w_maxed")
        exped = sem("w_exped")
        normed = sem("w_normed")
        prob_turned = sem("w_prob_turned")
        prob_t_ready = sem("w_prob_t_ready")
        lat_mm = sem("w_lat_mm")
        lat_ready = sem("w_lat_ready")
        out_mm = sem("w_out_mm")

        gt = GROUPS * GR
        block = ctx.enter_context(nc.Block())

        @block.sync
        def _(sp):
            for dst, src in ((seg_k, "seg_k"), (win_k, "c_win_k"), (seq_row, "c_seq_row"),
                             (seg_r, "seg_r"), (win_r, "c_win_r"), (diag, "c_diag")):
                sp.dma_start(dst[:, :], dram[src]).then_inc(idx_in, DMA)
            sp.dma_start(w_kvc_t[:, :], dram["w_kvc_t"]).then_inc(w_in, DMA)
            sp.dma_start(w_kr2[:, :], dram["w_kr2"]).then_inc(w_in, DMA)
            sp.dma_start(w_key[:, :, 0:KVC], dram["w_kvc"]).then_inc(w_in, DMA)
            for dst, src in ((w_dq, "w_dq"), (w_uq_t, "w_uq_t"), (w_uk_t, "w_uk_t"), (w_qr, "w_qr"),
                             (w_uv_t, "w_uv_t"), (w_o, "w_o"), (rope_q, "c_rope_q")):
                sp.dma_start(dst[:, :, :], dram[src]).then_inc(w_in, DMA)
        n_w = 10

        @block.gpsimd
        def _(pool):
            core.ln_pool(pool, k_ln)
            pool.wait_ge(rows_known, 1)

            for b in range(B):
                if b >= 2:
                    pool.wait_ge(got_turned, b - 1)
                for g in range(GROUPS):
                    n = b * GROUPS + g
                    pool.indirect_dma_start(
                        got[:, b % 2, g, :], None, dram["ctx_rope"],
                        bass.IndirectOffsetOnAxis(ap=rows_at[:, n:n + 1], axis=0),
                    ).then_inc(got_in[b % 2], DMA)
                if b == 0:
                    pool.wait_ge(q_rot, 2 * HH)
                    pool.wait_ge(q_abs, 1 + 2 * HH)
                if b >= 2:
                    pool.wait_ge(score_mm, GROUPS * (b - 1))
                pool.tensor_copy(q_now[:, b % 2, :, :, :], q_cat[:, b * GROUPS:(b + 1) * GROUPS, :, :]) \
                    .then_inc(q_staged, 1)

        @block.tensor
        def _(pe):
            pe.wait_ge(w_in, DMA * n_w)
            for c in range(DC):
                ins = pe.matmul(ps[:, 2, c * P:(c + 1) * P], w_kvc_t[:, c * P:(c + 1) * P], w_kr2[:, :],
                                start=True, stop=True)
            ins.then_inc(comp_mm, 1)
            for h in range(H):
                ins = pe.matmul(ps[0:QC, 3 + h // 8, (h % 8) * KVC:(h % 8 + 1) * KVC],
                                w_uq_t[:, h, :], w_uk_t[:, h, :], start=True, stop=True)
            ins.then_inc(comp_mm, 1)
            for j in range(HH):
                if j == 4:
                    pe.wait_ge(comp_ready, 4)
                for k in range(2):
                    ins = pe.matmul(ps[k * KVC:(k + 1) * KVC, 5 + j // 2 % 2, (j % 2) * D:(j % 2 + 1) * D],
                                    w_uv_t[:, j + k * HH, :], w_o[:, j + k * HH, :], start=True, stop=True)
                if j % 4 == 3:
                    ins.then_inc(comp_mm, 1)
            core.ln_tensor(pe, k_ln)
            pe.wait_ge(core.ln_cols, core.cols_ready(k_ln))
            for c in range(DC):
                ins = pe.matmul(ps[0:QC, 7, :], w_dq[:, c, :], core.xn_cols[:, c, :],
                                start=(c == 0), stop=(c == DC - 1))
            ins.then_inc(q_mm, 1)
            pe.wait_ge(q_abs, 1)
            pe.wait_ge(comp_ready, 3)
            lq = unpad(q_lat[:, :])
            for j in range(HH):
                if j >= 2:
                    pe.wait_ge(q_rot, 2 * (j - 1))
                    pe.wait_ge(q_abs, 1 + 2 * (j - 1))
                bank = 3 * (j % 2)
                pe.matmul(packed(ps[:, bank, 0:TOK]), w_abs[:, j * P:(j + 1) * P], lq, start=True, stop=True)
                for k in range(2):
                    ins = pe.matmul(packed(ps[:, bank + 1 + k, 0:TOK]), w_qr[:, k, j * P:(j + 1) * P], lq,
                                    start=True, stop=True)
                ins.then_inc(q_mm, 1)

            def keys_of(b):
                s = b % 2
                pe.wait_ge(got_in[s], DMA * GROUPS * (b // 2 + 1))
                if b == 0:
                    pe.wait_ge(q_rot, 2 * HH)
                    pe.wait_ge(q_abs, 1 + 2 * HH)
                else:
                    pe.wait_ge(got_t_ready, 3 * b)
                for g in range(GROUPS):
                    for c in range(3):
                        ins = pe.transpose(ps[:, c, g * GR:(g + 1) * GR], got[:, s, g, c * P:(c + 1) * P],
                                           core.ident[0:GR, 0:GR])
                ins.then_inc(got_turned, 1)
                pe.wait_ge(got_t_ready, 3 * (b + 1))
                if b >= 1:
                    pe.wait_ge(key_ready, b)
                    pe.wait_ge(val_ready, b)
                for c in range(DC):
                    pe.matmul(ps[:, 3, 0:gt], w_key[:, c, :], got_t[:, s, c, :],
                              start=(c == 0), stop=(c == DC - 1))
                for c in range(DC):
                    ins = pe.matmul(ps[0:R, 4, 0:gt], w_key_sw[:, c, :], got_t[:, s, c, :],
                                    start=(c == 0), stop=(c == DC - 1))
                ins.then_inc(key_mm, 1)
                pe.wait_ge(key_ready, b + 1)
                for g in range(GROUPS):
                    ins = pe.transpose(ps[0:GR, 4, g * KVC:(g + 1) * KVC],
                                       keys[0:KVC, s, g * GR:(g + 1) * GR], core.ident[0:KVC, 0:KVC])
                ins.then_inc(val_mm, 1)

            def scores_of(n):
                b, g = n // GROUPS, n % GROUPS
                if g == 0:
                    pe.wait_ge(q_staged, b + 1)
                if n >= 1:
                    pe.wait_ge(score_sb, n)
                for k in range(2):
                    ins = pe.matmul(ps[0:ROW0, 5, k * GR:(k + 1) * GR],
                                    q_now[:, b % 2, g, k * HH:(k + 1) * HH, :].rearrange("p h q -> p (h q)"),
                                    keys[:, b % 2, g * GR:(g + 1) * GR], start=True, stop=True)
                ins.then_inc(score_mm, 1)

            def attend(n):
                b, g = n // GROUPS, n % GROUPS
                pe.wait_ge(normed, n + 1)
                if n >= 1:
                    pe.wait_ge(prob_t_ready, n)
                for k in range(2):
                    ins = pe.transpose(ps[0:GR, 6, k * ROW0:(k + 1) * ROW0], prob[:, n % 2, k, :],
                                       core.ident[0:ROW0, 0:ROW0])
                ins.then_inc(prob_turned, 1)

            def mix(n):
                b, g = n // GROUPS, n % GROUPS
                pe.wait_ge(prob_t_ready, n + 1)
                pe.wait_ge(val_ready, b + 1)
                if n >= 1:
                    pe.wait_ge(lat_ready, n)
                for k in range(2):
                    ins = pe.matmul(ps[k * KVC:(k + 1) * KVC, 7, 0:ROW0], vals[:, b % 2, g, :],
                                    prob_t[:, n % 2, k, :], start=True, stop=True)
                ins.then_inc(lat_mm, 1)

            n_groups = B * GROUPS
            for n in range(n_groups + 2):
                if n < n_groups:
                    if n % GROUPS == 0:
                        keys_of(n // GROUPS)
                    scores_of(n)
                if 1 <= n <= n_groups:
                    attend(n - 1)
                if n >= 2:
                    mix(n - 2)
            pe.wait_ge(lat_ready, n_groups)
            pe.wait_ge(comp_ready, 5)
            for i in range(PAIRS):
                for j in range(HH):
                    ins = pe.matmul(ps[:, i // 2, (i % 2) * D:(i % 2 + 1) * D], lat[:, j, i * P:(i + 1) * P],
                                    w_vo[:, j, :], start=(j == 0), stop=(j == HH - 1))
            ins.then_inc(out_mm, 1)

        @block.scalar
        def _(act):
            act.wait_ge(comp_mm, 1)
            act.copy(w_key[:, :, KVC:P], ps[:, 2, 0:2 * P].rearrange("p (c k) -> p c k", c=2)[:, :, 0:R]) \
                .then_inc(comp_ready, 1)
            act.copy(w_key_sw[:, :, :], ps[:, 2, 0:2 * P].rearrange("p (c k) -> p c k", c=2)[:, :, R:P]) \
                .then_inc(comp_ready, 1)
            act.wait_ge(comp_mm, 2)
            act.copy(w_abs[:, :], ps[0:QC, 3:5, :].rearrange("p a n -> p (a n)")).then_inc(comp_ready, 1)
            for a in range(2):
                act.wait_ge(comp_mm, 3 + a)
                act.copy(w_vo[:, 4 * a:4 * a + 4, :].rearrange("p j n -> p (j n)"),
                         ps[:, 5:7, :].rearrange("p a n -> p (a n)")).then_inc(comp_ready, 1)
            core.ln_scalar(act, k_ln)
            act.wait_ge(q_mm, 1)
            act.copy(q_lat[:, :], ps[0:QC, 7, :]).then_inc(q_abs, 1)
            for j in range(HH):
                act.wait_ge(q_mm, 2 + j)
                for k in range(2):
                    act.copy(q_cat[0:KVC, :, 2 * j + k, :],
                             ps[k * KVC:(k + 1) * KVC, 3 * (j % 2), 0:TOK]
                             .rearrange("p (n q) -> p n q", q=GQ)).then_inc(q_abs, 1)

            def keys_of(b):
                s = b % 2
                act.wait_ge(got_turned, b + 1)
                if b >= 2:
                    act.wait_ge(key_ready, b - 1)
                for c in range(2):
                    act.copy(got_t[:, s, c, :], ps[:, c, 0:gt]).then_inc(got_t_ready, 1)
                act.wait_ge(key_mm, b + 1)
                act.copy(keys[0:KVC, s, :], ps[0:KVC, 3, 0:gt]).then_inc(key_latent, 1)
                act.wait_ge(val_mm, b + 1)
                act.copy(vals[:, s, :, :].rearrange("p g k -> p (g k)"), ps[0:GR, 4, 0:GROUPS * KVC]) \
                    .then_inc(val_ready, 1)

            def exps(n):
                act.wait_ge(maxed, n + 1)
                if n >= 2:
                    act.wait_ge(prob_turned, n - 1)
                for k in range(2):
                    act.activation(prob[:, n % 2, k, :], s_sb[:, n % 2, k, :], ACT.Exp,
                                   bias=neg_max[:, n % 2, k:k + 1],
                                   accum_out=sums[:, n % 2, k:k + 1]).then_inc(exped, 1)

            def turned(n):
                act.wait_ge(prob_turned, n + 1)
                if n >= 2:
                    act.wait_ge(lat_mm, n - 1)
                act.copy(prob_t[:, n % 2, :, :].rearrange("p k r -> p (k r)"),
                         ps[0:GR, 6, 0:2 * ROW0]).then_inc(prob_t_ready, 1)

            n_groups = B * GROUPS
            for n in range(n_groups + 1):
                if n < n_groups:
                    if n % GROUPS == 0:
                        keys_of(n // GROUPS)
                    exps(n)
                if n >= 1:
                    turned(n - 1)

        @block.vector
        def _(dve):
            link = InOrder(dve, core.dve_step, dve0)
            link(dve.memset(lat[:, :, :], 0.0))
            dve.wait_ge(idx_in, DMA * 6)
            link(dve.tensor_scalar(row_f[:, :], seg_k[:, :], win_k[:, 0:1], 0.0, ALU.add, ALU.max))
            link(dve.tensor_scalar(row_c[:, :], row_f[:, :], float(LK - 1), None, ALU.min))
            dve.tensor_tensor(rows_at[:, :], row_c[:, :], seq_row[:, :], ALU.add).then_inc(rows_known, 1)
            core.ln_vector(dve, link, k_ln)
            n_g = B * GROUPS
            link(dve.tensor_tensor(kid[:, :, :], seg_r[:, :].unsqueeze(2).to_broadcast([ROW0, n_g, WIN]),
                                   win_r[:, :].unsqueeze(1).to_broadcast([ROW0, n_g, WIN]), ALU.add))
            link(dve.tensor_scalar(kid_c[:, :, :], kid[:, :, :], 0.0, float(LK - 1), ALU.max, ALU.min))
            link(dve.tensor_tensor(outside[:, :, :], kid[:, :, :], kid_c[:, :, :], ALU.not_equal))
            link(dve.tensor_scalar(outside[:, :, :], outside[:, :, :], NEG, None, ALU.mult))
            for n in range(n_g):
                ins = dve.tensor_tensor(mask[:, n, :].rearrange("p (q w) -> p q w", w=WIN),
                                  diag[:, :].rearrange("p (q w) -> p q w", w=WIN),
                                  outside[:, n, :].unsqueeze(1).to_broadcast([ROW0, GQ, WIN]), ALU.add)
                link(ins)
            dve.wait_ge(w_in, DMA * n_w)
            for j in range(HH):
                bank = 3 * (j % 2)
                dve.wait_ge(q_mm, 2 + j)
                link(dve.tensor_tensor(packed(rope_a[:, :]), packed(ps[:, bank + 1, 0:TOK]),
                                       rope_q[:, 0:1, :].to_broadcast([P, B, S]), ALU.mult))
                link(dve.tensor_tensor(packed(rope_b[:, :]), packed(ps[:, bank + 2, 0:TOK]),
                                       rope_q[:, 1:2, :].to_broadcast([P, B, S]), ALU.mult))
                for k in range(2):
                    r = slice(k * R, (k + 1) * R)
                    dve.tensor_tensor(q_cat[KVC:P, :, 2 * j + k, :],
                                      rope_a[r, :].rearrange("p (n q) -> p n q", q=GQ),
                                      rope_b[r, :].rearrange("p (n q) -> p n q", q=GQ), ALU.add) \
                        .then_inc(q_rot, 1)
                    dve.wait_ge(q_rot, 2 * j + k + 1)

            def keys_of(b):
                s = b % 2
                dve.wait_ge(got_turned, b + 1)
                dve.tensor_copy(got_t[:, s, 2, :], ps[:, 2, 0:gt]).then_inc(got_t_ready, 1)
                dve.wait_ge(key_mm, b + 1)
                dve.wait_ge(got_t_ready, 3 * (b + 1))
                link(dve.tensor_tensor(key_sin[KVC:P, :], ps[0:R, 4, 0:gt], got_t[0:R, s, 2, :], ALU.mult))
                dve.wait_ge(key_latent, b + 1)
                link(dve.tensor_tensor(keys[KVC:P, s, :], ps[KVC:P, 3, 0:gt], got_t[KVC:P, s, 2, :], ALU.mult))
                dve.tensor_tensor(keys[KVC:P, s, :], keys[KVC:P, s, :], key_sin[KVC:P, :], ALU.add) \
                    .then_inc(key_ready, 1)
                dve.wait_ge(key_ready, b + 1)

            def scored(n):
                dve.wait_ge(score_mm, n + 1)
                if n >= 2:
                    dve.wait_ge(exped, 2 * (n - 1))
                dve.scalar_tensor_tensor(s_sb[:, n % 2, :, :],
                                         ps[0:ROW0, 5, 0:2 * GR].rearrange("p (k r) -> p k r", k=2),
                                         scale, mask[:, n:n + 1, :].to_broadcast([ROW0, 2, GR]),
                                         ALU.mult, ALU.add).then_inc(score_sb, 1)
                dve.wait_ge(score_sb, n + 1)
                dve.tensor_reduce(neg_max[:, n % 2, :], s_sb[:, n % 2, :, :], AXIS.X, ALU.max,
                                  negate=True).then_inc(maxed, 1)

            def normalise(n):
                dve.wait_ge(exped, 2 * (n + 1))
                link(dve.reciprocal(inv[:, n % 2, :], sums[:, n % 2, :]))
                dve.tensor_tensor(prob[:, n % 2, :, :], prob[:, n % 2, :, :],
                                  inv[:, n % 2, :].unsqueeze(2).to_broadcast([ROW0, 2, GR]), ALU.mult) \
                    .then_inc(normed, 1)

            def mixed(n):
                b, g = n // GROUPS, n % GROUPS
                dve.wait_ge(lat_mm, n + 1)
                dve.tensor_copy(lat[:, :, b * SP + g * GQ:b * SP + (g + 1) * GQ],
                                ps[:, 7, 0:ROW0].rearrange("p (j q) -> p j q", q=GQ)).then_inc(lat_ready, 1)

            for n in range(n_g + 3):
                if n < n_g:
                    if n % GROUPS == 0:
                        keys_of(n // GROUPS)
                    scored(n)
                if 1 <= n <= n_g:
                    normalise(n - 1)
                if n >= 3:
                    mixed(n - 3)
            dve.wait_ge(out_mm, 1)
            for a in range(2):
                link(dve.tensor_tensor(core.x_rows[:, 2 * a:2 * a + 2, :].rearrange("p i d -> p (i d)"),
                                       core.x_rows[:, 2 * a:2 * a + 2, :].rearrange("p i d -> p (i d)"),
                                       ps[:, a, :], ALU.add))
            core.dve_n = link.n


FF0 = 1024
FT0 = FF0 // P
STEP = 0.1
QMIN, QMAX = -32768.0, 32767.0
ROUND = 1.5 * 2.0 ** 23


def lookup_ffn(core):
    nc, dram, ps = core.nc, core.dram, core.psum
    k_ln = core.new_norm()
    dve0 = core.dve_n
    ctx = ExitStack()
    with ctx:
        def sb(name, shape, dt=F32):
            return ctx.enter_context(nc.sbuf_tensor(name, shape, dt))
        w1 = sb("f_w1", [P, DC, FF0])
        w2 = sb("f_w2", [P, FT0, D])
        tenths = sb("f_tenths", [P, 2, TOK])
        act_t = sb("f_act_t", [P, FT0, T])
        sem = core.sem
        w_in, up_mm, rounded, acted, out_mm = (sem("f_" + n) for n in
                                               ("weights_in", "up_mm", "rounded", "acted", "out_mm"))
        block = ctx.enter_context(nc.Block())

        @block.sync
        def _(sp):
            sp.dma_start(w1[:, :, :], dram["f_w1"]).then_inc(w_in, DMA)
            sp.dma_start(w2[:, :, :], dram["f_w2"]).then_inc(w_in, DMA)

        @block.gpsimd
        def _(pool):
            core.ln_pool(pool, k_ln)

        @block.tensor
        def _(pe):
            core.ln_tensor(pe, k_ln)
            pe.wait_ge(core.ln_cols, core.cols_ready(k_ln))
            pe.wait_ge(w_in, 2 * DMA)
            for f in range(FT0):
                if f >= 4:
                    pe.wait_ge(rounded, f - 3)
                for c in range(DC):
                    ins = pe.matmul(packed(ps[:, 2 + f % 4, 0:TOK]), w1[:, c, f * P:(f + 1) * P], core.tok(c),
                                    start=(c == 0), stop=(c == DC - 1))
                ins.then_inc(up_mm, 1)
            pe.wait_ge(acted, FT0)
            for i in range(PAIRS):
                for f in range(FT0):
                    ins = pe.matmul(ps[:, 6 + i // 2, (i % 2) * D:(i % 2 + 1) * D],
                                    act_t[:, f, i * P:(i + 1) * P], w2[:, f, :],
                                    start=(f == 0), stop=(f == FT0 - 1))
            ins.then_inc(out_mm, 1)

        @block.scalar
        def _(act):
            core.ln_scalar(act, k_ln)
            for f in range(FT0):
                act.wait_ge(rounded, f + 1)
                act.activation(unpad(act_t[:, f, :]), packed(tenths[:, f % 2, :]), ACT.Gelu_apprx_tanh,
                               scale=STEP).then_inc(acted, 1)

        @block.vector
        def _(dve):
            link = InOrder(dve, core.dve_step, dve0)
            link(dve.memset(act_t[:, :, :], 0.0))
            core.ln_vector(dve, link, k_ln)
            for f in range(FT0):
                dve.wait_ge(up_mm, f + 1)
                if f >= 2:
                    dve.wait_ge(acted, f - 1)
                t = tenths[:, f % 2, :]
                link(dve.tensor_scalar(t, ps[:, 2 + f % 4, 0:TOK], 1.0 / STEP, QMIN, ALU.mult, ALU.max))
                link(dve.tensor_scalar(t, t, QMAX, ROUND, ALU.min, ALU.add))
                dve.tensor_scalar(t, t, ROUND, None, ALU.subtract).then_inc(rounded, 1)
            dve.wait_ge(out_mm, 1)
            for a in range(2):
                rows = core.x_rows[:, 2 * a:2 * a + 2, :].rearrange("p i d -> p (i d)")
                link(dve.tensor_tensor(rows, rows, ps[:, 6 + a, :], ALU.add))
            core.dve_n = link.n


NH2, HD2, FD2 = 16, 16, 64
HP = NH2 // 2
VW = 2 * HD2 + 1
BW = 2 * HD2 + 2
FG = 512
AHEAD = 8


def memory_attention_and_features(core):
    nc, dram, ps = core.nc, core.dram, core.psum
    k_ln = core.new_norm()
    dve0, Z = core.dve_n, AHEAD
    ctx = ExitStack()
    with ctx:
        def sb(name, shape, dt=F32):
            return ctx.enter_context(nc.sbuf_tensor("c_" + name, shape, dt))
        ctx_t = sb("ctx_t", [P, 2, 2, DC, LK])
        ctx_r = sb("ctx_r", [KP, 2, 2, KT, D])
        w_k = sb("w_k", [P, DC, D])
        w_v = sb("w_v", [P, DC, D])
        b_k = sb("b_k", [P, 2])
        w_kf = sb("w_kf", [P, FG])
        mask2 = sb("mask2", [KP, B, KT])
        zero = sb("zero", [1, 512])
        q_pair = sb("q_pair", [P, 2, DC, P])
        mask_u8 = sb("mask_u8", [P, LK // 4], I32)
        mask_add = sb("mask_add", [P, LK])
        any_key = sb("any_key", [P, 1])
        prob = sb("prob", [P, LK])
        neg_max = sb("neg_max", [P, 1])
        sums = sb("sums", [P, 1])
        inv = sb("inv", [P, 1])
        prob_t = sb("prob_t", [KP, KT, P])
        k_t = sb("k_t", [P, 2, LK])
        feat = sb("feat", [KP, 2, 2, FG])
        v_aug = sb("v_aug", [KP, KT, HP, VW])
        sums_sb = sb("sums_sb", [P, 512])
        sem = core.sem
        w_in = sem("c_weights_in")
        ctx_in = [sem("c_ctx_in0"), sem("c_ctx_in1")]
        mask_in = sem("c_mask_in")
        names = ("q_staged", "score_mm", "maxed", "mask_read", "exped", "turned", "turned_sb", "out_mm", "added",
                 "kt_mm", "kt_sb", "v_mm", "v_sb", "feat_mm", "feat_act", "feat_dve", "sum_mm", "sum_sb",
                 "sum_turned", "sum_kept")
        (q_staged, score_mm, maxed, mask_read, exped, turned, turned_sb, out_mm, added, kt_mm, kt_sb, v_mm, v_sb,
         feat_mm, feat_act, feat_dve, sum_mm, sum_sb, sum_turned, sum_kept) = (
            sem("c_" + n) for n in names)
        kv_sums = core.kv_sums
        block = ctx.enter_context(nc.Block())

        @block.sync
        def _(sp):
            for dst, src in ((w_k[:, :, :], "c_w_k"), (w_v[:, :, :], "c_w_v"), (b_k[:, :], "c_b_k"),
                             (w_kf[:, :], "c_w_kf"), (mask2[:, :, :], "c_mask2")):
                sp.dma_start(dst, dram[src]).then_inc(w_in, DMA)
            with sp.Fori(0, 2) as i:
                for j in range(2):
                    n = 2 * i + j
                    sp.wait_ge(mask_read, Z + n)
                    for k in range(2):
                        sp.dma_start(mask_u8[k * SP:(k + 1) * SP, :],
                                     dram["c_mask"][2 * n + k].partition_broadcast(SP)).then_inc(mask_in, DMA)
                    sp.wait_ge(sum_turned, Z + 2 * (n - 1))
                    for k in range(2):
                        sp.dma_start(ctx_t[:, j, k, :, :], dram["ctx_t"][2 * n + k]).then_inc(ctx_in[j], DMA)
                        sp.dma_start(ctx_r[:, j, k, :, :], dram["ctx_r"][2 * n + k]).then_inc(ctx_in[j], DMA)

        @block.gpsimd
        def _(pool):
            core.ln_pool(pool, k_ln)
            pool.sem_inc(q_staged, Z)
            pool.wait_ge(core.ln_cols, core.cols_ready(k_ln))
            with pool.Fori(0, 2) as i:
                for j in range(2):
                    n = 2 * i + j
                    pool.wait_ge(score_mm, Z + n - 1)
                    pool.tensor_copy(q_pair[:, j, :, :], core.xn_cols[:, :, bass.ds(n * P, P)]) \
                        .then_inc(q_staged, 1)

        @block.tensor
        def _(pe):
            for s in (score_mm, turned, out_mm, kt_mm, v_mm, feat_mm, sum_mm, sum_turned):
                pe.sem_inc(s, Z)
            core.ln_tensor(pe, k_ln)
            pe.wait_ge(w_in, 5 * DMA)

            def scores(n, i, j):
                pe.wait_ge(ctx_in[j], 4 * DMA * (i + 1))
                pe.wait_ge(q_staged, Z + n + 1)
                pe.wait_ge(added, Z + n)
                for k in range(2):
                    for m in range(3):
                        for c in range(DC):
                            ins = pe.matmul(ps[k * SP:(k + 1) * SP, m, 0:KN], q_pair[:, j, c, k * SP:(k + 1) * SP],
                                            ctx_t[:, j, k, c, m * KN:(m + 1) * KN],
                                            start=(c == 0), stop=(c == DC - 1))
                ins.then_inc(score_mm, 1)

            def attend(n, j):
                pe.wait_ge(exped, Z + n + 1)
                for u in range(3):
                    if u == 2:
                        pe.wait_ge(turned_sb, Z + 3 * n + 1)
                    for x in range(4):
                        t = 4 * u + x
                        ins = pe.transpose(ps[0:KP, u % 2, x * P:(x + 1) * P], prob[:, t * KP:(t + 1) * KP],
                                           core.ident[:, :])
                    ins.then_inc(turned, 1)
                pe.wait_ge(turned_sb, Z + 3 * n + 3)
                for k in range(2):
                    for t in range(KT):
                        ins = pe.matmul(ps[k * SP:(k + 1) * SP, 2, 0:D], prob_t[:, t, k * SP:(k + 1) * SP],
                                        ctx_r[:, j, k, t, :], start=(t == 0), stop=(t == KT - 1))
                ins.then_inc(out_mm, 1)

            def features(b, j, k):
                for e in range(6):
                    g, m = e // 3, e % 3
                    if e == 0:
                        pe.wait_ge(feat_act, Z + KT * b)
                        pe.wait_ge(feat_dve, Z + KT * b)
                    if e >= 3:
                        pe.wait_ge(kt_sb, Z + 6 * b + e - 2)
                    for c in range(DC):
                        ins = pe.matmul(ps[:, 4 + e % 3, 0:KN], w_k[:, c, g * P:(g + 1) * P],
                                        ctx_t[:, j, k, c, m * KN:(m + 1) * KN],
                                        start=(c == 0), stop=(c == DC - 1))
                    ins.then_inc(kt_mm, 1)
                pe.wait_ge(sum_sb, Z + b)
                pe.matmul(ps[:, 7, :], zero[0:1, 0:P], zero[0:1, :], start=True, stop=True,
                          skip_group_check=True)
                for t in range(KT + 1):
                    if t < KT and t % 2 == 0:
                        if t == 0:
                            pe.wait_ge(sum_kept, Z + b)
                        pe.wait_ge(v_sb, Z + 6 * b + t // 2)
                        for x in range(2):
                            for c in range(DC):
                                ins = pe.matmul(ps[0:KP, 3, x * D:(x + 1) * D],
                                                ctx_t[:, j, k, c, (t + x) * KP:(t + x + 1) * KP], w_v[:, c, :],
                                                start=(c == 0), stop=(c == DC - 1))
                        ins.then_inc(v_mm, 1)
                    if t < KT:
                        for g in range(2):
                            m = 2 * t + g
                            if m < 3:
                                pe.wait_ge(kt_sb, Z + 6 * b + 6)
                            else:
                                pe.wait_ge(feat_act if (m - 3) % 2 == 0 else feat_dve,
                                           Z + KT * b + (m - 3) // 2 + 1)
                            pe.matmul(ps[0:KP, 4 + m % 3, :], k_t[:, g, t * KP:(t + 1) * KP], w_kf[:, :],
                                      start=True, stop=True).then_inc(feat_mm, 1)
                    if t >= 1:
                        u = t - 1
                        pe.wait_ge(feat_act, Z + KT * b + u + 1)
                        pe.wait_ge(feat_dve, Z + KT * b + u + 1)
                        pe.wait_ge(v_sb, Z + 6 * b + u // 2 + 1)
                        for p in range(HP):
                            r = (p % 2) * SP
                            ins = pe.matmul(ps[r:r + VW, 7, (p // 2) * P:(p // 2 + 1) * P], v_aug[:, u, p, :],
                                            feat[:, u % 2, p // 4, (p % 4) * P:(p % 4 + 1) * P],
                                            start=False, stop=False, skip_group_check=True)
                        ins.then_inc(sum_mm, 1)
                pe.wait_ge(sum_sb, Z + b + 1)
                for q in range(HP // 2):
                    ins = pe.transpose(ps[:, 3, q * P:(q + 1) * P], sums_sb[:, q * P:(q + 1) * P],
                                       core.ident[:, :])
                ins.then_inc(sum_turned, 1)

            with pe.Fori(0, 2) as i:
                for j in range(2):
                    n = 2 * i + j
                    scores(n, i, j)
                    features(2 * n, j, 0)
                    attend(n, j)
                    features(2 * n + 1, j, 1)

        @block.scalar
        def _(act):
            for s in (exped, turned_sb, kt_sb, feat_act, sum_sb):
                act.sem_inc(s, Z)
            core.ln_scalar(act, k_ln)
            act.wait_ge(w_in, 5 * DMA)

            def features(b):
                for e in range(6):
                    act.wait_ge(kt_mm, Z + 6 * b + e + 1)
                    act.activation(k_t[:, e // 3, (e % 3) * KN:(e % 3 + 1) * KN], ps[:, 4 + e % 3, 0:KN],
                                   ACT.Identity, bias=b_k[:, e // 3:e // 3 + 1]).then_inc(kt_sb, 1)
                for t in range(KT):
                    act.wait_ge(feat_mm, Z + 2 * KT * b + 2 * t + 1)
                    act.wait_ge(sum_mm, Z + KT * b + t - 1)
                    act.activation(feat[:, t % 2, 0, :], ps[0:KP, 4 + (2 * t) % 3, :], ACT.Relu) \
                        .then_inc(feat_act, 1)
                act.wait_ge(sum_mm, Z + KT * (b + 1))
                act.copy(sums_sb[:, :], ps[:, 7, :]).then_inc(sum_sb, 1)

            with act.Fori(0, 2) as i:
                for j in range(2):
                    n = 2 * i + j
                    act.wait_ge(maxed, Z + n + 1)
                    act.activation(prob[:, :], prob[:, :], ACT.Exp, bias=neg_max[:, 0:1],
                                   accum_out=sums[:, 0:1]).then_inc(exped, 1)
                    features(2 * n)
                    for u in range(3):
                        act.wait_ge(turned, Z + 3 * n + u + 1)
                        act.copy(prob_t[:, 4 * u:4 * u + 4, :].rearrange("p t q -> p (t q)"),
                                 ps[0:KP, u % 2, :]).then_inc(turned_sb, 1)
                    features(2 * n + 1)

        @block.vector
        def _(dve):
            link = InOrder(dve, core.dve_step, dve0)
            for s in (maxed, mask_read, added, v_sb, feat_dve, sum_kept):
                dve.sem_inc(s, Z)
            link(dve.memset(zero[:, :], 0.0))
            link(dve.memset(kv_sums[:, :, :, :], 0.0))
            core.ln_vector(dve, link, k_ln)
            dve.wait_ge(w_in, 5 * DMA)

            def softmax(n):
                dve.wait_ge(mask_in, 2 * DMA * (n + 1))
                dve.tensor_scalar(mask_add[:, :], mask_u8[:, :].bitcast(U8), 1.0, -NEG, ALU.subtract, ALU.mult) \
                    .then_inc(mask_read, 1)
                dve.wait_ge(mask_read, Z + n + 1)
                link(dve.tensor_reduce(any_key[:, :], mask_add[:, :], AXIS.X, ALU.max))
                link(dve.tensor_scalar(any_key[:, :], any_key[:, :], 0.0, None, ALU.is_equal))
                dve.wait_ge(score_mm, Z + n + 1)
                dve.wait_ge(turned, Z + 3 * n)
                link(dve.scalar_tensor_tensor(prob[:, :].rearrange("p (m n) -> p m n", m=3), ps[:, 0:3, 0:KN],
                                              1.0 / 16.0, mask_add[:, :].rearrange("p (m n) -> p m n", m=3),
                                              ALU.mult, ALU.add))
                dve.tensor_reduce(neg_max[:, :], prob[:, :], AXIS.X, ALU.max, negate=True).then_inc(maxed, 1)

            def add_out(n):
                dve.wait_ge(exped, Z + n + 1)
                link(dve.reciprocal(inv[:, :], sums[:, :]))
                link(dve.tensor_tensor(inv[:, :], inv[:, :], any_key[:, :], ALU.mult))
                dve.wait_ge(out_mm, Z + n + 1)
                row = core.x_rows[:, bass.ds(n, 1), :].rearrange("p a d -> p (a d)")
                dve.scalar_tensor_tensor(row, ps[:, 2, 0:D], inv[:, 0:1], row,
                                         ALU.mult, ALU.add).then_inc(added, 1)

            def features(b):
                dve.wait_ge(sum_mm, Z + KT * b)
                link(dve.tensor_copy(v_aug[:, :, :, 2 * HD2],
                                     mask2[:, bass.ds(b, 1), :].rearrange("p a t -> p (a t)").unsqueeze(2)
                                     .to_broadcast([KP, KT, HP])))
                for t in range(KT):
                    if t % 2 == 0:
                        dve.wait_ge(v_mm, Z + 6 * b + t // 2 + 1)
                        for x in range(2):
                            ins = dve.tensor_scalar(v_aug[:, t + x, :, 0:2 * HD2],
                                                    ps[0:KP, 3, x * D:(x + 1) * D].rearrange("p (h e) -> p h e", h=HP),
                                                    mask2[:, bass.ds(b, 1), t + x:t + x + 1]
                                                    .rearrange("p a t -> p (a t)"), None, ALU.mult)
                            if x == 0:
                                link(ins)
                        ins.then_inc(v_sb, 1)
                    dve.wait_ge(feat_mm, Z + 2 * KT * b + 2 * t + 2)
                    dve.wait_ge(sum_mm, Z + KT * b + t - 1)
                    dve.tensor_scalar(feat[:, t % 2, 1, :], ps[0:KP, 4 + (2 * t + 1) % 3, :], 0.0, None,
                                      ALU.max).then_inc(feat_dve, 1)
                dve.wait_ge(sum_turned, Z + b + 1)
                turned_sums = ps[:, 3, :].rearrange("p (h w) -> p h w", w=SP)
                dst = kv_sums[:, bass.ds(b, 1), :, :].rearrange("p a h w -> p (a h) w")
                lo, hi = slice(0, FD2), slice(FD2, P)
                link(dve.tensor_copy(dst[lo, :, 0:HD2], turned_sums[lo, :, 0:HD2]))
                link(dve.tensor_copy(dst[hi, :, HD2:2 * HD2], turned_sums[hi, :, HD2:2 * HD2]))
                link(dve.tensor_copy(dst[lo, :, 2 * HD2], turned_sums[lo, :, 2 * HD2]))
                dve.tensor_copy(dst[hi, :, 2 * HD2 + 1], turned_sums[hi, :, 2 * HD2]).then_inc(sum_kept, 1)

            first, per_pair = link.n, 3 + 2 + 2 * (1 + KT // 2 + 3)
            with dve.Fori(0, 2) as i:
                link.loop(i, first, 2 * per_pair)
                for j in range(2):
                    n = 2 * i + j
                    softmax(n)
                    features(2 * n)
                    add_out(n)
                    features(2 * n + 1)
            link.end(first, 2 * per_pair, 2)
            core.dve_n = link.n


def linear_attention(core):
    nc, dram, ps = core.nc, core.dram, core.psum
    k_ln = core.new_norm()
    dve0 = core.dve_n
    ctx = ExitStack()
    with ctx:
        def sb(name, shape, dt=F32):
            return ctx.enter_context(nc.sbuf_tensor("l_" + name, shape, dt))
        w_q = sb("w_q", [P, DC, D])
        w_o = sb("w_o", [P, DC, D])
        w_qf = sb("w_qf", [P, FG])
        b_q = sb("b_q", [P, 2])
        b_v = sb("b_v", [P, D])
        b_o = sb("b_o", [P, D])
        q_t = sb("q_t", [P, 2, T])
        feat_t = sb("feat_t", [P, HP, T])
        den = sb("den", [P, PAIRS, NH2])
        vals = sb("vals", [P, PAIRS, D])
        bias = sb("bias", [P, PAIRS, D])
        vals_t = sb("vals_t", [P, DC, T])
        sem = core.sem
        w_in, q_mm, q_sb, feat_mm, feat_sb, att_mm, divided, turned, turned_sb, out_mm = (sem("l_" + n) for n in (
            "weights_in", "q_mm", "q_sb", "feat_mm", "feat_sb", "att_mm", "divided", "turned", "turned_sb",
            "out_mm"))
        loads = ((w_q[:, :, :], "l_w_q"), (w_o[:, :, :], "l_w_o"), (w_qf[:, :], "l_w_qf"), (b_q[:, :], "l_b_q"))
        block = ctx.enter_context(nc.Block())

        @block.sync
        def _(sp):
            for dst, src in loads:
                sp.dma_start(dst, dram[src]).then_inc(w_in, DMA)
            sp.dma_start(b_v[:, :], dram["l_b_v"].partition_broadcast(P)).then_inc(w_in, DMA)
            sp.dma_start(b_o[:, :], dram["l_b_o"].partition_broadcast(P)).then_inc(w_in, DMA)
        n_in = DMA * (len(loads) + 2)

        @block.gpsimd
        def _(pool):
            core.ln_pool(pool, k_ln)

        @block.tensor
        def _(pe):
            core.ln_tensor(pe, k_ln)
            pe.wait_ge(core.ln_cols, core.cols_ready(k_ln))
            pe.wait_ge(w_in, n_in)
            for g in range(2):
                for c in range(DC):
                    ins = pe.matmul(ps[:, 2 + g, :], w_q[:, c, g * P:(g + 1) * P], core.xn_cols[:, c, :],
                                    start=(c == 0), stop=(c == DC - 1))
                ins.then_inc(q_mm, 1)
            for p in range(HP):
                if p % 4 == 0:
                    pe.wait_ge(q_sb, p // 4 + 1)
                if p >= 4:
                    pe.wait_ge(feat_sb, p - 3)
                pe.matmul(ps[:, 4 + p % 4, :], w_qf[:, (p % 4) * P:(p % 4 + 1) * P], q_t[:, p // 4, :],
                          start=True, stop=True).then_inc(feat_mm, 1)
            pe.wait_ge(feat_sb, HP)
            for b in range(B):
                for p in range(HP):
                    ins = pe.matmul(ps[(b % 2) * SP:(b % 2 + 1) * SP, b // 2, p * BW:(p + 1) * BW],
                                    feat_t[:, p, b * SP:(b + 1) * SP], core.kv_sums[:, b, p, :],
                                    start=True, stop=True)
                if b % 2:
                    ins.then_inc(att_mm, 1)
            for i in range(PAIRS):
                pe.wait_ge(divided, i + 1)
                for c in range(DC):
                    ins = pe.transpose(ps[:, 4 + c, i * P:(i + 1) * P], vals[:, i, c * P:(c + 1) * P],
                                       core.ident[:, :])
            ins.then_inc(turned, 1)
            pe.wait_ge(turned_sb, DC)
            for i in range(PAIRS):
                for c in range(DC):
                    ins = pe.matmul(ps[:, 6 + i // 2, (i % 2) * D:(i % 2 + 1) * D],
                                    vals_t[:, c, i * P:(i + 1) * P], w_o[:, c, :],
                                    start=(c == 0), stop=(c == DC - 1))
            ins.then_inc(out_mm, 1)

        @block.scalar
        def _(act):
            core.ln_scalar(act, k_ln)
            act.wait_ge(w_in, n_in)
            for g in range(2):
                act.wait_ge(q_mm, g + 1)
                act.activation(q_t[:, g, :], ps[:, 2 + g, :], ACT.Identity, bias=b_q[:, g:g + 1]) \
                    .then_inc(q_sb, 1)
            for p in range(HP):
                act.wait_ge(feat_mm, p + 1)
                act.activation(feat_t[:, p, :], ps[:, 4 + p % 4, :], ACT.Relu).then_inc(feat_sb, 1)
            act.wait_ge(turned, 1)
            for c in range(DC):
                act.copy(vals_t[:, c, :], ps[:, 4 + c, :]).then_inc(turned_sb, 1)

        @block.vector
        def _(dve):
            link = InOrder(dve, core.dve_step, dve0)
            core.ln_vector(dve, link, k_ln)
            dve.wait_ge(w_in, n_in)
            for i in range(PAIRS):
                dve.wait_ge(att_mm, i + 1)
                got = ps[:, i, 0:HP * BW].rearrange("p (h w) -> p h w", w=BW)
                row = vals[:, i, :].rearrange("p (h e) -> p h e", e=HD2)
                bias_row = bias[:, i, :].rearrange("p (h e) -> p h e", e=HD2)
                each = den[:, i, :].rearrange("p (h k) -> p h k", k=2)
                link(dve.tensor_copy(each, got[:, :, 2 * HD2:BW]))
                link(dve.tensor_tensor(bias_row, b_v[:, :].rearrange("p (h e) -> p h e", e=HD2),
                                       den[:, i, :].unsqueeze(2).to_broadcast([P, NH2, HD2]), ALU.mult))
                link(dve.tensor_tensor(vals[:, i, :].rearrange("p (h e) -> p h e", h=HP),
                                       bias[:, i, :].rearrange("p (h e) -> p h e", h=HP),
                                       got[:, :, 0:2 * HD2], ALU.add))
                link(dve.tensor_scalar(den[:, i, :], den[:, i, :], 1e-8, None, ALU.add))
                link(dve.reciprocal(den[:, i, :], den[:, i, :]))
                dve.tensor_tensor(row, row, den[:, i, :].unsqueeze(2).to_broadcast([P, NH2, HD2]),
                                  ALU.mult).then_inc(divided, 1)
            for i in range(PAIRS):
                link(dve.tensor_tensor(core.x_rows[:, i, :], core.x_rows[:, i, :], b_o[:, :], ALU.add))
            dve.wait_ge(out_mm, 1)
            for a in range(2):
                rows = core.x_rows[:, 2 * a:2 * a + 2, :].rearrange("p i d -> p (i d)")
                link(dve.tensor_tensor(rows, rows, ps[:, 6 + a, :], ALU.add))
            core.dve_n = link.n


FF2 = 704
FT2 = -(-FF2 // P)
FP8_MAX = 448.0
GLOBAL_DIV = 448.0 * 6.0
EXPONENT = 0x7F800000
FP8_LEAST = 2.0 ** -6
FP8_ROUND = 1.5 * 2.0 ** 20


def quantised_ffn(core):
    nc, dram, ps = core.nc, core.dram, core.psum
    k_ln = core.new_norm(turned=False)
    dve0, pool0 = core.dve_n, core.pool_n
    ctx = ExitStack()
    with ctx:
        def sb(name, shape, dt=F32):
            return ctx.enter_context(nc.sbuf_tensor("q_" + name, shape, dt))
        order = sb("order", [P, FT2], I32)
        w_rows = sb("w_rows", [P, 2, FT2, D])
        w_cols = sb("w_cols", [P, 2, DC, FT2 * P])
        wd_rows = sb("wd_rows", [P, DC, FF2])
        wd_cols = sb("wd_cols", [P, FT2, D])
        peak = sb("peak", [P, 2 * FT2 + DC])
        w_scale = sb("w_scale", [P, 2 * FT2 + DC])
        w_inv = sb("w_inv", [P, 2 * FT2 + DC])
        unit = sb("unit", [P, 2, FF2])
        row_peak = sb("row_peak", [P, PAIRS])
        all_peak = sb("all_peak", [P, 4])
        row_scale = sb("row_scale", [P, PAIRS])
        row_inv = sb("row_inv", [P, PAIRS])
        row_peak2 = sb("row_peak2", [P, PAIRS])
        all_peak2 = sb("all_peak2", [P, 4])
        row_scale2 = sb("row_scale2", [P, PAIRS])
        row_inv2 = sb("row_inv2", [P, PAIRS])
        xq = sb("xq", [P, PAIRS, D])
        xq_cols = sb("xq_cols", [P, DC, T])
        silu = sb("silu", [P, 2, FF2])
        hid = sb("hid", [P, PAIRS, FF2])
        hid_cols = sb("hid_cols", [P, 2, FT2, P])
        sem = core.sem
        (order_in, rows_in, wd_in, w_quant, w_turned, w_cols_ready, peak_known, peak_all, x_quant, x_turned,
         x_cols_ready, up_mm, silued, hid_ready, peak2_known, peak2_all, hid_quant, hid_turned, hid_cols_ready,
         out_mm) = (sem("q_" + n) for n in (
            "order_in", "rows_in", "wd_in", "w_quant", "w_turned", "w_cols_ready", "peak_known", "peak_all",
            "x_quant", "x_turned", "x_cols_ready", "up_mm", "silued", "hid_ready", "peak2_known", "peak2_all",
            "hid_quant", "hid_turned", "hid_cols_ready", "out_mm"))
        block = ctx.enter_context(nc.Block())
        half = FF2 // 2

        @block.sync
        def _(sp):
            sp.dma_start(order[:, :], dram["q_order"]).then_inc(order_in, DMA)
            sp.dma_start(wd_rows[:, :, :], dram["q_w_down"]).then_inc(wd_in, DMA)

        @block.gpsimd
        def _(pool):
            pool.wait_ge(order_in, DMA)
            for k, src in enumerate(("q_w_gate", "q_w_up")):
                for f in range(FT2):
                    pool.indirect_dma_start(w_rows[:, k, f, :], None, dram[src],
                                            bass.IndirectOffsetOnAxis(ap=order[:, f:f + 1], axis=0)) \
                        .then_inc(rows_in, DMA)
            core.ln_pool(pool, k_ln)
            pool.wait_ge(peak_known, 1)
            pool.partition_all_reduce(all_peak[:, 1:2], all_peak[:, 0:1], P, REDUCE.max).then_inc(peak_all, 1)
            pool.wait_ge(peak2_known, 1)
            pool.partition_all_reduce(all_peak2[:, 1:2], all_peak2[:, 0:1], P, REDUCE.max).then_inc(peak2_all, 1)

        @block.tensor
        def _(pe):
            n = 0
            for k in range(2):
                for f in range(FT2):
                    pe.wait_ge(w_quant, k * FT2 + f + 1)
                    if n >= 6:
                        pe.wait_ge(w_cols_ready, n - 5)
                    for c in range(DC):
                        ins = pe.transpose(ps[:, 2 + n % 6, c * P:(c + 1) * P], w_rows[:, k, f, c * P:(c + 1) * P],
                                           core.ident[:, :])
                    ins.then_inc(w_turned, 1)
                    n += 1
            pe.wait_ge(w_quant, 2 * FT2 + DC)
            for f in range(FT2):
                w = min(P, FF2 - f * P)
                pe.wait_ge(w_cols_ready, n - 5)
                for c in range(DC):
                    ins = pe.transpose(ps[0:w, 2 + n % 6, c * P:(c + 1) * P], wd_rows[:, c, f * P:f * P + w],
                                       core.ident[:, :])
                ins.then_inc(w_turned, 1)
                n += 1
            for i in range(PAIRS):
                pe.wait_ge(x_quant, i + 1)
                for c in range(DC):
                    ins = pe.transpose(ps[:, c, i * P:(i + 1) * P], xq[:, i, c * P:(c + 1) * P], core.ident[:, :])
            ins.then_inc(x_turned, 1)
            pe.wait_ge(x_cols_ready, DC)
            pe.wait_ge(w_cols_ready, 3 * FT2)
            for i in range(PAIRS):
                if i >= 2:
                    pe.wait_ge(hid_ready, i - 1)
                for k in range(2):
                    for a in range(2):
                        for c in range(DC):
                            ins = pe.matmul(ps[:, 4 * (i % 2) + 2 * k + a, 0:half], xq_cols[:, c, i * P:(i + 1) * P],
                                            w_cols[:, k, c, a * half:(a + 1) * half],
                                            start=(c == 0), stop=(c == DC - 1))
                ins.then_inc(up_mm, 1)
            pe.wait_ge(hid_ready, PAIRS)
            for i in range(PAIRS):
                pe.wait_ge(hid_quant, i + 1)
                if i >= 2:
                    pe.wait_ge(hid_cols_ready, 2 * (i - 1))
                for f in range(FT2):
                    w = min(P, FF2 - f * P)
                    ins = pe.transpose(ps[0:w, 2 * (i % 2) + f // 4, (f % 4) * P:(f % 4 + 1) * P],
                                       hid[:, i, f * P:f * P + w], core.ident[:, :])
                ins.then_inc(hid_turned, 1)
                pe.wait_ge(hid_cols_ready, 2 * (i + 1))
                for f in range(FT2):
                    w = min(P, FF2 - f * P)
                    ins = pe.matmul(ps[:, 6 + i // 2, (i % 2) * D:(i % 2 + 1) * D], hid_cols[0:w, i % 2, f, :],
                                    wd_cols[0:w, f, :], start=(f == 0), stop=(f == FT2 - 1))
            ins.then_inc(out_mm, 1)

        @block.scalar
        def _(act):
            n = 0
            for k in range(2):
                for f in range(FT2):
                    act.wait_ge(w_turned, n + 1)
                    act.copy(w_cols[:, k, :, f * P:(f + 1) * P],
                             ps[:, 2 + n % 6, 0:D].rearrange("p (c d) -> p c d", c=DC)).then_inc(w_cols_ready, 1)
                    n += 1
            for f in range(FT2):
                w = min(P, FF2 - f * P)
                act.wait_ge(w_turned, n + 1)
                act.copy(wd_cols[0:w, f, :], ps[0:w, 2 + n % 6, 0:D]).then_inc(w_cols_ready, 1)
                n += 1
            act.wait_ge(x_turned, 1)
            for c in range(DC):
                act.copy(xq_cols[:, c, :], ps[:, c, :]).then_inc(x_cols_ready, 1)
            for i in range(PAIRS):
                act.wait_ge(up_mm, i + 1)
                if i >= 2:
                    act.wait_ge(hid_ready, i - 1)
                act.activation(silu[:, i % 2, :].rearrange("p (a n) -> p a n", a=2),
                               ps[:, 4 * (i % 2):4 * (i % 2) + 2, 0:half], ACT.Silu,
                               scale=all_peak[:, 2:3]).then_inc(silued, 1)
            for i in range(PAIRS):
                act.wait_ge(hid_turned, i + 1)
                b = 2 * (i % 2)
                act.copy(hid_cols[:, i % 2, 0:4, :].rearrange("p f n -> p (f n)"), ps[:, b, :]) \
                    .then_inc(hid_cols_ready, 1)
                act.copy(hid_cols[:, i % 2, 4, :], ps[:, b + 1, 0:P]).then_inc(core.act_step, 1)
                act.copy(hid_cols[0:FF2 % P, i % 2, 5, :], ps[0:FF2 % P, b + 1, P:2 * P]) \
                    .then_inc(hid_cols_ready, 1)

        @block.vector
        def _(dve):
            link = InOrder(dve, core.dve_step, dve0)

            def rounded(v, e, out_scale, done=None):
                link(dve.tensor_scalar(e.bitcast(U32), v.bitcast(U32), EXPONENT, None, ALU.bitwise_and))
                link(dve.tensor_scalar(e, e, FP8_LEAST, FP8_ROUND, ALU.max, ALU.mult))
                link(dve.tensor_tensor(v, v, e, ALU.add))
                link(dve.tensor_tensor(v, v, e, ALU.subtract))
                ins = dve.tensor_scalar(v, v, out_scale, None, ALU.mult)
                if done is None:
                    link(ins)
                else:
                    ins.then_inc(done, 1)

            def scales(peak, scale, inv):
                link(dve.tensor_scalar(scale, peak, 1.0 / FP8_MAX, 1e-30, ALU.mult, ALU.max))
                link(dve.reciprocal(inv, scale))

            dve.wait_ge(rows_in, DMA * 2 * FT2)
            dve.wait_ge(wd_in, DMA)
            tiles = [(w_rows[:, k, f, :], D) for k in range(2) for f in range(FT2)]
            tiles += [(wd_rows[:, c, :], FF2) for c in range(DC)]
            for n, (w, _) in enumerate(tiles):
                link(dve.tensor_reduce(peak[:, n:n + 1], w, AXIS.X, ALU.max, apply_absolute_value=True))
            scales(peak[:, :], w_scale[:, :], w_inv[:, :])
            for n, (w, size) in enumerate(tiles):
                link(dve.tensor_scalar(w, w, w_inv[:, n:n + 1], None, ALU.mult))
                rounded(w, unit[:, 0, 0:size], w_scale[:, n:n + 1], w_quant)

            core.ln_vector(dve, link, k_ln)
            dve.wait_ge(core.ln_rows, PAIRS * (k_ln + 1))

            def global_scale(rows_peak, g, known, reduced):
                link(dve.tensor_reduce(g[:, 0:1], rows_peak[:, :], AXIS.X, ALU.max))
                known_ins = dve.tensor_copy(g[:, 3:4], g[:, 0:1])
                known_ins.then_inc(known, 1)
                dve.wait_ge(reduced, 1)
                link(dve.tensor_scalar(g[:, 2:3], g[:, 1:2], 1.0 / GLOBAL_DIV, 1e-30, ALU.mult, ALU.max))
                link(dve.reciprocal(g[:, 3:4], g[:, 2:3]))
                link(dve.tensor_scalar(rows_peak[:, :], rows_peak[:, :], g[:, 3:4], None, ALU.mult))

            link(dve.tensor_reduce(row_peak[:, :], core.xn_rows[:, :, :], AXIS.X, ALU.max,
                                   apply_absolute_value=True))
            global_scale(row_peak, all_peak, peak_known, peak_all)
            scales(row_peak[:, :], row_scale[:, :], row_inv[:, :])
            for i in range(PAIRS):
                link(dve.tensor_scalar(xq[:, i, :], core.xn_rows[:, i, :], all_peak[:, 3:4], row_inv[:, i:i + 1],
                                       ALU.mult, ALU.mult))
                rounded(xq[:, i, :], unit[:, 0, 0:D], row_scale[:, i:i + 1], x_quant)
            for i in range(PAIRS):
                dve.wait_ge(silued, i + 1)
                dve.scalar_tensor_tensor(hid[:, i, :].rearrange("p (a n) -> p a n", a=2),
                                         ps[:, 4 * (i % 2) + 2:4 * (i % 2) + 4, 0:half], all_peak[:, 2:3],
                                         silu[:, i % 2, :].rearrange("p (a n) -> p a n", a=2),
                                         ALU.mult, ALU.mult).then_inc(hid_ready, 1)
                dve.wait_ge(hid_ready, i + 1)
                link(dve.tensor_reduce(row_peak2[:, i:i + 1], hid[:, i, :], AXIS.X, ALU.max,
                                       apply_absolute_value=True))
            global_scale(row_peak2, all_peak2, peak2_known, peak2_all)
            scales(row_peak2[:, :], row_scale2[:, :], row_inv2[:, :])
            for i in range(PAIRS):
                link(dve.tensor_scalar(hid[:, i, :], hid[:, i, :], all_peak2[:, 3:4], row_inv2[:, i:i + 1],
                                       ALU.mult, ALU.mult))
                rounded(hid[:, i, :], unit[:, 1, :], row_scale2[:, i:i + 1], hid_quant)
            dve.wait_ge(out_mm, 1)
            for a in range(2):
                rows = core.x_rows[:, 2 * a:2 * a + 2, :].rearrange("p i d -> p (i d)")
                link(dve.scalar_tensor_tensor(rows, ps[:, 6 + a, :], all_peak2[:, 2:3], rows, ALU.mult, ALU.add))
            core.dve_n = link.n


RT = H * S // P
WS = 4
F32R = mybir.dt.float32r


def full_attention(core):
    nc, dram, ps = core.nc, core.dram, core.psum
    k_ln = core.new_norm()
    dve0, Z = core.dve_n, AHEAD
    ctx = ExitStack()
    with ctx:
        def sb(name, shape, dt=F32):
            return ctx.enter_context(nc.sbuf_tensor("a_" + name, shape, dt))
        w = sb("w", [P, WS, 2 * D])
        head_cols = sb("head_cols", [P, 2, T])
        q_all = sb("q_all", [P, DC, B, H * S])
        q_tile = sb("q_tile", [P, 2, DC, P])
        q_hi = sb("q_hi", [P, 2, DC, P], F32R)
        q_lo = sb("q_lo", [P, 2, DC, P], F32R)
        raw = sb("raw", [P, KT * D])
        t_hi = sb("t_hi", [P, 2, DC, LK], F32R)
        t_lo = sb("t_lo", [P, 2, DC, LK], F32R)
        r_hi = sb("r_hi", [KP, KT, D], F32R)
        r_lo = sb("r_lo", [KP, KT, D], F32R)
        neg_max = sb("neg_max", [P, 2])
        sums = sb("sums", [P, 2])
        inv = sb("inv", [P, 2])
        prob = sb("prob", [P, 2, LK])
        p_hi = sb("p_hi", [KP, KT, P], F32R)
        p_lo = sb("p_lo", [KP, KT, P], F32R)
        mixed = sb("mixed", [P, 2, D])
        zero = sb("zero", [1, 512])
        q_head = head_cols[:, :, 0:TOK]
        v_head = head_cols
        sem = core.sem
        w_in = [sem(f"a_w_in{s}") for s in range(WS)]
        names = ("raw_in", "t_hi_ready", "t_lo_ready", "r_hi_ready", "r_lo_ready", "head_mm", "head_sb",
                 "fold_mm", "fold_sb", "q_staged", "q_hi_ready", "q_lo_ready", "score_mm", "maxed", "exped", "turned",
                 "p_hi_ready", "p_lo_ready", "mix_mm", "mix_sb", "mix_turned", "mix_kept", "v_mm", "v_sb", "out_mm")
        (raw_in, t_hi_ready, t_lo_ready, r_hi_ready, r_lo_ready, head_mm, head_sb,
         fold_mm, fold_sb, q_staged, q_hi_ready, q_lo_ready, score_mm, maxed, exped, turned,
         p_hi_ready, p_lo_ready, mix_mm, mix_sb, mix_turned, mix_kept, v_mm, v_sb, out_mm) = (
            sem("a_" + n) for n in names)
        turns = H // WS
        scale = 1.0 / float(np.sqrt(HD))
        raw_t = raw[:, 0:DC * LK].rearrange("p (c k) -> p c k", c=DC)
        raw_r = raw[0:KP, :].rearrange("p (t d) -> p t d", t=KT)

        def query_tile(i, x):
            return q_all[:, :, bass.ds(2 * i + x // RT, 1), x % RT * P:(x % RT + 1) * P] \
                .rearrange("p c b n -> p c (b n)")
        block = ctx.enter_context(nc.Block())

        @block.sync
        def _(sp):
            def weights(n, s):
                sp.dma_start(w[:, s, :], dram["a_w"][n]).then_inc(w_in[s], DMA)

            def context_turned(b):
                sp.wait_ge(r_hi_ready, Z + 3 * b)
                sp.wait_ge(r_lo_ready, Z + 3 * b)
                sp.dma_start(raw_t, dram["ctx_t"][b]).then_inc(raw_in, DMA)

            def context_rows(b):
                sp.wait_ge(t_hi_ready, Z + 2 * (b + 1))
                sp.wait_ge(t_lo_ready, Z + 2 * (b + 1))
                sp.dma_start(raw_r, dram["ctx_r"][b]).then_inc(raw_in, DMA)
            for s in range(WS):
                weights(s, s)
            context_turned(0)
            context_rows(0)
            with sp.Fori(1, turns) as i:
                for s in range(WS):
                    sp.wait_ge(fold_mm, Z + (i - 1) * WS + s + 1)
                    weights(i * WS + s, s)
            with sp.Fori(1, B) as b:
                context_turned(b)
                context_rows(b)
            for s in range(WS):
                weights(H + s, s)
            with sp.Fori(1, turns) as i:
                for s in range(WS):
                    sp.wait_ge(out_mm, Z + (i - 1) * WS + s + 1)
                    weights((turns + i) * WS + s, s)

        @block.gpsimd
        def _(pool):
            core.ln_pool(pool, k_ln)
            pool.sem_inc(q_staged, Z)
            pool.wait_ge(fold_sb, Z + H)
            with pool.Fori(0, PAIRS) as i:
                for x in range(2 * RT):
                    n = i * 2 * RT + x
                    pool.wait_ge(q_lo_ready, Z + n - 1)
                    pool.tensor_copy(q_tile[:, x % 2, :, :], query_tile(i, x)).then_inc(q_staged, 1)

        @block.tensor
        def _(pe):
            for x in (head_mm, fold_mm, score_mm, turned, mix_mm, mix_turned, v_mm, out_mm):
                pe.sem_inc(x, Z)
            core.ln_tensor(pe, k_ln)
            pe.wait_ge(core.ln_cols, core.cols_ready(k_ln))

            def head(n, i, s):
                pe.wait_ge(w_in[s], DMA * (i + 1))
                pe.wait_ge(head_sb, Z + n - 1)
                for c in range(DC):
                    ins = pe.matmul(packed(ps[:, 2 + s % 2, 0:TOK]), w[:, s, c * P:(c + 1) * P], core.tok(c),
                                    start=(c == 0), stop=(c == DC - 1))
                ins.then_inc(head_mm, 1)

            def fold(n, s):
                pe.wait_ge(head_sb, Z + n + 1)
                pe.wait_ge(fold_sb, Z + n - 1)
                for c in range(DC):
                    ins = pe.matmul(ps[:, 4 + 2 * (s % 2) + c, 0:TOK], w[:, s, D + c * P:D + (c + 1) * P],
                                    q_head[:, s % 2, :], start=True, stop=True)
                ins.then_inc(fold_mm, 1)
            with pe.Fori(0, turns) as i:
                for s in range(WS):
                    head(i * WS + s, i, s)
                    if s:
                        fold(i * WS + s - 1, s - 1)
                fold(i * WS + WS - 1, WS - 1)

            def score_part(n, turn, x, k):
                b = x // RT
                if k == 0:
                    pe.wait_ge(exped, Z + n - 1)
                    pe.wait_ge(q_lo_ready, Z + n + 1)
                    if x % RT == 0:
                        pe.wait_ge(t_lo_ready, Z + 2 * (2 * turn + b + 1))
                products = [(q, t, c) for q, t in ((q_hi, t_hi), (q_hi, t_lo), (q_lo, t_hi)) for c in range(DC)]
                for m, (q, t, c) in enumerate(products):
                    ins = pe.matmul(ps[:, 3 * (x % 2) + k, 0:KN], q[:, x % 2, c, :],
                                    t[:, b, c, k * KN:(k + 1) * KN],
                                    start=(m == 0), stop=(m == len(products) - 1))
                if k == 2:
                    ins.then_inc(score_mm, 1)

            def turn_mixed(n, x):
                pe.wait_ge(mix_sb, Z + n + 1)
                for c in range(DC):
                    ins = pe.transpose(ps[:, 7, D + c * P:D + (c + 1) * P], mixed[:, x % 2, c * P:(c + 1) * P],
                                       core.ident[:, :])
                ins.then_inc(mix_turned, 1)

            def mix_part(n, i, x, u):
                if u == 0:
                    pe.wait_ge(mix_kept, Z + n)
                pe.wait_ge(p_lo_ready, Z + 3 * n + u + 1)
                if x % RT == 0:
                    pe.wait_ge(r_lo_ready, Z + 3 * (2 * i + x // RT) + u + 1)
                for t in range(4 * u, 4 * u + 4):
                    for m, (p, v) in enumerate(((p_hi, r_hi), (p_hi, r_lo), (p_lo, r_hi))):
                        ins = pe.matmul(ps[:, 7, 0:D], p[:, t, :], v[:, t, :],
                                        start=(t == 0 and m == 0), stop=(t == KT - 1 and m == 2))
                ins.then_inc(mix_mm, 1)

            def attention(i, last):
                for x in range(2 * RT):
                    n = i * 2 * RT + x
                    pe.wait_ge(exped, Z + n + 1)
                    for u in range(3):
                        if x > 0:
                            mix_part(n - 1, i, x - 1, u)
                            if u == 2:
                                turn_mixed(n - 1, x - 1)
                        pe.wait_ge(p_hi_ready, Z + 3 * n + u)
                        pe.wait_ge(p_lo_ready, Z + 3 * n + u)
                        for y in range(4):
                            t = 4 * u + y
                            ins = pe.transpose(ps[0:KP, 6, y * P:(y + 1) * P],
                                               prob[:, x % 2, t * KP:(t + 1) * KP], core.ident[:, :])
                        ins.then_inc(turned, 1)
                        if x < 2 * RT - 2:
                            score_part(n + 2, i, x + 2, u)
                        elif not last:
                            score_part(n + 2, i + 1, x + 2 - 2 * RT, u)
                for u in range(3):
                    mix_part(i * 2 * RT + 2 * RT - 1, i, 2 * RT - 1, u)
                turn_mixed(i * 2 * RT + 2 * RT - 1, 2 * RT - 1)

            for x in range(2):
                for k in range(3):
                    score_part(x, 0, x, k)
            with pe.Fori(0, PAIRS - 1) as i:
                attention(i, last=False)
            attention(PAIRS - 1, last=True)

            for a in range(2):
                pe.matmul(ps[:, a, :], zero[0:1, 0:P], zero[0:1, :], start=True, stop=True,
                          skip_group_check=True)
            pe.wait_ge(mix_kept, Z + B * RT)

            def value(n, i, s):
                pe.wait_ge(w_in[s], DMA * (turns + i + 1))
                pe.wait_ge(v_sb, Z + n - 1)
                for c in range(DC):
                    ins = pe.matmul(packed(ps[:, 2 + s % 2, 0:TOK]), w[:, s, c * P:(c + 1) * P],
                                    q_all[:, c, :, bass.ds(n * S, S)], start=(c == 0), stop=(c == DC - 1))
                ins.then_inc(v_mm, 1)

            def output(n, s):
                pe.wait_ge(v_sb, Z + n + 1)
                for t in range(PAIRS):
                    ins = pe.matmul(ps[:, t // 2, (t % 2) * D:(t % 2 + 1) * D],
                                    v_head[:, s % 2, t * P:(t + 1) * P], w[:, s, D:2 * D],
                                    start=False, stop=False, skip_group_check=True)
                ins.then_inc(out_mm, 1)
            with pe.Fori(0, turns) as i:
                for s in range(WS):
                    value(i * WS + s, i, s)
                    if s:
                        output(i * WS + s - 1, s - 1)
                output(i * WS + WS - 1, WS - 1)

        @block.scalar
        def _(act):
            for x in (head_sb, exped, q_hi_ready, t_hi_ready, r_hi_ready, p_hi_ready, mix_kept, v_sb):
                act.sem_inc(x, Z)

            def split_turned(b, s, c):
                act.wait_ge(raw_in, DMA * (2 * b + 1))
                act.wait_ge(score_mm, Z + RT * (b - 1))
                act.copy(t_hi[:, s, c, :], raw_t[:, c, :]).then_inc(t_hi_ready, 1)

            def split_rows(b, u):
                act.wait_ge(raw_in, DMA * (2 * b + 2))
                act.wait_ge(mix_mm, Z + 3 * (RT * b - 1) + u + 1)
                act.copy(r_hi[:, 4 * u:4 * u + 4, :], raw_r[:, 4 * u:4 * u + 4, :]).then_inc(r_hi_ready, 1)
            core.ln_scalar(act, k_ln)
            for c in range(DC):
                split_turned(0, 0, c)
            for u in range(3):
                split_rows(0, u)
            with act.Fori(0, turns) as i:
                for s in range(WS):
                    n = i * WS + s
                    act.wait_ge(head_mm, Z + n + 1)
                    act.wait_ge(fold_mm, Z + n - 1)
                    act.copy(q_head[:, s % 2, :], ps[:, 2 + s % 2, 0:TOK]).then_inc(head_sb, 1)

            def split_queries(n, x):
                act.wait_ge(q_staged, Z + n + 1)
                act.wait_ge(score_mm, Z + n - 1)
                act.copy(q_hi[:, x % 2, :, :], q_tile[:, x % 2, :, :]).then_inc(q_hi_ready, 1)

            def exp(n, x):
                act.wait_ge(maxed, Z + n + 1)
                act.wait_ge(turned, Z + 3 * (n - 1))
                act.activation(prob[:, x % 2, :].rearrange("p (k n) -> p k n", k=3),
                               ps[:, 3 * (x % 2):3 * (x % 2) + 3, 0:KN], ACT.Exp,
                               bias=neg_max[:, x % 2:x % 2 + 1],
                               accum_out=sums[:, x % 2:x % 2 + 1]).then_inc(exped, 1)

            def keep_mixed(i, x, n):
                act.wait_ge(mix_turned, Z + n + 1)
                act.copy(query_tile(i, x), ps[:, 7, D:2 * D].rearrange("p (c n) -> p c n", c=DC)) \
                    .then_inc(mix_kept, 1)

            def attention(i, last):
                for x in range(2 * RT):
                    n = i * 2 * RT + x
                    b, r = x // RT, x % RT
                    for u in range(3):
                        if u == 2 and x > 0:
                            keep_mixed(i, x - 1, n - 1)
                        act.wait_ge(turned, Z + 3 * n + u + 1)
                        act.wait_ge(mix_mm, Z + 3 * n + u - 2)
                        act.copy(p_hi[:, 4 * u:4 * u + 4, :].rearrange("p t n -> p (t n)"),
                                 ps[0:KP, 6, :]).then_inc(p_hi_ready, 1)
                        if u == 0 and not (last and x == 2 * RT - 1):
                            exp(n + 1, x + 1)
                        if u == 1 and not (last and x + 3 >= 2 * RT):
                            split_queries(n + 3, x + 3)
                        if r == 0 and x > 0:
                            split_rows(2 * i + b, u)
                    if r in (2, 3) and not (last and b == 1):
                        split_turned(2 * i + b + 1, 1 - b, r - 2)
                keep_mixed(i, 2 * RT - 1, i * 2 * RT + 2 * RT - 1)
                if not last:
                    for u in range(3):
                        split_rows(2 * i + 2, u)
            for x in range(2):
                split_queries(x, x)
            exp(0, 0)
            split_queries(2, 2)
            with act.Fori(0, PAIRS - 1) as i:
                attention(i, last=False)
            attention(PAIRS - 1, last=True)
            with act.Fori(0, turns) as i:
                for s in range(WS):
                    n = i * WS + s
                    act.wait_ge(v_mm, Z + n + 1)
                    act.wait_ge(out_mm, Z + n - 1)
                    act.copy(unpad(v_head[:, s % 2, :]), packed(ps[:, 2 + s % 2, 0:TOK])).then_inc(v_sb, 1)

        @block.vector
        def _(dve):
            link = InOrder(dve, core.dve_step, dve0)
            for x in (fold_sb, maxed, q_lo_ready, t_lo_ready, r_lo_ready, p_lo_ready, mix_sb):
                dve.sem_inc(x, Z)
            core.ln_vector(dve, link, k_ln)
            link(dve.memset(zero[:, :], 0.0))
            link(dve.memset(head_cols[:, :, :], 0.0))

            def split_turned(b, s, c):
                dve.wait_ge(t_hi_ready, Z + 2 * b + c + 1)
                dve.tensor_tensor(t_lo[:, s, c, :], raw_t[:, c, :], t_hi[:, s, c, :].bitcast(F32),
                                  ALU.subtract).then_inc(t_lo_ready, 1)

            def split_rows(b, u):
                dve.wait_ge(r_hi_ready, Z + 3 * b + u + 1)
                dve.tensor_tensor(r_lo[:, 4 * u:4 * u + 4, :], raw_r[:, 4 * u:4 * u + 4, :],
                                  r_hi[:, 4 * u:4 * u + 4, :].bitcast(F32), ALU.subtract).then_inc(r_lo_ready, 1)
            for c in range(DC):
                split_turned(0, 0, c)
            for u in range(3):
                split_rows(0, u)
            with dve.Fori(0, turns) as i:
                for s in range(WS):
                    n = i * WS + s
                    dve.wait_ge(fold_mm, Z + n + 1)
                    for c in range(DC):
                        ins = dve.tensor_scalar(q_all[:, c, :, bass.ds(n * S, S)],
                                                packed(ps[:, 4 + 2 * (s % 2) + c, 0:TOK]), scale, None, ALU.mult)
                    ins.then_inc(fold_sb, 1)

            def split_queries(n, x):
                dve.wait_ge(q_hi_ready, Z + n + 1)
                dve.tensor_tensor(q_lo[:, x % 2, :, :], q_tile[:, x % 2, :, :], q_hi[:, x % 2, :, :].bitcast(F32),
                                  ALU.subtract).then_inc(q_lo_ready, 1)

            def row_max(n, x):
                dve.wait_ge(score_mm, Z + n + 1)
                dve.wait_ge(exped, Z + n - 1)
                dve.tensor_reduce(neg_max[:, x % 2:x % 2 + 1], ps[:, 3 * (x % 2):3 * (x % 2) + 3, 0:KN],
                                  AXIS.XY, ALU.max, negate=True).then_inc(maxed, 1)

            def keep(n, x):
                dve.wait_ge(mix_mm, Z + 3 * n + 3)
                dve.tensor_scalar(mixed[:, x % 2, :], ps[:, 7, 0:D], inv[:, x % 2:x % 2 + 1], None,
                                  ALU.mult).then_inc(mix_sb, 1)

            def attention(i, last):
                for x in range(2 * RT):
                    n = i * 2 * RT + x
                    b, r = x // RT, x % RT
                    dve.wait_ge(exped, Z + n + 1)
                    link(dve.reciprocal(inv[:, x % 2:x % 2 + 1], sums[:, x % 2:x % 2 + 1]))
                    if not (last and x == 2 * RT - 1):
                        row_max(n + 1, x + 1)
                    for u in range(3):
                        if u == 2 and x > 0:
                            keep(n - 1, x - 1)
                        dve.wait_ge(p_hi_ready, Z + 3 * n + u + 1)
                        p4 = slice(4 * u, 4 * u + 4)
                        dve.tensor_tensor(p_lo[:, p4, :].rearrange("p t n -> p (t n)"), ps[0:KP, 6, :],
                                          p_hi[:, p4, :].rearrange("p t n -> p (t n)").bitcast(F32),
                                          ALU.subtract).then_inc(p_lo_ready, 1)
                        if u == 1 and not (last and x + 3 >= 2 * RT):
                            split_queries(n + 3, x + 3)
                        if r == 0 and x > 0:
                            split_rows(2 * i + b, u)
                    if r in (2, 3) and not (last and b == 1):
                        split_turned(2 * i + b + 1, 1 - b, r - 2)
                keep(i * 2 * RT + 2 * RT - 1, 2 * RT - 1)
                if not last:
                    for u in range(3):
                        split_rows(2 * i + 2, u)
            for x in range(2):
                split_queries(x, x)
            row_max(0, 0)
            split_queries(2, 2)
            first = link.n
            with dve.Fori(0, PAIRS - 1) as i:
                link.loop(i, first, 2 * RT)
                attention(i, last=False)
            link.end(first, 2 * RT, PAIRS - 1)
            attention(PAIRS - 1, last=True)
            dve.wait_ge(out_mm, Z + H)
            for a in range(2):
                rows = core.x_rows[:, 2 * a:2 * a + 2, :].rearrange("p i d -> p (i d)")
                link(dve.tensor_tensor(rows, rows, ps[:, a, :], ALU.add))
            core.dve_n = link.n


PACK = 4 * P + D + P
SLOTS = 4


def moe(core, tag, experts, top_k, tiles, shared_gate):
    nc, dram, ps = core.nc, core.dram, core.psum
    k_ln = core.new_norm()
    dve0 = core.dve_n
    ne = experts + 1
    nl = experts + int(shared_gate)
    ctx = ExitStack()
    with ctx:
        def sb(name, shape, dt=F32):
            return ctx.enter_context(nc.sbuf_tensor(tag + name, shape, dt))
        w_gate = sb("gate", [P, DC, nl])
        w = sb("w", [P, SLOTS, PACK])
        before = sb("before", [P, experts, experts])
        zero = sb("zero", [1, 512])
        gate_silu = sb("gate_silu", [P, 2, TOK])
        prod = sb("prod", [P, 2, TOK])
        hid = sb("hid", [P, 4, T])
        top = sb("top", [P, PAIRS])
        logit = sb("logit", [P, PAIRS, nl])
        prob = sb("prob", [P, PAIRS, experts])
        sig = sb("sig", [P, PAIRS])
        gt = sb("gt", [P, PAIRS, experts * experts])
        eq = sb("eq", [P, PAIRS, experts * experts])
        rank = sb("rank", [P, PAIRS, experts])
        total = sb("total", [P, PAIRS])
        combine = sb("combine", [P, PAIRS, ne])
        combine_t = sb("combine_t", [ne, T])
        sem = core.sem
        gate_in = sem(tag + "gate_in")
        w_in = [sem(f"{tag}w_in{s}") for s in range(SLOTS)]
        (gate_mm, maxed, exped, combined, comb_turned, comb_ready, up_mm, silued, product, scaled, owner_mm,
         down_mm, cleared) = (sem(tag + n) for n in (
            "gate_mm", "maxed", "exped", "combined", "comb_turned", "comb_ready", "up_mm", "silued",
            "product", "scaled", "owner_mm", "down_mm", "cleared"))
        turns = tiles // SLOTS
        block = ctx.enter_context(nc.Block())

        @block.sync
        def _(sp):
            sp.dma_start(w_gate[:, :, :], dram[tag + "gate"]).then_inc(gate_in, DMA)
            sp.dma_start(before[:, :, :], dram[tag + "before"]).then_inc(gate_in, DMA)
            for s in range(SLOTS):
                sp.dma_start(w[:, s, :], dram[tag + "pack"][s]).then_inc(w_in[s], DMA)
            with sp.Fori(1, turns) as i:
                for s in range(SLOTS):
                    sp.wait_ge(down_mm, (i - 1) * SLOTS + s + 1)
                    sp.dma_start(w[:, s, :], dram[tag + "pack"][i * SLOTS + s]).then_inc(w_in[s], DMA)

        @block.gpsimd
        def _(pool):
            core.ln_pool(pool, k_ln)

        @block.tensor
        def _(pe):
            core.ln_tensor(pe, k_ln)
            pe.wait_ge(core.ln_cols, core.cols_ready(k_ln))
            pe.wait_ge(gate_in, 2 * DMA)
            for t in range(PAIRS):
                for c in range(DC):
                    ins = pe.matmul(ps[:, 7, t * nl:(t + 1) * nl], core.xn_cols[:, c, t * P:(t + 1) * P],
                                    w_gate[:, c, :], start=(c == 0), stop=(c == DC - 1))
            ins.then_inc(gate_mm, 1)

            def up(n, s, first=False):
                pe.wait_ge(w_in[s], (n // SLOTS + 1) * DMA if isinstance(n, int) else n[1] * DMA + DMA)
                at = n if isinstance(n, int) else n[0]
                if not first:
                    pe.wait_ge(silued, at - 1)
                    pe.wait_ge(product, at - 1)
                for k in range(2):
                    for c in range(DC):
                        ins = pe.matmul(packed(ps[:, 2 + 2 * k + s % 2, 0:TOK]),
                                        w[:, s, (2 * k + c) * P:(2 * k + c + 1) * P], core.tok(c),
                                        start=(c == 0), stop=(c == DC - 1))
                ins.then_inc(up_mm, 1)

            def owner(n, s, first=False):
                if not first:
                    pe.wait_ge(scaled, n)
                pe.matmul(packed(ps[:, 6, 0:TOK]), w[0:ne, s, 4 * P + D:], unpad(combine_t[:, :]),
                          start=True, stop=True).then_inc(owner_mm, 1)

            def down(n, s):
                pe.wait_ge(scaled, n + 1)
                for t in range(PAIRS):
                    ins = pe.matmul(ps[:, t // 2, (t % 2) * D:(t % 2 + 1) * D], hid[:, s, t * P:(t + 1) * P],
                                    w[:, s, 4 * P:4 * P + D], start=False, stop=False, skip_group_check=True)
                ins.then_inc(down_mm, 1)

            up(0, 0, first=True)
            pe.wait_ge(cleared, 1)
            for a in range(2):
                pe.matmul(ps[:, a, :], zero[0:1, 0:P], zero[0:1, :], start=True, stop=True,
                          skip_group_check=True)
            pe.wait_ge(combined, 1)
            for t in range(PAIRS):
                ins = pe.transpose(ps[0:ne, 7, t * P:(t + 1) * P], combine[:, t, :], core.ident[:, :])
            ins.then_inc(comb_turned, 1)
            pe.wait_ge(comb_ready, 1)
            owner(0, 0, first=True)
            for n in range(1, SLOTS):
                up(n, n, first=(n < 2))
                down(n - 1, n - 1)
                owner(n, n)
            with pe.Fori(1, turns) as i:
                for s in range(SLOTS):
                    n = i * SLOTS + s
                    up((n, i), s)
                    down(n - 1, (s - 1) % SLOTS)
                    owner(n, s)
            down(tiles - 1, SLOTS - 1)

        @block.scalar
        def _(act):
            core.ln_scalar(act, k_ln)
            act.wait_ge(maxed, 1)
            act.activation(prob[:, :, :], prob[:, :, :], ACT.Exp).then_inc(exped, 1)
            if shared_gate:
                act.activation(sig[:, :], logit[:, :, experts], ACT.Sigmoid).then_inc(exped, 1)
            act.wait_ge(comb_turned, 1)
            act.copy(combine_t[:, :], ps[0:ne, 7, :]).then_inc(comb_ready, 1)

            def silu(n, s, first=False):
                act.wait_ge(up_mm, n + 1)
                if not first:
                    act.wait_ge(product, n - 1)
                act.activation(gate_silu[:, s % 2, :], ps[:, 2 + s % 2, 0:TOK], ACT.Silu).then_inc(silued, 1)
            for n in range(SLOTS):
                silu(n, n, first=(n < 2))
            with act.Fori(1, turns) as i:
                for s in range(SLOTS):
                    silu(i * SLOTS + s, s)

        @block.vector
        def _(dve):
            link = InOrder(dve, core.dve_step, dve0)
            dve.memset(zero[:, :], 0.0).then_inc(cleared, 1)
            link(dve.memset(hid[:, :, :], 0.0))
            core.ln_vector(dve, link, k_ln)
            dve.wait_ge(gate_mm, 1)
            link(dve.tensor_copy(logit[:, :, :].rearrange("p t e -> p (t e)"), ps[:, 7, 0:PAIRS * nl]))
            link(dve.tensor_reduce(top[:, :], logit[:, :, 0:experts], AXIS.X, ALU.max))
            dve.tensor_tensor(prob[:, :, :], logit[:, :, 0:experts],
                              top[:, :].unsqueeze(2).to_broadcast([P, PAIRS, experts]),
                              ALU.subtract).then_inc(maxed, 1)
            dve.wait_ge(exped, 1 + int(shared_gate))
            for t in range(PAIRS):
                mine = prob[:, t, :].unsqueeze(2).to_broadcast([P, experts, experts])
                other = prob[:, t, :].unsqueeze(1).to_broadcast([P, experts, experts])
                g3 = gt[:, t, :].rearrange("p (a b) -> p a b", b=experts)
                e3 = eq[:, t, :].rearrange("p (a b) -> p a b", b=experts)
                link(dve.tensor_tensor(g3, other, mine, ALU.is_gt))
                link(dve.tensor_tensor(e3, other, mine, ALU.is_equal))
                link(dve.tensor_tensor(e3, e3, before[:, :, :], ALU.mult))
                link(dve.tensor_tensor(g3, g3, e3, ALU.add))
                link(dve.tensor_reduce(rank[:, t, :], g3, AXIS.X, ALU.add))
            link(dve.tensor_scalar(rank[:, :, :], rank[:, :, :], float(top_k), None, ALU.is_lt))
            link(dve.tensor_tensor(prob[:, :, :], prob[:, :, :], rank[:, :, :], ALU.mult))
            link(dve.tensor_reduce(total[:, :], prob[:, :, :], AXIS.X, ALU.add))
            link(dve.reciprocal(total[:, :], total[:, :]))
            if shared_gate:
                link(dve.tensor_copy(combine[:, :, experts], sig[:, :]))
            else:
                link(dve.memset(combine[:, :, experts], 1.0))
            dve.tensor_tensor(combine[:, :, 0:experts], prob[:, :, :],
                              total[:, :].unsqueeze(2).to_broadcast([P, PAIRS, experts]),
                              ALU.mult).then_inc(combined, 1)

            def gated(n, s, first=False):
                dve.wait_ge(silued, n + 1)
                dve.tensor_tensor(prod[:, s % 2, :], gate_silu[:, s % 2, :], ps[:, 4 + s % 2, 0:TOK],
                                  ALU.mult).then_inc(product, 1)
                dve.wait_ge(product, n + 1)
                dve.wait_ge(owner_mm, n + 1)
                if not first:
                    dve.wait_ge(down_mm, n - SLOTS + 1)
                dve.tensor_tensor(unpad(hid[:, s, :]), packed(prod[:, s % 2, :]), packed(ps[:, 6, 0:TOK]),
                                  ALU.mult).then_inc(scaled, 1)
            for n in range(SLOTS):
                gated(n, n, first=True)
            with dve.Fori(1, turns) as i:
                for s in range(SLOTS):
                    gated(i * SLOTS + s, s)
            dve.wait_ge(down_mm, tiles)
            for a in range(2):
                rows = core.x_rows[:, 2 * a:2 * a + 2, :].rearrange("p i d -> p (i d)")
                link(dve.tensor_tensor(rows, rows, ps[:, a, :], ALU.add))
            core.dve_n = link.n


E1, K1, I1, SI1 = 16, 4, 176, 704
TILES1 = -(-(E1 * I1 + SI1) // P)
E3, K3, I3 = 8, 2, 512
TILES3 = (E3 + 1) * I3 // P


def moe_1(core):
    moe(core, "m1_", E1, K1, TILES1, shared_gate=True)


def moe_3(core):
    moe(core, "m3_", E3, K3, TILES3, shared_gate=False)


def chunks(w, p=P):
    return w.reshape(w.shape[0] // p, p, w.shape[1]).transpose(1, 0, 2)


def rope_tables(length):
    half = R // 2
    freq = (1.0 / 10000.0 ** (np.arange(half, dtype=np.float32) / np.float32(half))).astype(np.float32)
    ang = np.arange(length, dtype=np.float32)[:, None] * freq
    cos, sin = np.cos(ang), np.sin(ang)
    return (np.concatenate([cos, cos], 1).astype(np.float32),
            np.concatenate([-sin, sin], 1).astype(np.float32))


def layouts(a):
    out = {"x": a["x"], "c_ident": np.eye(P, dtype=np.float32)}
    seg = a["itok_BxS_0_1023"].reshape(B, GROUPS, GQ)
    out["seg_k"] = np.repeat(seg.transpose(2, 0, 1).reshape(GQ, B * GROUPS), WIN, axis=0)
    out["seg_r"] = np.tile(seg.transpose(2, 0, 1).reshape(GQ, B * GROUPS), (HH, 1))
    win = np.arange(WIN, dtype=np.float32) - (WIN - 1)
    out["c_win_k"] = np.tile(win, GQ)[:, None]
    out["c_seq_row"] = np.tile(np.repeat(np.arange(B, dtype=np.float32) * LK, GROUPS), (GR, 1))
    out["c_win_r"] = np.tile(win, (ROW0, 1))
    own = np.tile(np.arange(GQ), HH)[:, None] == np.repeat(np.arange(GQ), WIN)[None, :]
    out["c_diag"] = np.where(own, 0.0, NEG).astype(np.float32)
    cos, sin = rope_tables(LK)
    ctx = a["ctx_2048"]
    table = np.broadcast_to(np.concatenate([sin, cos], 1)[None], (B, LK, 2 * R))
    out["ctx_rope"] = np.concatenate([ctx, table], 2).reshape(B * LK, D + 2 * R)
    out["c_rope_q"] = np.tile(np.stack([cos[:S].T, sin[:S].T], 1), (2, 1, 1))

    def swap(w):
        w = w.reshape(w.shape[0], -1, 2, R // 2)
        return w[:, :, ::-1, :].reshape(w.shape[0], -1)
    out["w_kvc"] = chunks(a["L0_xattn_W_kvc"])
    out["w_kvc_t"] = a["L0_xattn_W_kvc"].T
    out["w_kr2"] = np.concatenate([a["L0_xattn_W_kr"], swap(a["L0_xattn_W_kr"])], 1)
    out["w_dq"] = chunks(a["L0_xattn_W_dq"])
    out["w_uq_t"] = a["L0_xattn_W_uq"].reshape(QC, H, HD).transpose(2, 1, 0)
    out["w_uk_t"] = a["L0_xattn_W_uk"].reshape(KVC, H, HD).transpose(2, 1, 0)
    out["w_uv_t"] = a["L0_xattn_W_uv"].reshape(KVC, H, HD).transpose(2, 1, 0)
    out["w_qr"] = np.stack([a["L0_xattn_W_qr"], swap(a["L0_xattn_W_qr"])], 1)
    out["w_o"] = a["L0_xattn_W_o"].reshape(H, HD, D).transpose(1, 0, 2)
    out["f_w1"] = chunks(a["L0_ffn_W1"].T)
    out["f_w2"] = chunks(a["L0_ffn_W2"].T)
    out["ctx_r"] = ctx.reshape(B, KP, KT, D)
    out["ctx_t"] = ctx.reshape(B, KP, KT, DC, P).transpose(0, 4, 3, 2, 1).reshape(B, P, DC, LK)
    out["c_mask"] = a["mask_BxS2_bk0"].reshape(B, KP, KT).transpose(0, 2, 1).reshape(B, LK).view(np.int32)
    out["c_mask2"] = a["mask_BxS2_ff1"].reshape(B, KP, KT).transpose(1, 0, 2)
    out["c_w_k"] = chunks(a["L2_xattn_Wk"].T)
    out["c_w_v"] = chunks(a["L2_xattn_Wv"].T)
    out["c_b_k"] = a["L2_xattn_bk"].reshape(2, P).T

    def block_diagonal(w):
        out = np.zeros((8, HD2, 8, FD2), np.float32)
        out[np.arange(8), :, np.arange(8), :] = w.T
        return out.reshape(P, FG)
    out["c_w_kf"] = block_diagonal(a["L2_xattn_Wkf"])
    out["l_w_q"] = chunks(a["L2_xattn_Wq"].T)
    out["l_w_o"] = chunks(a["L2_xattn_Wo"].T)
    out["l_w_qf"] = block_diagonal(a["L2_xattn_Wqf"])
    out["l_b_q"] = a["L2_xattn_bq"].reshape(2, P).T
    out["l_b_v"] = a["L2_xattn_bv"]
    out["l_b_o"] = a["L2_xattn_bo"]
    order = np.pad(a["L2_ffn_down_reorder_index"], (0, FT2 * P - FF2))
    out["q_order"] = order.reshape(FT2, P).T
    out["q_w_gate"] = a["L2_ffn_w_gate"]
    out["q_w_up"] = a["L2_ffn_w_up"]
    out["q_w_down"] = a["L2_ffn_w_down"].reshape(DC, P, FF2).transpose(1, 0, 2)
    wq = a["L3_xattn_Wq"].reshape(DC, P, H, HD).transpose(2, 1, 0, 3).reshape(H, P, D)
    wk = a["L3_xattn_Wk"].reshape(D, H, HD).transpose(1, 2, 0)
    wv = a["L3_xattn_Wv"].reshape(DC, P, H, HD).transpose(2, 1, 0, 3).reshape(H, P, D)
    wo = a["L3_xattn_Wo"].reshape(H, HD, D)
    out["a_w"] = np.concatenate([np.concatenate([wq, wk], 2), np.concatenate([wv, wo], 2)])

    def pack(gate, up, down, owner, tiles, experts):
        pad = tiles * P - len(gate)
        gate, up, down = (np.pad(w, ((0, pad), (0, 0))) for w in (gate, up, down))
        one = np.zeros((P, tiles * P), np.float32)
        one[owner, np.arange(len(owner))] = 1.0
        up_in = np.stack([gate, up]).reshape(2, tiles, P, DC, P).transpose(1, 4, 0, 3, 2)
        return np.concatenate([up_in.reshape(tiles, P, 4 * P), down.reshape(tiles, P, D),
                               one.reshape(P, tiles, P).transpose(1, 0, 2)], 2)

    def before(n):
        return np.tile((np.arange(n)[None, :] < np.arange(n)[:, None]).astype(np.float32), (P, 1, 1))
    gu, dn = a["L1_ffn_expert_gate_up"], a["L1_ffn_expert_down"]
    sgu, sdn = a["L1_ffn_shared_gate_up"], a["L1_ffn_shared_down"]
    out["m1_pack"] = pack(np.concatenate([gu[:, :I1].reshape(-1, D), sgu[:SI1]]),
                          np.concatenate([gu[:, I1:].reshape(-1, D), sgu[SI1:]]),
                          np.concatenate([dn.transpose(0, 2, 1).reshape(-1, D), sdn.T]),
                          np.concatenate([np.repeat(np.arange(E1), I1), np.full(SI1, E1)]), TILES1, E1)
    out["m1_gate"] = chunks(np.concatenate([a["L1_ffn_gate_w"], a["L1_ffn_shared_gate_vec"]]).T)
    out["m1_before"] = before(E1)
    gu, dn = a["L3_ffn_w_gate_up"].transpose(0, 2, 1), a["L3_ffn_w_down"]
    sgu, sdn = a["L3_ffn_shared_gate_up"].T, a["L3_ffn_shared_down"]
    out["m3_pack"] = pack(np.concatenate([gu[:, :I3].reshape(-1, D), sgu[:I3]]),
                          np.concatenate([gu[:, I3:].reshape(-1, D), sgu[I3:]]),
                          np.concatenate([dn.reshape(-1, D), sdn]),
                          np.repeat(np.arange(E3 + 1), I3), TILES3, E3)
    out["m3_gate"] = chunks(a["L3_ffn_gate_w"])
    out["m3_before"] = before(E3)
    return {k: np.ascontiguousarray(v) for k, v in out.items()}


def program(nc, dram):
    with ExitStack() as ctx:
        core = Core(nc, ctx, dram)
        setup(core)
        with ExitStack() as sums:
            core.open_kv_sums(sums)
            for stage in STAGES_A:
                stage(core)
                if stage is moe_1:
                    core.retire_sems()
        for stage in STAGES_B:
            stage(core)
        store(core)


STAGES_A = [window_attention, lookup_ffn, memory_attention_and_features, moe_1, linear_attention]
STAGES_B = [quantised_ffn, full_attention, moe_3]


def kernel(**inputs):
    import numpy as _np
    import concourse.bacc as _bacc
    from concourse import mybir as _mybir
    from concourse.bass_utils import run_bass_kernel_spmd as _run

    nc = _bacc.Bacc("TRN2", target_bir_lowering=False, num_devices=1)
    arrays, dram = {}, {}
    for name, a in layouts({k: _np.asarray(v) for k, v in inputs.items()}).items():
        arrays[f"in_{name}"] = a
        dram[name] = nc.dram_tensor(f"in_{name}", a.shape, _mybir.dt.from_np(a.dtype),
                                    kind="ExternalInput").ap()
    dram["out"] = nc.dram_tensor("out_0", (B, S, D), _mybir.dt.float32, kind="ExternalOutput").ap()
    program(nc, dram)
    r = _run(nc, [arrays], core_ids=[0])
    return r.results[0]["out_0"]
```

```python
from contextlib import ExitStack

import numpy as np

import concourse.bass as bass
from concourse import mybir

F32 = mybir.dt.float32
BF16 = mybir.dt.bfloat16
I32 = mybir.dt.int32
U32 = mybir.dt.uint32
U8 = mybir.dt.uint8
ACT = mybir.ActivationFunctionType
ALU = mybir.AluOpType
AXIS = mybir.AxisListType
REDUCE = bass.bass_isa.ReduceOp

P = 128
B, S, D = 8, 56, 256
SP = 64
PAIRS = B // 2
T = B * SP
TOK = B * S
DC = D // P
LK = 1500
KT, KP = 12, 125
KN = 500
EPS = 1e-5
NEG = -1e30
DMA = 16


class InOrder:

    def __init__(self, eng, sem, n=0):
        self.eng, self.sem, self.n, self.base = eng, sem, n, 0

    def __call__(self, ins):
        ins.then_inc(self.sem, 1)
        self.n += 1
        self.eng.wait_ge(self.sem, self.base + self.n)

    def loop(self, i, first, per_turn):
        self.base, self.n = first + i * per_turn, 0

    def end(self, first, per_turn, turns):
        assert self.n == per_turn, (self.n, per_turn)
        self.base, self.n = 0, first + per_turn * turns


class Core:

    def __init__(self, nc, ctx, dram):
        self.nc, self.dram = nc, dram

        def sb(name, shape, dt=F32):
            return ctx.enter_context(nc.sbuf_tensor(name, shape, dt))

        self.x_rows = sb("x_rows", [P, PAIRS, D])
        self.xn_rows = sb("xn_rows", [P, PAIRS, D])
        self.xn_cols = sb("xn_cols", [P, DC, T])
        self.ident = sb("ident", [P, P])
        self.bn = sb("bn", [P, PAIRS, 6])
        self.mean_var = sb("mean_var", [P, PAIRS, 2])
        self.var_eps = sb("var_eps", [P, PAIRS])
        self.rstd = sb("rstd", [P, PAIRS])
        self.minus_half = sb("minus_half", [P, PAIRS])
        self.psum = ctx.enter_context(nc.psum_tensor("psum", [P, 8, 512], F32))

        self.stage_sems = []
        self.const_ready = self.sem("const_ready")
        self.dve_step = self.sem("dve_step")
        self.act_step = self.sem("act_step")
        self.pool_step = self.sem("pool_step")
        self.ln_stats = self.sem("ln_stats")
        self.ln_rstd = self.sem("ln_rstd")
        self.ln_rows = self.sem("ln_rows")
        self.ln_turned = self.sem("ln_turned")
        self.ln_cols = self.sem("ln_cols")
        self.keep_sems()
        self.norms = 0
        self.turn_of = {}
        self.dve_n = self.act_n = self.pool_n = 0

    def sem(self, name):
        self.stage_sems.append(self.nc.alloc_semaphore(name=name))
        return self.stage_sems[-1]

    def keep_sems(self):
        self.stage_sems = []

    def retire_sems(self):
        self.nc.clear_and_free_semaphores(self.stage_sems)
        self.nc.all_engine_barrier()
        self.stage_sems = []

    def open_kv_sums(self, ctx):
        self.kv_sums = ctx.enter_context(self.nc.sbuf_tensor("kv_sums", [P, B, 8, 34], F32))

    def new_norm(self, turned=True):
        k = self.norms
        self.norms += 1
        if turned:
            self.turn_of[k] = len(self.turn_of)
        return k

    def cols_ready(self, k):
        return DC * (self.turn_of[k] + 1)

    def ln_vector(self, dve, link, k):
        for i in range(PAIRS):
            ins = dve.bn_stats(self.bn[:, i, :], self.x_rows[:, i, :])
            link(ins)
        for i in range(PAIRS):
            ins = dve.bn_aggr(self.mean_var[:, i, :], self.bn[:, i, :])
            link(ins)
        dve.tensor_scalar(self.var_eps[:, :], self.mean_var[:, :, 1], EPS, None,
                          ALU.add).then_inc(self.ln_stats, 1)
        dve.wait_ge(self.ln_rstd, k + 1)
        for i in range(PAIRS):
            dve.tensor_scalar(self.xn_rows[:, i, :], self.x_rows[:, i, :], self.mean_var[:, i, 0:1],
                              self.rstd[:, i:i + 1], ALU.subtract, ALU.mult).then_inc(self.ln_rows, 1)

    def ln_pool(self, pool, k):
        pool.wait_ge(self.ln_stats, k + 1)
        pool.tensor_tensor(self.rstd[:, :], self.var_eps[:, :], self.minus_half[:, :],
                           ALU.pow).then_inc(self.ln_rstd, 1)

    def ln_tensor(self, pe, k):
        for i in range(PAIRS):
            pe.wait_ge(self.ln_rows, PAIRS * k + i + 1)
            for c in range(DC):
                ins = pe.transpose(self.psum[:, c, i * P:(i + 1) * P],
                                   self.xn_rows[:, i, c * P:(c + 1) * P], self.ident[:, :])
        ins.then_inc(self.ln_turned, 1)

    def ln_scalar(self, act, k):
        act.wait_ge(self.ln_turned, self.turn_of[k] + 1)
        for c in range(DC):
            act.copy(self.xn_cols[:, c, :], self.psum[:, c, :]).then_inc(self.ln_cols, 1)

    def tok(self, c):
        return self.xn_cols[:, c, :].rearrange("p (b s) -> p b s", b=B)[:, :, 0:S]


def unpad(cols):
    return cols.rearrange("p (b s) -> p b s", b=B)[:, :, 0:S]


def packed(cols):
    return cols.rearrange("p (b s) -> p b s", b=B)


def setup(core):
    nc, dram = core.nc, core.dram
    x_loaded, zeroed = core.sem("x_loaded"), core.sem("zeroed")
    core.x_loaded = x_loaded
    with nc.Block() as block:
        @block.vector
        def _(dve):
            dve.memset(core.x_rows[:, :, :], 0.0).then_inc(zeroed, 1)
            dve.memset(core.minus_half[:, :], -0.5).then_inc(zeroed, 1)

        @block.sync
        def _(sp):
            sp.dma_start(core.ident[:, :], dram["c_ident"]).then_inc(core.const_ready, DMA)
            sp.wait_ge(zeroed, 1)
            for b in range(B):
                r = (b % 2) * SP
                sp.dma_start(core.x_rows[r:r + S, b // 2, :], dram["x"][b]).then_inc(x_loaded, DMA)
            sp.wait_ge(x_loaded, DMA * B)
            sp.wait_ge(core.const_ready, DMA)


def store(core):
    dram = core.dram
    stored = core.sem("stored")
    with core.nc.Block() as block:
        @block.sync
        def _(sp):
            for b in range(B):
                r = (b % 2) * SP
                sp.dma_start(dram["out"][b], core.x_rows[r:r + S, b // 2, :]).then_inc(stored, DMA)
            sp.wait_ge(stored, DMA * B)


H, HD = 16, 128
KVC, QC, R = 64, 96, 64
WIN = 9
GQ = 14
GROUPS = S // GQ
GR = GQ * WIN
HH = H // 2
ROW0 = GQ * HH


def window_attention(core):
    nc, dram, ps = core.nc, core.dram, core.psum
    k_ln = core.new_norm()
    dve0, act0 = core.dve_n, core.act_n
    scale = 1.0 / float(np.sqrt(np.float32(HD + R)))
    ctx = ExitStack()
    with ctx:
        def sb(name, shape, dt=F32):
            return ctx.enter_context(nc.sbuf_tensor(name, shape, dt))
        w_dq = sb("w_dq", [P, DC, QC])
        w_kvc_t = sb("w_kvc_t", [KVC, D])
        w_kr2 = sb("w_kr2", [KVC, 2 * R])
        w_key = sb("w_key", [P, DC, P])
        w_key_sw = sb("w_key_sw", [P, DC, R])
        w_uq_t = sb("w_uq_t", [P, H, QC])
        w_uk_t = sb("w_uk_t", [P, H, KVC])
        w_qr = sb("w_qr", [QC, 2, H * R])
        w_abs = sb("w_abs", [QC, H * KVC])
        w_uv_t = sb("w_uv_t", [P, H, KVC])
        w_o = sb("w_o", [P, H, D])
        w_vo = sb("w_vo", [P, HH, D])
        q_lat = sb("q_lat", [QC, T])
        rope_q = sb("rope_q", [P, 2, S])
        rope_a = sb("rope_a", [P, TOK])
        rope_b = sb("rope_b", [P, TOK])
        q_cat = sb("q_cat", [P, B * GROUPS, H, GQ])
        q_now = sb("q_now", [P, 2, GROUPS, H, GQ])
        seg_k = sb("seg_k", [GR, B * GROUPS], I32)
        seg_r = sb("seg_r", [ROW0, B * GROUPS], I32)
        win_k = sb("win_k", [GR, 1])
        seq_row = sb("seq_row", [GR, B * GROUPS])
        win_r = sb("win_r", [ROW0, WIN])
        diag = sb("diag", [ROW0, GR])
        row_f = sb("row_f", [GR, B * GROUPS])
        row_c = sb("row_c", [GR, B * GROUPS])
        rows_at = sb("rows_at", [GR, B * GROUPS], I32)
        kid = sb("kid", [ROW0, B * GROUPS, WIN])
        kid_c = sb("kid_c", [ROW0, B * GROUPS, WIN])
        outside = sb("outside", [ROW0, B * GROUPS, WIN])
        mask = sb("mask", [ROW0, B * GROUPS, GR])
        got = sb("got", [GR, 2, GROUPS, 3 * P])
        got_t = sb("got_t", [P, 2, 3, GROUPS * GR])
        key_sin = sb("key_sin", [P, GROUPS * GR])
        keys = sb("keys", [P, 2, GROUPS * GR])
        vals = sb("vals", [GR, 2, GROUPS, KVC])
        s_sb = sb("s_sb", [ROW0, 2, 2, GR])
        neg_max = sb("neg_max", [ROW0, 2, 2])
        sums = sb("sums", [ROW0, 2, 2])
        inv = sb("inv", [ROW0, 2, 2])
        prob = sb("prob", [ROW0, 2, 2, GR])
        prob_t = sb("prob_t", [GR, 2, 2, ROW0])
        lat = sb("lat", [P, HH, T])

        sem = core.sem
        idx_in = sem("w_idx_in")
        w_in = sem("w_weights_in")
        rows_known = sem("w_rows_known")
        got_in = [sem("w_got_in0"), sem("w_got_in1")]
        got_turned = sem("w_got_turned")
        got_t_ready = sem("w_got_t_ready")
        key_mm = sem("w_key_mm")
        key_latent = sem("w_key_latent")
        key_ready = sem("w_key_ready")
        val_mm = sem("w_val_mm")
        val_ready = sem("w_val_ready")
        comp_mm = sem("w_comp_mm")
        comp_ready = sem("w_comp_ready")
        q_mm = sem("w_q_mm")
        q_rot = sem("w_q_rot")
        q_abs = sem("w_q_abs")
        q_staged = sem("w_q_staged")
        score_mm = sem("w_score_mm")
        score_sb = sem("w_score_sb")
        maxed = sem("w_maxed")
        exped = sem("w_exped")
        normed = sem("w_normed")
        prob_turned = sem("w_prob_turned")
        prob_t_ready = sem("w_prob_t_ready")
        lat_mm = sem("w_lat_mm")
        lat_ready = sem("w_lat_ready")
        out_mm = sem("w_out_mm")

        gt = GROUPS * GR
        block = ctx.enter_context(nc.Block())

        @block.sync
        def _(sp):
            for dst, src in ((seg_k, "seg_k"), (win_k, "c_win_k"), (seq_row, "c_seq_row"),
                             (seg_r, "seg_r"), (win_r, "c_win_r"), (diag, "c_diag")):
                sp.dma_start(dst[:, :], dram[src]).then_inc(idx_in, DMA)
            sp.dma_start(w_kvc_t[:, :], dram["w_kvc_t"]).then_inc(w_in, DMA)
            sp.dma_start(w_kr2[:, :], dram["w_kr2"]).then_inc(w_in, DMA)
            sp.dma_start(w_key[:, :, 0:KVC], dram["w_kvc"]).then_inc(w_in, DMA)
            for dst, src in ((w_dq, "w_dq"), (w_uq_t, "w_uq_t"), (w_uk_t, "w_uk_t"), (w_qr, "w_qr"),
                             (w_uv_t, "w_uv_t"), (w_o, "w_o"), (rope_q, "c_rope_q")):
                sp.dma_start(dst[:, :, :], dram[src]).then_inc(w_in, DMA)
        n_w = 10

        @block.gpsimd
        def _(pool):
            core.ln_pool(pool, k_ln)
            pool.wait_ge(rows_known, 1)

            for b in range(B):
                if b >= 2:
                    pool.wait_ge(got_turned, b - 1)
                for g in range(GROUPS):
                    n = b * GROUPS + g
                    pool.indirect_dma_start(
                        got[:, b % 2, g, :], None, dram["ctx_rope"],
                        bass.IndirectOffsetOnAxis(ap=rows_at[:, n:n + 1], axis=0),
                    ).then_inc(got_in[b % 2], DMA)
                if b == 0:
                    pool.wait_ge(q_rot, 2 * HH)
                    pool.wait_ge(q_abs, 1 + 2 * HH)
                if b >= 2:
                    pool.wait_ge(score_mm, GROUPS * (b - 1))
                pool.tensor_copy(q_now[:, b % 2, :, :, :], q_cat[:, b * GROUPS:(b + 1) * GROUPS, :, :]) \
                    .then_inc(q_staged, 1)

        @block.tensor
        def _(pe):
            pe.wait_ge(w_in, DMA * n_w)
            for c in range(DC):
                ins = pe.matmul(ps[:, 2, c * P:(c + 1) * P], w_kvc_t[:, c * P:(c + 1) * P], w_kr2[:, :],
                                start=True, stop=True)
            ins.then_inc(comp_mm, 1)
            for h in range(H):
                ins = pe.matmul(ps[0:QC, 3 + h // 8, (h % 8) * KVC:(h % 8 + 1) * KVC],
                                w_uq_t[:, h, :], w_uk_t[:, h, :], start=True, stop=True)
            ins.then_inc(comp_mm, 1)
            for j in range(HH):
                if j == 4:
                    pe.wait_ge(comp_ready, 4)
                for k in range(2):
                    ins = pe.matmul(ps[k * KVC:(k + 1) * KVC, 5 + j // 2 % 2, (j % 2) * D:(j % 2 + 1) * D],
                                    w_uv_t[:, j + k * HH, :], w_o[:, j + k * HH, :], start=True, stop=True)
                if j % 4 == 3:
                    ins.then_inc(comp_mm, 1)
            core.ln_tensor(pe, k_ln)
            pe.wait_ge(core.ln_cols, core.cols_ready(k_ln))
            for c in range(DC):
                ins = pe.matmul(ps[0:QC, 7, :], w_dq[:, c, :], core.xn_cols[:, c, :],
                                start=(c == 0), stop=(c == DC - 1))
            ins.then_inc(q_mm, 1)
            pe.wait_ge(q_abs, 1)
            pe.wait_ge(comp_ready, 3)
            lq = unpad(q_lat[:, :])
            for j in range(HH):
                if j >= 2:
                    pe.wait_ge(q_rot, 2 * (j - 1))
                    pe.wait_ge(q_abs, 1 + 2 * (j - 1))
                bank = 3 * (j % 2)
                pe.matmul(packed(ps[:, bank, 0:TOK]), w_abs[:, j * P:(j + 1) * P], lq, start=True, stop=True)
                for k in range(2):
                    ins = pe.matmul(packed(ps[:, bank + 1 + k, 0:TOK]), w_qr[:, k, j * P:(j + 1) * P], lq,
                                    start=True, stop=True)
                ins.then_inc(q_mm, 1)

            def keys_of(b):
                s = b % 2
                pe.wait_ge(got_in[s], DMA * GROUPS * (b // 2 + 1))
                if b == 0:
                    pe.wait_ge(q_rot, 2 * HH)
                    pe.wait_ge(q_abs, 1 + 2 * HH)
                else:
                    pe.wait_ge(got_t_ready, 3 * b)
                for g in range(GROUPS):
                    for c in range(3):
                        ins = pe.transpose(ps[:, c, g * GR:(g + 1) * GR], got[:, s, g, c * P:(c + 1) * P],
                                           core.ident[0:GR, 0:GR])
                ins.then_inc(got_turned, 1)
                pe.wait_ge(got_t_ready, 3 * (b + 1))
                if b >= 1:
                    pe.wait_ge(key_ready, b)
                    pe.wait_ge(val_ready, b)
                for c in range(DC):
                    pe.matmul(ps[:, 3, 0:gt], w_key[:, c, :], got_t[:, s, c, :],
                              start=(c == 0), stop=(c == DC - 1))
                for c in range(DC):
                    ins = pe.matmul(ps[0:R, 4, 0:gt], w_key_sw[:, c, :], got_t[:, s, c, :],
                                    start=(c == 0), stop=(c == DC - 1))
                ins.then_inc(key_mm, 1)
                pe.wait_ge(key_ready, b + 1)
                for g in range(GROUPS):
                    ins = pe.transpose(ps[0:GR, 4, g * KVC:(g + 1) * KVC],
                                       keys[0:KVC, s, g * GR:(g + 1) * GR], core.ident[0:KVC, 0:KVC])
                ins.then_inc(val_mm, 1)

            def scores_of(n):
                b, g = n // GROUPS, n % GROUPS
                if g == 0:
                    pe.wait_ge(q_staged, b + 1)
                if n >= 1:
                    pe.wait_ge(score_sb, n)
                for k in range(2):
                    ins = pe.matmul(ps[0:ROW0, 5, k * GR:(k + 1) * GR],
                                    q_now[:, b % 2, g, k * HH:(k + 1) * HH, :].rearrange("p h q -> p (h q)"),
                                    keys[:, b % 2, g * GR:(g + 1) * GR], start=True, stop=True)
                ins.then_inc(score_mm, 1)

            def attend(n):
                b, g = n // GROUPS, n % GROUPS
                pe.wait_ge(normed, n + 1)
                if n >= 1:
                    pe.wait_ge(prob_t_ready, n)
                for k in range(2):
                    ins = pe.transpose(ps[0:GR, 6, k * ROW0:(k + 1) * ROW0], prob[:, n % 2, k, :],
                                       core.ident[0:ROW0, 0:ROW0])
                ins.then_inc(prob_turned, 1)

            def mix(n):
                b, g = n // GROUPS, n % GROUPS
                pe.wait_ge(prob_t_ready, n + 1)
                pe.wait_ge(val_ready, b + 1)
                if n >= 1:
                    pe.wait_ge(lat_ready, n)
                for k in range(2):
                    ins = pe.matmul(ps[k * KVC:(k + 1) * KVC, 7, 0:ROW0], vals[:, b % 2, g, :],
                                    prob_t[:, n % 2, k, :], start=True, stop=True)
                ins.then_inc(lat_mm, 1)

            n_groups = B * GROUPS
            for n in range(n_groups + 2):
                if n < n_groups:
                    if n % GROUPS == 0:
                        keys_of(n // GROUPS)
                    scores_of(n)
                if 1 <= n <= n_groups:
                    attend(n - 1)
                if n >= 2:
                    mix(n - 2)
            pe.wait_ge(lat_ready, n_groups)
            pe.wait_ge(comp_ready, 5)
            for i in range(PAIRS):
                for j in range(HH):
                    ins = pe.matmul(ps[:, i // 2, (i % 2) * D:(i % 2 + 1) * D], lat[:, j, i * P:(i + 1) * P],
                                    w_vo[:, j, :], start=(j == 0), stop=(j == HH - 1))
            ins.then_inc(out_mm, 1)

        @block.scalar
        def _(act):
            act.wait_ge(comp_mm, 1)
            act.copy(w_key[:, :, KVC:P], ps[:, 2, 0:2 * P].rearrange("p (c k) -> p c k", c=2)[:, :, 0:R]) \
                .then_inc(comp_ready, 1)
            act.copy(w_key_sw[:, :, :], ps[:, 2, 0:2 * P].rearrange("p (c k) -> p c k", c=2)[:, :, R:P]) \
                .then_inc(comp_ready, 1)
            act.wait_ge(comp_mm, 2)
            act.copy(w_abs[:, :], ps[0:QC, 3:5, :].rearrange("p a n -> p (a n)")).then_inc(comp_ready, 1)
            for a in range(2):
                act.wait_ge(comp_mm, 3 + a)
                act.copy(w_vo[:, 4 * a:4 * a + 4, :].rearrange("p j n -> p (j n)"),
                         ps[:, 5:7, :].rearrange("p a n -> p (a n)")).then_inc(comp_ready, 1)
            core.ln_scalar(act, k_ln)
            act.wait_ge(q_mm, 1)
            act.copy(q_lat[:, :], ps[0:QC, 7, :]).then_inc(q_abs, 1)
            for j in range(HH):
                act.wait_ge(q_mm, 2 + j)
                for k in range(2):
                    act.copy(q_cat[0:KVC, :, 2 * j + k, :],
                             ps[k * KVC:(k + 1) * KVC, 3 * (j % 2), 0:TOK]
                             .rearrange("p (n q) -> p n q", q=GQ)).then_inc(q_abs, 1)

            def keys_of(b):
                s = b % 2
                act.wait_ge(got_turned, b + 1)
                if b >= 2:
                    act.wait_ge(key_ready, b - 1)
                for c in range(2):
                    act.copy(got_t[:, s, c, :], ps[:, c, 0:gt]).then_inc(got_t_ready, 1)
                act.wait_ge(key_mm, b + 1)
                act.copy(keys[0:KVC, s, :], ps[0:KVC, 3, 0:gt]).then_inc(key_latent, 1)
                act.wait_ge(val_mm, b + 1)
                act.copy(vals[:, s, :, :].rearrange("p g k -> p (g k)"), ps[0:GR, 4, 0:GROUPS * KVC]) \
                    .then_inc(val_ready, 1)

            def exps(n):
                act.wait_ge(maxed, n + 1)
                if n >= 2:
                    act.wait_ge(prob_turned, n - 1)
                for k in range(2):
                    act.activation(prob[:, n % 2, k, :], s_sb[:, n % 2, k, :], ACT.Exp,
                                   bias=neg_max[:, n % 2, k:k + 1],
                                   accum_out=sums[:, n % 2, k:k + 1]).then_inc(exped, 1)

            def turned(n):
                act.wait_ge(prob_turned, n + 1)
                if n >= 2:
                    act.wait_ge(lat_mm, n - 1)
                act.copy(prob_t[:, n % 2, :, :].rearrange("p k r -> p (k r)"),
                         ps[0:GR, 6, 0:2 * ROW0]).then_inc(prob_t_ready, 1)

            n_groups = B * GROUPS
            for n in range(n_groups + 1):
                if n < n_groups:
                    if n % GROUPS == 0:
                        keys_of(n // GROUPS)
                    exps(n)
                if n >= 1:
                    turned(n - 1)

        @block.vector
        def _(dve):
            link = InOrder(dve, core.dve_step, dve0)
            link(dve.memset(lat[:, :, :], 0.0))
            dve.wait_ge(idx_in, DMA * 6)
            link(dve.tensor_scalar(row_f[:, :], seg_k[:, :], win_k[:, 0:1], 0.0, ALU.add, ALU.max))
            link(dve.tensor_scalar(row_c[:, :], row_f[:, :], float(LK - 1), None, ALU.min))
            dve.tensor_tensor(rows_at[:, :], row_c[:, :], seq_row[:, :], ALU.add).then_inc(rows_known, 1)
            core.ln_vector(dve, link, k_ln)
            n_g = B * GROUPS
            link(dve.tensor_tensor(kid[:, :, :], seg_r[:, :].unsqueeze(2).to_broadcast([ROW0, n_g, WIN]),
                                   win_r[:, :].unsqueeze(1).to_broadcast([ROW0, n_g, WIN]), ALU.add))
            link(dve.tensor_scalar(kid_c[:, :, :], kid[:, :, :], 0.0, float(LK - 1), ALU.max, ALU.min))
            link(dve.tensor_tensor(outside[:, :, :], kid[:, :, :], kid_c[:, :, :], ALU.not_equal))
            link(dve.tensor_scalar(outside[:, :, :], outside[:, :, :], NEG, None, ALU.mult))
            for n in range(n_g):
                ins = dve.tensor_tensor(mask[:, n, :].rearrange("p (q w) -> p q w", w=WIN),
                                  diag[:, :].rearrange("p (q w) -> p q w", w=WIN),
                                  outside[:, n, :].unsqueeze(1).to_broadcast([ROW0, GQ, WIN]), ALU.add)
                link(ins)
            dve.wait_ge(w_in, DMA * n_w)
            for j in range(HH):
                bank = 3 * (j % 2)
                dve.wait_ge(q_mm, 2 + j)
                link(dve.tensor_tensor(packed(rope_a[:, :]), packed(ps[:, bank + 1, 0:TOK]),
                                       rope_q[:, 0:1, :].to_broadcast([P, B, S]), ALU.mult))
                link(dve.tensor_tensor(packed(rope_b[:, :]), packed(ps[:, bank + 2, 0:TOK]),
                                       rope_q[:, 1:2, :].to_broadcast([P, B, S]), ALU.mult))
                for k in range(2):
                    r = slice(k * R, (k + 1) * R)
                    dve.tensor_tensor(q_cat[KVC:P, :, 2 * j + k, :],
                                      rope_a[r, :].rearrange("p (n q) -> p n q", q=GQ),
                                      rope_b[r, :].rearrange("p (n q) -> p n q", q=GQ), ALU.add) \
                        .then_inc(q_rot, 1)
                    dve.wait_ge(q_rot, 2 * j + k + 1)

            def keys_of(b):
                s = b % 2
                dve.wait_ge(got_turned, b + 1)
                dve.tensor_copy(got_t[:, s, 2, :], ps[:, 2, 0:gt]).then_inc(got_t_ready, 1)
                dve.wait_ge(key_mm, b + 1)
                dve.wait_ge(got_t_ready, 3 * (b + 1))
                link(dve.tensor_tensor(key_sin[KVC:P, :], ps[0:R, 4, 0:gt], got_t[0:R, s, 2, :], ALU.mult))
                dve.wait_ge(key_latent, b + 1)
                link(dve.tensor_tensor(keys[KVC:P, s, :], ps[KVC:P, 3, 0:gt], got_t[KVC:P, s, 2, :], ALU.mult))
                dve.tensor_tensor(keys[KVC:P, s, :], keys[KVC:P, s, :], key_sin[KVC:P, :], ALU.add) \
                    .then_inc(key_ready, 1)
                dve.wait_ge(key_ready, b + 1)

            def scored(n):
                dve.wait_ge(score_mm, n + 1)
                if n >= 2:
                    dve.wait_ge(exped, 2 * (n - 1))
                dve.scalar_tensor_tensor(s_sb[:, n % 2, :, :],
                                         ps[0:ROW0, 5, 0:2 * GR].rearrange("p (k r) -> p k r", k=2),
                                         scale, mask[:, n:n + 1, :].to_broadcast([ROW0, 2, GR]),
                                         ALU.mult, ALU.add).then_inc(score_sb, 1)
                dve.wait_ge(score_sb, n + 1)
                dve.tensor_reduce(neg_max[:, n % 2, :], s_sb[:, n % 2, :, :], AXIS.X, ALU.max,
                                  negate=True).then_inc(maxed, 1)

            def normalise(n):
                dve.wait_ge(exped, 2 * (n + 1))
                link(dve.reciprocal(inv[:, n % 2, :], sums[:, n % 2, :]))
                dve.tensor_tensor(prob[:, n % 2, :, :], prob[:, n % 2, :, :],
                                  inv[:, n % 2, :].unsqueeze(2).to_broadcast([ROW0, 2, GR]), ALU.mult) \
                    .then_inc(normed, 1)

            def mixed(n):
                b, g = n // GROUPS, n % GROUPS
                dve.wait_ge(lat_mm, n + 1)
                dve.tensor_copy(lat[:, :, b * SP + g * GQ:b * SP + (g + 1) * GQ],
                                ps[:, 7, 0:ROW0].rearrange("p (j q) -> p j q", q=GQ)).then_inc(lat_ready, 1)

            for n in range(n_g + 3):
                if n < n_g:
                    if n % GROUPS == 0:
                        keys_of(n // GROUPS)
                    scored(n)
                if 1 <= n <= n_g:
                    normalise(n - 1)
                if n >= 3:
                    mixed(n - 3)
            dve.wait_ge(out_mm, 1)
            for a in range(2):
                link(dve.tensor_tensor(core.x_rows[:, 2 * a:2 * a + 2, :].rearrange("p i d -> p (i d)"),
                                       core.x_rows[:, 2 * a:2 * a + 2, :].rearrange("p i d -> p (i d)"),
                                       ps[:, a, :], ALU.add))
            core.dve_n = link.n


FF0 = 1024
FT0 = FF0 // P
STEP = 0.1
QMIN, QMAX = -32768.0, 32767.0
ROUND = 1.5 * 2.0 ** 23


def lookup_ffn(core):
    nc, dram, ps = core.nc, core.dram, core.psum
    k_ln = core.new_norm()
    dve0 = core.dve_n
    ctx = ExitStack()
    with ctx:
        def sb(name, shape, dt=F32):
            return ctx.enter_context(nc.sbuf_tensor(name, shape, dt))
        w1 = sb("f_w1", [P, DC, FF0])
        w2 = sb("f_w2", [P, FT0, D])
        tenths = sb("f_tenths", [P, 2, TOK])
        act_t = sb("f_act_t", [P, FT0, T])
        sem = core.sem
        w_in, up_mm, rounded, acted, out_mm = (sem("f_" + n) for n in
                                               ("weights_in", "up_mm", "rounded", "acted", "out_mm"))
        block = ctx.enter_context(nc.Block())

        @block.sync
        def _(sp):
            sp.dma_start(w1[:, :, :], dram["f_w1"]).then_inc(w_in, DMA)
            sp.dma_start(w2[:, :, :], dram["f_w2"]).then_inc(w_in, DMA)

        @block.gpsimd
        def _(pool):
            core.ln_pool(pool, k_ln)

        @block.tensor
        def _(pe):
            core.ln_tensor(pe, k_ln)
            pe.wait_ge(core.ln_cols, core.cols_ready(k_ln))
            pe.wait_ge(w_in, 2 * DMA)
            for f in range(FT0):
                if f >= 4:
                    pe.wait_ge(rounded, f - 3)
                for c in range(DC):
                    ins = pe.matmul(packed(ps[:, 2 + f % 4, 0:TOK]), w1[:, c, f * P:(f + 1) * P], core.tok(c),
                                    start=(c == 0), stop=(c == DC - 1))
                ins.then_inc(up_mm, 1)
            pe.wait_ge(acted, FT0)
            for i in range(PAIRS):
                for f in range(FT0):
                    ins = pe.matmul(ps[:, 6 + i // 2, (i % 2) * D:(i % 2 + 1) * D],
                                    act_t[:, f, i * P:(i + 1) * P], w2[:, f, :],
                                    start=(f == 0), stop=(f == FT0 - 1))
            ins.then_inc(out_mm, 1)

        @block.scalar
        def _(act):
            core.ln_scalar(act, k_ln)
            for f in range(FT0):
                act.wait_ge(rounded, f + 1)
                act.activation(unpad(act_t[:, f, :]), packed(tenths[:, f % 2, :]), ACT.Gelu_apprx_tanh,
                               scale=STEP).then_inc(acted, 1)

        @block.vector
        def _(dve):
            link = InOrder(dve, core.dve_step, dve0)
            link(dve.memset(act_t[:, :, :], 0.0))
            core.ln_vector(dve, link, k_ln)
            for f in range(FT0):
                dve.wait_ge(up_mm, f + 1)
                if f >= 2:
                    dve.wait_ge(acted, f - 1)
                t = tenths[:, f % 2, :]
                link(dve.tensor_scalar(t, ps[:, 2 + f % 4, 0:TOK], 1.0 / STEP, QMIN, ALU.mult, ALU.max))
                link(dve.tensor_scalar(t, t, QMAX, ROUND, ALU.min, ALU.add))
                dve.tensor_scalar(t, t, ROUND, None, ALU.subtract).then_inc(rounded, 1)
            dve.wait_ge(out_mm, 1)
            for a in range(2):
                rows = core.x_rows[:, 2 * a:2 * a + 2, :].rearrange("p i d -> p (i d)")
                link(dve.tensor_tensor(rows, rows, ps[:, 6 + a, :], ALU.add))
            core.dve_n = link.n


NH2, HD2, FD2 = 16, 16, 64
HP = NH2 // 2
VW = 2 * HD2 + 1
BW = 2 * HD2 + 2
FG = 512
AHEAD = 8
F32R = mybir.dt.float32r


def split(x, y):
    (x_hi, x_lo), (y_hi, y_lo) = x, y
    return (x_hi, y_hi), (x_hi, y_lo), (x_lo, y_hi)


def memory_attention_and_features(core):
    nc, dram, ps = core.nc, core.dram, core.psum
    k_ln = core.new_norm()
    dve0, Z = core.dve_n, AHEAD
    ctx = ExitStack()
    with ctx:
        def sb(name, shape, dt=F32):
            return ctx.enter_context(nc.sbuf_tensor("c_" + name, shape, dt))

        def parts(name, shape):
            return sb(name + "_hi", shape, F32R), sb(name + "_lo", shape, F32R)
        ctx_t = sb("ctx_t", [P, 2, DC, LK])
        ctx_r = sb("ctx_r", [KP, 2, KT, D])
        t_hi, t_lo = t_parts = parts("t", [P, DC, LK])
        w_k = sb("w_k", [P, DC, D])
        w_v = sb("w_v", [P, DC, D])
        w_kf = sb("w_kf", [P, FG])
        wk_hi, wk_lo = wk_parts = parts("wk", [P, DC, D])
        wv_hi, wv_lo = wv_parts = parts("wv", [P, DC, D])
        wf_hi, wf_lo = wf_parts = parts("wf", [P, FG])
        b_k = sb("b_k", [P, 2])
        mask2 = sb("mask2", [KP, B, KT])
        mask_now = sb("mask_now", [KP, KT])
        zero = sb("zero", [1, 512])
        q_pair = sb("q_pair", [P, DC, P])
        mask_u8 = sb("mask_u8", [P, LK // 4], I32)
        mask_add = sb("mask_add", [P, LK])
        any_key = sb("any_key", [P, 1])
        prob = sb("prob", [P, LK])
        neg_max = sb("neg_max", [P, 1])
        sums = sb("sums", [P, 1])
        inv = sb("inv", [P, 1])
        prob_t = sb("prob_t", [KP, KT, P])
        k_hi, k_lo = k_parts = parts("k", [P, 2, LK])
        feat = sb("feat", [KP, 2, 2, FG])
        v_aug = sb("v_aug", [KP, 2, 2, HP, VW])
        sums_sb = sb("sums_sb", [P, 512])
        sem = core.sem
        w_in = sem("c_weights_in")
        t_in = [sem("c_t_in0"), sem("c_t_in1")]
        names = ("r_in", "mask_in", "w_hi_ready", "w_lo_ready", "t_hi_ready", "t_lo_ready", "q_staged",
                 "score_mm", "maxed", "mask_read", "exped", "turned", "turned_sb", "out_mm", "added",
                 "kt_mm", "k_hi_ready", "k_lo_ready", "v_mm", "v_sb",
                 "feat_mm", "feat_act", "feat_dve", "sum_mm", "sum_sb", "sum_turned", "sum_kept")
        (r_in, mask_in, w_hi_ready, w_lo_ready, t_hi_ready, t_lo_ready, q_staged,
         score_mm, maxed, mask_read, exped, turned, turned_sb, out_mm, added,
         kt_mm, k_hi_ready, k_lo_ready, v_mm, v_sb,
         feat_mm, feat_act, feat_dve, sum_mm, sum_sb, sum_turned, sum_kept) = (
            sem("c_" + n) for n in names)
        weights = ((w_k[:, :, :], "c_w_k"), (w_v[:, :, :], "c_w_v"), (w_kf[:, :], "c_w_kf"))
        w_splits = ((w_k[:, :, :], wk_hi[:, :, :], wk_lo[:, :, :]), (w_v[:, :, :], wv_hi[:, :, :], wv_lo[:, :, :]),
                    (w_kf[:, :], wf_hi[:, :], wf_lo[:, :]))
        n_in = DMA * (len(weights) + 2)
        KT2 = KT // 2
        kv_sums = core.kv_sums
        block = ctx.enter_context(nc.Block())

        @block.sync
        def _(sp):
            for k in range(2):
                sp.dma_start(ctx_t[:, k, :, :], dram["ctx_t"][k]).then_inc(t_in[k], DMA)
            for dst, src in weights + ((b_k[:, :], "c_b_k"), (mask2[:, :, :], "c_mask2")):
                sp.dma_start(dst, dram[src]).then_inc(w_in, DMA)
            for k in range(2):
                sp.dma_start(mask_u8[k * SP:(k + 1) * SP, :],
                             dram["c_mask"][k].partition_broadcast(SP)).then_inc(mask_in, DMA)
            for k in range(2):
                sp.dma_start(ctx_r[:, k, :, :], dram["ctx_r"][k]).then_inc(r_in, DMA)
            with sp.Fori(1, PAIRS) as n:
                sp.wait_ge(mask_read, Z + n)
                for k in range(2):
                    sp.dma_start(mask_u8[k * SP:(k + 1) * SP, :],
                                 dram["c_mask"][2 * n + k].partition_broadcast(SP)).then_inc(mask_in, DMA)
                sp.wait_ge(score_mm, Z + n)
                for k in range(2):
                    sp.wait_ge(t_hi_ready, Z + DC * (2 * n - 1 + k))
                    sp.wait_ge(t_lo_ready, Z + DC * (2 * n - 1 + k))
                    sp.dma_start(ctx_t[:, k, :, :], dram["ctx_t"][2 * n + k]).then_inc(t_in[k], DMA)
                sp.wait_ge(out_mm, Z + n)
                for k in range(2):
                    sp.dma_start(ctx_r[:, k, :, :], dram["ctx_r"][2 * n + k]).then_inc(r_in, DMA)

        @block.gpsimd
        def _(pool):
            core.ln_pool(pool, k_ln)
            pool.sem_inc(q_staged, Z)
            pool.wait_ge(core.ln_cols, core.cols_ready(k_ln))
            with pool.Fori(0, PAIRS) as n:
                pool.wait_ge(score_mm, Z + n)
                pool.tensor_copy(q_pair[:, :, :], core.xn_cols[:, :, bass.ds(n * P, P)]).then_inc(q_staged, 1)

        @block.tensor
        def _(pe):
            for s in (score_mm, turned, out_mm, kt_mm, v_mm, feat_mm, sum_mm, sum_turned):
                pe.sem_inc(s, Z)
            core.ln_tensor(pe, k_ln)
            pe.wait_ge(w_lo_ready, len(weights))

            def scores(n):
                pe.wait_ge(q_staged, Z + n + 1)
                pe.wait_ge(added, Z + n)
                for k in range(2):
                    pe.wait_ge(t_in[k], DMA * (n + 1))
                    for m in range(3):
                        for c in range(DC):
                            ins = pe.matmul(ps[k * SP:(k + 1) * SP, m, 0:KN], q_pair[:, c, k * SP:(k + 1) * SP],
                                            ctx_t[:, k, c, m * KN:(m + 1) * KN],
                                            start=(c == 0), stop=(c == DC - 1))
                ins.then_inc(score_mm, 1)

            def attend(n):
                pe.wait_ge(exped, Z + n + 1)
                for u in range(3):
                    if u == 2:
                        pe.wait_ge(turned_sb, Z + 3 * n + 1)
                    for x in range(4):
                        t = 4 * u + x
                        ins = pe.transpose(ps[0:KP, u % 2, x * P:(x + 1) * P], prob[:, t * KP:(t + 1) * KP],
                                           core.ident[:, :])
                    ins.then_inc(turned, 1)
                turn_sums(2 * n)
                pe.wait_ge(turned_sb, Z + 3 * n + 3)
                pe.wait_ge(r_in, 2 * DMA * (n + 1))
                for k in range(2):
                    for t in range(KT):
                        ins = pe.matmul(ps[k * SP:(k + 1) * SP, 2, 0:D], prob_t[:, t, k * SP:(k + 1) * SP],
                                        ctx_r[:, k, t, :], start=(t == 0), stop=(t == KT - 1))
                ins.then_inc(out_mm, 1)

            def keys(b):
                pe.wait_ge(t_lo_ready, Z + DC * (b + 1))
                pe.wait_ge(feat_act, Z + KT * b)
                pe.wait_ge(feat_dve, Z + KT * b)
                for e in range(6):
                    g, m = e // 3, e % 3
                    if e >= 3:
                        pe.wait_ge(k_lo_ready, Z + 6 * b + e - 2)
                    for c in range(DC):
                        for y, (wt, x) in enumerate(split(wk_parts, t_parts)):
                            ins = pe.matmul(ps[:, 4 + m, 0:KN], wt[:, c, g * P:(g + 1) * P],
                                            x[:, c, m * KN:(m + 1) * KN],
                                            start=(c == 0 and y == 0), stop=(c == DC - 1 and y == 2))
                    ins.then_inc(kt_mm, 1)

            def values(b, t):
                if t == 0:
                    pe.wait_ge(sum_kept, Z + b)
                pe.wait_ge(v_sb, Z + 2 * (KT2 * b + t // 2))
                for x in range(2):
                    for c in range(DC):
                        for y, (xt, wt) in enumerate(split(t_parts, wv_parts)):
                            ins = pe.matmul(ps[0:KP, 3, x * D:(x + 1) * D],
                                            xt[:, c, (t + x) * KP:(t + x + 1) * KP], wt[:, c, :],
                                            start=(c == 0 and y == 0), stop=(c == DC - 1 and y == 2))
                ins.then_inc(v_mm, 1)

            def features(b, t):
                for g in range(2):
                    m = 2 * t + g
                    if m < 3:
                        pe.wait_ge(k_lo_ready, Z + 6 * (b + 1))
                    else:
                        pe.wait_ge(feat_dve if m % 2 == 0 else feat_act, Z + KT * b + (m - 3) // 2 + 1)
                    for y, (k, wt) in enumerate(split(k_parts, wf_parts)):
                        ins = pe.matmul(ps[0:KP, 4 + m % 3, :], k[:, g, t * KP:(t + 1) * KP], wt[:, :],
                                        start=(y == 0), stop=(y == 2))
                    ins.then_inc(feat_mm, 1)

            def add_sums(b, t):
                pe.wait_ge(feat_act, Z + KT * b + t + 1)
                pe.wait_ge(feat_dve, Z + KT * b + t + 1)
                pe.wait_ge(v_sb, Z + 2 * (KT2 * b + t // 2 + 1))
                for p in range(HP):
                    r = (p % 2) * SP
                    ins = pe.matmul(ps[r:r + VW, 7, (p // 2) * P:(p // 2 + 1) * P], v_aug[:, t // 2 % 2, t % 2, p, :],
                                    feat[:, t % 2, p // 4, (p % 4) * P:(p % 4 + 1) * P],
                                    start=False, stop=False, skip_group_check=True)
                ins.then_inc(sum_mm, 1)

            def turn_sums(b):
                pe.wait_ge(sum_sb, Z + b + 1)
                for q in range(HP // 2):
                    ins = pe.transpose(ps[:, 3, q * P:(q + 1) * P], sums_sb[:, q * P:(q + 1) * P],
                                       core.ident[:, :])
                ins.then_inc(sum_turned, 1)

            def sequence(b):
                keys(b)
                pe.wait_ge(sum_sb, Z + b)
                pe.matmul(ps[:, 7, :], zero[0:1, 0:P], zero[0:1, :], start=True, stop=True,
                          skip_group_check=True)
                for t in range(KT + 1):
                    if t < KT:
                        if t % 2 == 0:
                            values(b, t)
                        features(b, t)
                    if t >= 1:
                        add_sums(b, t - 1)

            with pe.Fori(0, PAIRS) as n:
                scores(n)
                sequence(2 * n)
                attend(n)
                sequence(2 * n + 1)
                turn_sums(2 * n + 1)

        @block.scalar
        def _(act):
            for s in (exped, turned_sb, t_hi_ready, k_hi_ready, feat_act, sum_sb):
                act.sem_inc(s, Z)

            def split_context(b, n, k):
                act.wait_ge(t_in[k], DMA * (n + 1))
                for c in range(DC):
                    act.copy(t_hi[:, c, :], ctx_t[:, k, c, :]).then_inc(t_hi_ready, 1)
            core.ln_scalar(act, k_ln)
            act.wait_ge(w_in, n_in)
            for full, hi, _lo in w_splits:
                act.copy(hi, full).then_inc(w_hi_ready, 1)
            split_context(0, 0, 0)

            def sequence(b, n, k, last):
                for e in range(6):
                    act.wait_ge(kt_mm, Z + 6 * b + e + 1)
                    act.activation(k_hi[:, e // 3, (e % 3) * KN:(e % 3 + 1) * KN], ps[:, 4 + e % 3, 0:KN],
                                   ACT.Identity, bias=b_k[:, e // 3:e // 3 + 1]).then_inc(k_hi_ready, 1)
                for t in range(KT):
                    act.wait_ge(sum_mm, Z + KT * b + t - 1)
                    act.wait_ge(feat_mm, Z + 2 * (KT * b + t) + 1)
                    act.activation(feat[:, t % 2, 0, :], ps[0:KP, 4 + (2 * t) % 3, :], ACT.Relu) \
                        .then_inc(feat_act, 1)
                    if t == KT - 2 and not last:
                        act.wait_ge(v_mm, Z + KT2 * (b + 1))
                        split_context(b + 1, n + k, 1 - k)
                act.wait_ge(sum_mm, Z + KT * (b + 1))
                act.wait_ge(sum_turned, Z + b)
                act.copy(sums_sb[:, :], ps[:, 7, :]).then_inc(sum_sb, 1)

            def pair(n, last):
                act.wait_ge(maxed, Z + n + 1)
                act.activation(prob[:, :], prob[:, :], ACT.Exp, bias=neg_max[:, 0:1],
                               accum_out=sums[:, 0:1]).then_inc(exped, 1)
                sequence(2 * n, n, 0, False)
                for u in range(3):
                    act.wait_ge(turned, Z + 3 * n + u + 1)
                    act.copy(prob_t[:, 4 * u:4 * u + 4, :].rearrange("p t q -> p (t q)"),
                             ps[0:KP, u % 2, :]).then_inc(turned_sb, 1)
                sequence(2 * n + 1, n, 1, last)
            with act.Fori(0, PAIRS - 1) as n:
                pair(n, last=False)
            pair(PAIRS - 1, last=True)

        @block.vector
        def _(dve):
            link = InOrder(dve, core.dve_step, dve0)
            for s in (maxed, mask_read, added, t_lo_ready, k_lo_ready, v_sb, feat_dve, sum_kept):
                dve.sem_inc(s, Z)
            core.ln_vector(dve, link, k_ln)
            link(dve.memset(zero[:, :], 0.0))
            link(dve.memset(kv_sums[:, :, :, :], 0.0))

            def split_context(b, k):
                for c in range(DC):
                    dve.wait_ge(t_hi_ready, Z + DC * b + c + 1)
                    dve.tensor_tensor(t_lo[:, c, :], ctx_t[:, k, c, :], t_hi[:, c, :].bitcast(F32),
                                      ALU.subtract).then_inc(t_lo_ready, 1)
            for y, (full, hi, lo) in enumerate(w_splits):
                dve.wait_ge(w_hi_ready, y + 1)
                dve.tensor_tensor(lo, full, hi.bitcast(F32), ALU.subtract).then_inc(w_lo_ready, 1)
            split_context(0, 0)

            def softmax(n):
                dve.wait_ge(mask_in, 2 * DMA * (n + 1))
                dve.tensor_scalar(mask_add[:, :], mask_u8[:, :].bitcast(U8), 1.0, -NEG, ALU.subtract, ALU.mult) \
                    .then_inc(mask_read, 1)
                dve.wait_ge(mask_read, Z + n + 1)
                link(dve.tensor_reduce(any_key[:, :], mask_add[:, :], AXIS.X, ALU.max))
                link(dve.tensor_scalar(any_key[:, :], any_key[:, :], 0.0, None, ALU.is_equal))
                dve.wait_ge(score_mm, Z + n + 1)
                dve.wait_ge(turned, Z + 3 * n)
                link(dve.scalar_tensor_tensor(prob[:, :].rearrange("p (m n) -> p m n", m=3), ps[:, 0:3, 0:KN],
                                              1.0 / 16.0, mask_add[:, :].rearrange("p (m n) -> p m n", m=3),
                                              ALU.mult, ALU.add))
                dve.tensor_reduce(neg_max[:, :], prob[:, :], AXIS.X, ALU.max, negate=True).then_inc(maxed, 1)

            def add_out(n):
                dve.wait_ge(exped, Z + n + 1)
                link(dve.reciprocal(inv[:, :], sums[:, :]))
                link(dve.tensor_tensor(inv[:, :], inv[:, :], any_key[:, :], ALU.mult))
                dve.wait_ge(out_mm, Z + n + 1)
                row = core.x_rows[:, bass.ds(n, 1), :].rearrange("p a d -> p (a d)")
                dve.scalar_tensor_tensor(row, ps[:, 2, 0:D], inv[:, 0:1], row,
                                         ALU.mult, ALU.add).then_inc(added, 1)

            def sequence(b, k, last):
                dve.wait_ge(v_sb, Z + 2 * KT2 * b)
                link(dve.tensor_copy(mask_now[:, :], mask2[:, bass.ds(b, 1), :].rearrange("p a t -> p (a t)")))
                for e in range(6):
                    dve.wait_ge(k_hi_ready, Z + 6 * b + e + 1)
                    at = slice((e % 3) * KN, (e % 3 + 1) * KN)
                    dve.scalar_tensor_tensor(k_lo[:, e // 3, at], ps[:, 4 + e % 3, 0:KN],
                                             b_k[:, e // 3:e // 3 + 1], k_hi[:, e // 3, at].bitcast(F32),
                                             ALU.add, ALU.subtract).then_inc(k_lo_ready, 1)
                for t in range(KT):
                    slot = t // 2 % 2
                    dve.wait_ge(sum_mm, Z + KT * b + t - 1)
                    if t % 2 == 0:
                        dve.wait_ge(v_mm, Z + KT2 * b + t // 2 + 1)
                        dve.tensor_tensor(v_aug[:, slot, :, :, 0:2 * HD2],
                                          ps[0:KP, 3, :].rearrange("p (x h e) -> p x h e", x=2, h=HP),
                                          mask_now[:, t:t + 2].unsqueeze(2).unsqueeze(3)
                                          .to_broadcast([KP, 2, HP, 2 * HD2]), ALU.mult).then_inc(v_sb, 1)
                        dve.tensor_copy(v_aug[:, slot, :, :, 2 * HD2],
                                        mask_now[:, t:t + 2].unsqueeze(2).to_broadcast([KP, 2, HP])) \
                            .then_inc(v_sb, 1)
                    dve.wait_ge(feat_mm, Z + 2 * (KT * b + t) + 2)
                    dve.tensor_scalar(feat[:, t % 2, 1, :], ps[0:KP, 4 + (2 * t + 1) % 3, :], 0.0, None,
                                      ALU.max).then_inc(feat_dve, 1)
                    if t == KT - 2 and not last:
                        split_context(b + 1, 1 - k)
                dve.wait_ge(sum_turned, Z + b + 1)
                turned_sums = ps[:, 3, :].rearrange("p (h w) -> p h w", w=SP)
                dst = kv_sums[:, bass.ds(b, 1), :, :].rearrange("p a h w -> p (a h) w")
                lo, hi = slice(0, FD2), slice(FD2, P)
                link(dve.tensor_copy(dst[lo, :, 0:HD2], turned_sums[lo, :, 0:HD2]))
                link(dve.tensor_copy(dst[hi, :, HD2:2 * HD2], turned_sums[hi, :, HD2:2 * HD2]))
                link(dve.tensor_copy(dst[lo, :, 2 * HD2], turned_sums[lo, :, 2 * HD2]))
                dve.tensor_copy(dst[hi, :, 2 * HD2 + 1], turned_sums[hi, :, 2 * HD2]).then_inc(sum_kept, 1)

            def pair(n, last):
                softmax(n)
                sequence(2 * n, 0, False)
                add_out(n)
                sequence(2 * n + 1, 1, last)
            first, per_pair = link.n, 3 + 2 + 2 * (1 + 3)
            with dve.Fori(0, PAIRS - 1) as n:
                link.loop(n, first, per_pair)
                pair(n, last=False)
            link.end(first, per_pair, PAIRS - 1)
            pair(PAIRS - 1, last=True)
            core.dve_n = link.n


def linear_attention(core):
    nc, dram, ps = core.nc, core.dram, core.psum
    k_ln = core.new_norm()
    dve0 = core.dve_n
    ctx = ExitStack()
    with ctx:
        def sb(name, shape, dt=F32):
            return ctx.enter_context(nc.sbuf_tensor("l_" + name, shape, dt))
        w_q = sb("w_q", [P, DC, D])
        w_o = sb("w_o", [P, DC, D])
        w_qf = sb("w_qf", [P, FG])
        b_q = sb("b_q", [P, 2])
        b_v = sb("b_v", [P, D])
        b_o = sb("b_o", [P, D])
        q_t = sb("q_t", [P, 2, T])
        feat_t = sb("feat_t", [P, HP, T])
        den = sb("den", [P, PAIRS, NH2])
        vals = sb("vals", [P, PAIRS, D])
        bias = sb("bias", [P, PAIRS, D])
        vals_t = sb("vals_t", [P, DC, T])
        sem = core.sem
        w_in, q_mm, q_sb, feat_mm, feat_sb, att_mm, divided, turned, turned_sb, out_mm = (sem("l_" + n) for n in (
            "weights_in", "q_mm", "q_sb", "feat_mm", "feat_sb", "att_mm", "divided", "turned", "turned_sb",
            "out_mm"))
        loads = ((w_q[:, :, :], "l_w_q"), (w_o[:, :, :], "l_w_o"), (w_qf[:, :], "l_w_qf"), (b_q[:, :], "l_b_q"))
        block = ctx.enter_context(nc.Block())

        @block.sync
        def _(sp):
            for dst, src in loads:
                sp.dma_start(dst, dram[src]).then_inc(w_in, DMA)
            sp.dma_start(b_v[:, :], dram["l_b_v"].partition_broadcast(P)).then_inc(w_in, DMA)
            sp.dma_start(b_o[:, :], dram["l_b_o"].partition_broadcast(P)).then_inc(w_in, DMA)
        n_in = DMA * (len(loads) + 2)

        @block.gpsimd
        def _(pool):
            core.ln_pool(pool, k_ln)

        @block.tensor
        def _(pe):
            core.ln_tensor(pe, k_ln)
            pe.wait_ge(core.ln_cols, core.cols_ready(k_ln))
            pe.wait_ge(w_in, n_in)
            for g in range(2):
                for c in range(DC):
                    ins = pe.matmul(ps[:, 2 + g, :], w_q[:, c, g * P:(g + 1) * P], core.xn_cols[:, c, :],
                                    start=(c == 0), stop=(c == DC - 1))
                ins.then_inc(q_mm, 1)
            for p in range(HP):
                if p % 4 == 0:
                    pe.wait_ge(q_sb, p // 4 + 1)
                if p >= 4:
                    pe.wait_ge(feat_sb, p - 3)
                pe.matmul(ps[:, 4 + p % 4, :], w_qf[:, (p % 4) * P:(p % 4 + 1) * P], q_t[:, p // 4, :],
                          start=True, stop=True).then_inc(feat_mm, 1)
            pe.wait_ge(feat_sb, HP)
            for b in range(B):
                for p in range(HP):
                    ins = pe.matmul(ps[(b % 2) * SP:(b % 2 + 1) * SP, b // 2, p * BW:(p + 1) * BW],
                                    feat_t[:, p, b * SP:(b + 1) * SP], core.kv_sums[:, b, p, :],
                                    start=True, stop=True)
                if b % 2:
                    ins.then_inc(att_mm, 1)
            for i in range(PAIRS):
                pe.wait_ge(divided, i + 1)
                for c in range(DC):
                    ins = pe.transpose(ps[:, 4 + c, i * P:(i + 1) * P], vals[:, i, c * P:(c + 1) * P],
                                       core.ident[:, :])
            ins.then_inc(turned, 1)
            pe.wait_ge(turned_sb, DC)
            for i in range(PAIRS):
                for c in range(DC):
                    ins = pe.matmul(ps[:, 6 + i // 2, (i % 2) * D:(i % 2 + 1) * D],
                                    vals_t[:, c, i * P:(i + 1) * P], w_o[:, c, :],
                                    start=(c == 0), stop=(c == DC - 1))
            ins.then_inc(out_mm, 1)

        @block.scalar
        def _(act):
            core.ln_scalar(act, k_ln)
            act.wait_ge(w_in, n_in)
            for g in range(2):
                act.wait_ge(q_mm, g + 1)
                act.activation(q_t[:, g, :], ps[:, 2 + g, :], ACT.Identity, bias=b_q[:, g:g + 1]) \
                    .then_inc(q_sb, 1)
            for p in range(HP):
                act.wait_ge(feat_mm, p + 1)
                act.activation(feat_t[:, p, :], ps[:, 4 + p % 4, :], ACT.Relu).then_inc(feat_sb, 1)
            act.wait_ge(turned, 1)
            for c in range(DC):
                act.copy(vals_t[:, c, :], ps[:, 4 + c, :]).then_inc(turned_sb, 1)

        @block.vector
        def _(dve):
            link = InOrder(dve, core.dve_step, dve0)
            core.ln_vector(dve, link, k_ln)
            dve.wait_ge(w_in, n_in)
            for i in range(PAIRS):
                dve.wait_ge(att_mm, i + 1)
                got = ps[:, i, 0:HP * BW].rearrange("p (h w) -> p h w", w=BW)
                row = vals[:, i, :].rearrange("p (h e) -> p h e", e=HD2)
                bias_row = bias[:, i, :].rearrange("p (h e) -> p h e", e=HD2)
                each = den[:, i, :].rearrange("p (h k) -> p h k", k=2)
                link(dve.tensor_copy(each, got[:, :, 2 * HD2:BW]))
                link(dve.tensor_tensor(bias_row, b_v[:, :].rearrange("p (h e) -> p h e", e=HD2),
                                       den[:, i, :].unsqueeze(2).to_broadcast([P, NH2, HD2]), ALU.mult))
                link(dve.tensor_tensor(vals[:, i, :].rearrange("p (h e) -> p h e", h=HP),
                                       bias[:, i, :].rearrange("p (h e) -> p h e", h=HP),
                                       got[:, :, 0:2 * HD2], ALU.add))
                link(dve.tensor_scalar(den[:, i, :], den[:, i, :], 1e-8, None, ALU.add))
                link(dve.reciprocal(den[:, i, :], den[:, i, :]))
                dve.tensor_tensor(row, row, den[:, i, :].unsqueeze(2).to_broadcast([P, NH2, HD2]),
                                  ALU.mult).then_inc(divided, 1)
            for i in range(PAIRS):
                link(dve.tensor_tensor(core.x_rows[:, i, :], core.x_rows[:, i, :], b_o[:, :], ALU.add))
            dve.wait_ge(out_mm, 1)
            for a in range(2):
                rows = core.x_rows[:, 2 * a:2 * a + 2, :].rearrange("p i d -> p (i d)")
                link(dve.tensor_tensor(rows, rows, ps[:, 6 + a, :], ALU.add))
            core.dve_n = link.n


FF2 = 704
FT2 = -(-FF2 // P)
FP8_MAX = 448.0
GLOBAL_DIV = 448.0 * 6.0
EXPONENT = 0x7F800000
FP8_LEAST = 2.0 ** -6
FP8_ROUND = 1.5 * 2.0 ** 20


def quantised_ffn(core):
    nc, dram, ps = core.nc, core.dram, core.psum
    k_ln = core.new_norm(turned=False)
    dve0, pool0 = core.dve_n, core.pool_n
    ctx = ExitStack()
    with ctx:
        def sb(name, shape, dt=F32):
            return ctx.enter_context(nc.sbuf_tensor("q_" + name, shape, dt))
        order = sb("order", [P, FT2], I32)
        w_rows = sb("w_rows", [P, 2, FT2, D])
        w_cols = sb("w_cols", [P, 2, DC, FT2 * P])
        wd_rows = sb("wd_rows", [P, DC, FF2])
        wd_cols = sb("wd_cols", [P, FT2, D])
        peak = sb("peak", [P, 2 * FT2 + DC])
        w_scale = sb("w_scale", [P, 2 * FT2 + DC])
        w_inv = sb("w_inv", [P, 2 * FT2 + DC])
        unit = sb("unit", [P, 2, FF2])
        row_peak = sb("row_peak", [P, PAIRS])
        all_peak = sb("all_peak", [P, 4])
        row_scale = sb("row_scale", [P, PAIRS])
        row_inv = sb("row_inv", [P, PAIRS])
        row_peak2 = sb("row_peak2", [P, PAIRS])
        all_peak2 = sb("all_peak2", [P, 4])
        row_scale2 = sb("row_scale2", [P, PAIRS])
        row_inv2 = sb("row_inv2", [P, PAIRS])
        xq = sb("xq", [P, PAIRS, D])
        xq_cols = sb("xq_cols", [P, DC, T])
        silu = sb("silu", [P, 2, FF2])
        hid = sb("hid", [P, PAIRS, FF2])
        hid_cols = sb("hid_cols", [P, 2, FT2, P])
        sem = core.sem
        (order_in, rows_in, wd_in, w_quant, w_turned, w_cols_ready, peak_known, peak_all, x_quant, x_turned,
         x_cols_ready, up_mm, silued, hid_ready, peak2_known, peak2_all, hid_quant, hid_turned, hid_cols_ready,
         out_mm) = (sem("q_" + n) for n in (
            "order_in", "rows_in", "wd_in", "w_quant", "w_turned", "w_cols_ready", "peak_known", "peak_all",
            "x_quant", "x_turned", "x_cols_ready", "up_mm", "silued", "hid_ready", "peak2_known", "peak2_all",
            "hid_quant", "hid_turned", "hid_cols_ready", "out_mm"))
        block = ctx.enter_context(nc.Block())
        half = FF2 // 2

        @block.sync
        def _(sp):
            sp.dma_start(order[:, :], dram["q_order"]).then_inc(order_in, DMA)
            sp.dma_start(wd_rows[:, :, :], dram["q_w_down"]).then_inc(wd_in, DMA)

        @block.gpsimd
        def _(pool):
            pool.wait_ge(order_in, DMA)
            for k, src in enumerate(("q_w_gate", "q_w_up")):
                for f in range(FT2):
                    pool.indirect_dma_start(w_rows[:, k, f, :], None, dram[src],
                                            bass.IndirectOffsetOnAxis(ap=order[:, f:f + 1], axis=0)) \
                        .then_inc(rows_in, DMA)
            core.ln_pool(pool, k_ln)
            pool.wait_ge(peak_known, 1)
            pool.partition_all_reduce(all_peak[:, 1:2], all_peak[:, 0:1], P, REDUCE.max).then_inc(peak_all, 1)
            pool.wait_ge(peak2_known, 1)
            pool.partition_all_reduce(all_peak2[:, 1:2], all_peak2[:, 0:1], P, REDUCE.max).then_inc(peak2_all, 1)

        @block.tensor
        def _(pe):
            n = 0
            for k in range(2):
                for f in range(FT2):
                    pe.wait_ge(w_quant, k * FT2 + f + 1)
                    if n >= 6:
                        pe.wait_ge(w_cols_ready, n - 5)
                    for c in range(DC):
                        ins = pe.transpose(ps[:, 2 + n % 6, c * P:(c + 1) * P], w_rows[:, k, f, c * P:(c + 1) * P],
                                           core.ident[:, :])
                    ins.then_inc(w_turned, 1)
                    n += 1
            pe.wait_ge(w_quant, 2 * FT2 + DC)
            for f in range(FT2):
                w = min(P, FF2 - f * P)
                pe.wait_ge(w_cols_ready, n - 5)
                for c in range(DC):
                    ins = pe.transpose(ps[0:w, 2 + n % 6, c * P:(c + 1) * P], wd_rows[:, c, f * P:f * P + w],
                                       core.ident[:, :])
                ins.then_inc(w_turned, 1)
                n += 1
            for i in range(PAIRS):
                pe.wait_ge(x_quant, i + 1)
                for c in range(DC):
                    ins = pe.transpose(ps[:, c, i * P:(i + 1) * P], xq[:, i, c * P:(c + 1) * P], core.ident[:, :])
            ins.then_inc(x_turned, 1)
            pe.wait_ge(x_cols_ready, DC)
            pe.wait_ge(w_cols_ready, 3 * FT2)
            for i in range(PAIRS):
                if i >= 2:
                    pe.wait_ge(hid_ready, i - 1)
                for k in range(2):
                    for a in range(2):
                        for c in range(DC):
                            ins = pe.matmul(ps[:, 4 * (i % 2) + 2 * k + a, 0:half], xq_cols[:, c, i * P:(i + 1) * P],
                                            w_cols[:, k, c, a * half:(a + 1) * half],
                                            start=(c == 0), stop=(c == DC - 1))
                ins.then_inc(up_mm, 1)
            pe.wait_ge(hid_ready, PAIRS)
            for i in range(PAIRS):
                pe.wait_ge(hid_quant, i + 1)
                if i >= 2:
                    pe.wait_ge(hid_cols_ready, 2 * (i - 1))
                for f in range(FT2):
                    w = min(P, FF2 - f * P)
                    ins = pe.transpose(ps[0:w, 2 * (i % 2) + f // 4, (f % 4) * P:(f % 4 + 1) * P],
                                       hid[:, i, f * P:f * P + w], core.ident[:, :])
                ins.then_inc(hid_turned, 1)
                pe.wait_ge(hid_cols_ready, 2 * (i + 1))
                for f in range(FT2):
                    w = min(P, FF2 - f * P)
                    ins = pe.matmul(ps[:, 6 + i // 2, (i % 2) * D:(i % 2 + 1) * D], hid_cols[0:w, i % 2, f, :],
                                    wd_cols[0:w, f, :], start=(f == 0), stop=(f == FT2 - 1))
            ins.then_inc(out_mm, 1)

        @block.scalar
        def _(act):
            n = 0
            for k in range(2):
                for f in range(FT2):
                    act.wait_ge(w_turned, n + 1)
                    act.copy(w_cols[:, k, :, f * P:(f + 1) * P],
                             ps[:, 2 + n % 6, 0:D].rearrange("p (c d) -> p c d", c=DC)).then_inc(w_cols_ready, 1)
                    n += 1
            for f in range(FT2):
                w = min(P, FF2 - f * P)
                act.wait_ge(w_turned, n + 1)
                act.copy(wd_cols[0:w, f, :], ps[0:w, 2 + n % 6, 0:D]).then_inc(w_cols_ready, 1)
                n += 1
            act.wait_ge(x_turned, 1)
            for c in range(DC):
                act.copy(xq_cols[:, c, :], ps[:, c, :]).then_inc(x_cols_ready, 1)
            for i in range(PAIRS):
                act.wait_ge(up_mm, i + 1)
                if i >= 2:
                    act.wait_ge(hid_ready, i - 1)
                act.activation(silu[:, i % 2, :].rearrange("p (a n) -> p a n", a=2),
                               ps[:, 4 * (i % 2):4 * (i % 2) + 2, 0:half], ACT.Silu,
                               scale=all_peak[:, 2:3]).then_inc(silued, 1)
            for i in range(PAIRS):
                act.wait_ge(hid_turned, i + 1)
                b = 2 * (i % 2)
                act.copy(hid_cols[:, i % 2, 0:4, :].rearrange("p f n -> p (f n)"), ps[:, b, :]) \
                    .then_inc(hid_cols_ready, 1)
                act.copy(hid_cols[:, i % 2, 4, :], ps[:, b + 1, 0:P]).then_inc(core.act_step, 1)
                act.copy(hid_cols[0:FF2 % P, i % 2, 5, :], ps[0:FF2 % P, b + 1, P:2 * P]) \
                    .then_inc(hid_cols_ready, 1)

        @block.vector
        def _(dve):
            link = InOrder(dve, core.dve_step, dve0)

            def rounded(v, e, out_scale, done=None):
                link(dve.tensor_scalar(e.bitcast(U32), v.bitcast(U32), EXPONENT, None, ALU.bitwise_and))
                link(dve.tensor_scalar(e, e, FP8_LEAST, FP8_ROUND, ALU.max, ALU.mult))
                link(dve.tensor_tensor(v, v, e, ALU.add))
                link(dve.tensor_tensor(v, v, e, ALU.subtract))
                ins = dve.tensor_scalar(v, v, out_scale, None, ALU.mult)
                if done is None:
                    link(ins)
                else:
                    ins.then_inc(done, 1)

            def scales(peak, scale, inv):
                link(dve.tensor_scalar(scale, peak, 1.0 / FP8_MAX, 1e-30, ALU.mult, ALU.max))
                link(dve.reciprocal(inv, scale))

            dve.wait_ge(rows_in, DMA * 2 * FT2)
            dve.wait_ge(wd_in, DMA)
            tiles = [(w_rows[:, k, f, :], D) for k in range(2) for f in range(FT2)]
            tiles += [(wd_rows[:, c, :], FF2) for c in range(DC)]
            for n, (w, _) in enumerate(tiles):
                link(dve.tensor_reduce(peak[:, n:n + 1], w, AXIS.X, ALU.max, apply_absolute_value=True))
            scales(peak[:, :], w_scale[:, :], w_inv[:, :])
            for n, (w, size) in enumerate(tiles):
                link(dve.tensor_scalar(w, w, w_inv[:, n:n + 1], None, ALU.mult))
                rounded(w, unit[:, 0, 0:size], w_scale[:, n:n + 1], w_quant)

            core.ln_vector(dve, link, k_ln)
            dve.wait_ge(core.ln_rows, PAIRS * (k_ln + 1))

            def global_scale(rows_peak, g, known, reduced):
                link(dve.tensor_reduce(g[:, 0:1], rows_peak[:, :], AXIS.X, ALU.max))
                known_ins = dve.tensor_copy(g[:, 3:4], g[:, 0:1])
                known_ins.then_inc(known, 1)
                dve.wait_ge(reduced, 1)
                link(dve.tensor_scalar(g[:, 2:3], g[:, 1:2], 1.0 / GLOBAL_DIV, 1e-30, ALU.mult, ALU.max))
                link(dve.reciprocal(g[:, 3:4], g[:, 2:3]))
                link(dve.tensor_scalar(rows_peak[:, :], rows_peak[:, :], g[:, 3:4], None, ALU.mult))

            link(dve.tensor_reduce(row_peak[:, :], core.xn_rows[:, :, :], AXIS.X, ALU.max,
                                   apply_absolute_value=True))
            global_scale(row_peak, all_peak, peak_known, peak_all)
            scales(row_peak[:, :], row_scale[:, :], row_inv[:, :])
            for i in range(PAIRS):
                link(dve.tensor_scalar(xq[:, i, :], core.xn_rows[:, i, :], all_peak[:, 3:4], row_inv[:, i:i + 1],
                                       ALU.mult, ALU.mult))
                rounded(xq[:, i, :], unit[:, 0, 0:D], row_scale[:, i:i + 1], x_quant)
            for i in range(PAIRS):
                dve.wait_ge(silued, i + 1)
                dve.scalar_tensor_tensor(hid[:, i, :].rearrange("p (a n) -> p a n", a=2),
                                         ps[:, 4 * (i % 2) + 2:4 * (i % 2) + 4, 0:half], all_peak[:, 2:3],
                                         silu[:, i % 2, :].rearrange("p (a n) -> p a n", a=2),
                                         ALU.mult, ALU.mult).then_inc(hid_ready, 1)
                dve.wait_ge(hid_ready, i + 1)
                link(dve.tensor_reduce(row_peak2[:, i:i + 1], hid[:, i, :], AXIS.X, ALU.max,
                                       apply_absolute_value=True))
            global_scale(row_peak2, all_peak2, peak2_known, peak2_all)
            scales(row_peak2[:, :], row_scale2[:, :], row_inv2[:, :])
            for i in range(PAIRS):
                link(dve.tensor_scalar(hid[:, i, :], hid[:, i, :], all_peak2[:, 3:4], row_inv2[:, i:i + 1],
                                       ALU.mult, ALU.mult))
                rounded(hid[:, i, :], unit[:, 1, :], row_scale2[:, i:i + 1], hid_quant)
            dve.wait_ge(out_mm, 1)
            for a in range(2):
                rows = core.x_rows[:, 2 * a:2 * a + 2, :].rearrange("p i d -> p (i d)")
                link(dve.scalar_tensor_tensor(rows, ps[:, 6 + a, :], all_peak2[:, 2:3], rows, ALU.mult, ALU.add))
            core.dve_n = link.n


RT = H * S // P
WS = 4


def full_attention(core):
    nc, dram, ps = core.nc, core.dram, core.psum
    k_ln = core.new_norm()
    dve0, Z = core.dve_n, AHEAD
    ctx = ExitStack()
    with ctx:
        def sb(name, shape, dt=F32):
            return ctx.enter_context(nc.sbuf_tensor("a_" + name, shape, dt))
        w = sb("w", [P, WS, 2 * D])
        head_cols = sb("head_cols", [P, 2, T])
        q_all = sb("q_all", [P, DC, B, H * S])
        q_tile = sb("q_tile", [P, 2, DC, P])
        q_hi = sb("q_hi", [P, 2, DC, P], F32R)
        q_lo = sb("q_lo", [P, 2, DC, P], F32R)
        raw = sb("raw", [P, KT * D])
        t_hi = sb("t_hi", [P, 2, DC, LK], F32R)
        t_lo = sb("t_lo", [P, 2, DC, LK], F32R)
        r_hi = sb("r_hi", [KP, KT, D], F32R)
        r_lo = sb("r_lo", [KP, KT, D], F32R)
        neg_max = sb("neg_max", [P, 2])
        sums = sb("sums", [P, 2])
        inv = sb("inv", [P, 2])
        prob = sb("prob", [P, 2, LK])
        p_hi = sb("p_hi", [KP, KT, P], F32R)
        p_lo = sb("p_lo", [KP, KT, P], F32R)
        mixed = sb("mixed", [P, 2, D])
        zero = sb("zero", [1, 512])
        q_head = head_cols[:, :, 0:TOK]
        v_head = head_cols
        sem = core.sem
        w_in = [sem(f"a_w_in{s}") for s in range(WS)]
        names = ("raw_in", "t_hi_ready", "t_lo_ready", "r_hi_ready", "r_lo_ready", "head_mm", "head_sb",
                 "fold_mm", "fold_sb", "q_staged", "q_hi_ready", "q_lo_ready", "score_mm", "maxed", "exped", "turned",
                 "p_hi_ready", "p_lo_ready", "mix_mm", "mix_sb", "mix_turned", "mix_kept", "v_mm", "v_sb", "out_mm")
        (raw_in, t_hi_ready, t_lo_ready, r_hi_ready, r_lo_ready, head_mm, head_sb,
         fold_mm, fold_sb, q_staged, q_hi_ready, q_lo_ready, score_mm, maxed, exped, turned,
         p_hi_ready, p_lo_ready, mix_mm, mix_sb, mix_turned, mix_kept, v_mm, v_sb, out_mm) = (
            sem("a_" + n) for n in names)
        turns = H // WS
        scale = 1.0 / float(np.sqrt(HD))
        raw_t = raw[:, 0:DC * LK].rearrange("p (c k) -> p c k", c=DC)
        raw_r = raw[0:KP, :].rearrange("p (t d) -> p t d", t=KT)

        def query_tile(i, x):
            return q_all[:, :, bass.ds(2 * i + x // RT, 1), x % RT * P:(x % RT + 1) * P] \
                .rearrange("p c b n -> p c (b n)")
        block = ctx.enter_context(nc.Block())

        @block.sync
        def _(sp):
            def weights(n, s):
                sp.dma_start(w[:, s, :], dram["a_w"][n]).then_inc(w_in[s], DMA)

            def context_turned(b):
                sp.wait_ge(r_hi_ready, Z + 3 * b)
                sp.wait_ge(r_lo_ready, Z + 3 * b)
                sp.dma_start(raw_t, dram["ctx_t"][b]).then_inc(raw_in, DMA)

            def context_rows(b):
                sp.wait_ge(t_hi_ready, Z + 2 * (b + 1))
                sp.wait_ge(t_lo_ready, Z + 2 * (b + 1))
                sp.dma_start(raw_r, dram["ctx_r"][b]).then_inc(raw_in, DMA)
            for s in range(WS):
                weights(s, s)
            context_turned(0)
            context_rows(0)
            with sp.Fori(1, turns) as i:
                for s in range(WS):
                    sp.wait_ge(fold_mm, Z + (i - 1) * WS + s + 1)
                    weights(i * WS + s, s)
            with sp.Fori(1, B) as b:
                context_turned(b)
                context_rows(b)
            for s in range(WS):
                weights(H + s, s)
            with sp.Fori(1, turns) as i:
                for s in range(WS):
                    sp.wait_ge(out_mm, Z + (i - 1) * WS + s + 1)
                    weights((turns + i) * WS + s, s)

        @block.gpsimd
        def _(pool):
            core.ln_pool(pool, k_ln)
            pool.sem_inc(q_staged, Z)
            pool.wait_ge(fold_sb, Z + H)
            with pool.Fori(0, PAIRS) as i:
                for x in range(2 * RT):
                    n = i * 2 * RT + x
                    pool.wait_ge(q_lo_ready, Z + n - 1)
                    pool.tensor_copy(q_tile[:, x % 2, :, :], query_tile(i, x)).then_inc(q_staged, 1)

        @block.tensor
        def _(pe):
            for x in (head_mm, fold_mm, score_mm, turned, mix_mm, mix_turned, v_mm, out_mm):
                pe.sem_inc(x, Z)
            core.ln_tensor(pe, k_ln)
            pe.wait_ge(core.ln_cols, core.cols_ready(k_ln))

            def head(n, i, s):
                pe.wait_ge(w_in[s], DMA * (i + 1))
                pe.wait_ge(head_sb, Z + n - 1)
                for c in range(DC):
                    ins = pe.matmul(packed(ps[:, 2 + s % 2, 0:TOK]), w[:, s, c * P:(c + 1) * P], core.tok(c),
                                    start=(c == 0), stop=(c == DC - 1))
                ins.then_inc(head_mm, 1)

            def fold(n, s):
                pe.wait_ge(head_sb, Z + n + 1)
                pe.wait_ge(fold_sb, Z + n - 1)
                for c in range(DC):
                    ins = pe.matmul(ps[:, 4 + 2 * (s % 2) + c, 0:TOK], w[:, s, D + c * P:D + (c + 1) * P],
                                    q_head[:, s % 2, :], start=True, stop=True)
                ins.then_inc(fold_mm, 1)
            with pe.Fori(0, turns) as i:
                for s in range(WS):
                    head(i * WS + s, i, s)
                    if s:
                        fold(i * WS + s - 1, s - 1)
                fold(i * WS + WS - 1, WS - 1)

            def score_part(n, turn, x, k):
                b = x // RT
                if k == 0:
                    pe.wait_ge(exped, Z + n - 1)
                    pe.wait_ge(q_lo_ready, Z + n + 1)
                    if x % RT == 0:
                        pe.wait_ge(t_lo_ready, Z + 2 * (2 * turn + b + 1))
                products = [(q, t, c) for q, t in ((q_hi, t_hi), (q_hi, t_lo), (q_lo, t_hi)) for c in range(DC)]
                for m, (q, t, c) in enumerate(products):
                    ins = pe.matmul(ps[:, 3 * (x % 2) + k, 0:KN], q[:, x % 2, c, :],
                                    t[:, b, c, k * KN:(k + 1) * KN],
                                    start=(m == 0), stop=(m == len(products) - 1))
                if k == 2:
                    ins.then_inc(score_mm, 1)

            def turn_mixed(n, x):
                pe.wait_ge(mix_sb, Z + n + 1)
                for c in range(DC):
                    ins = pe.transpose(ps[:, 7, D + c * P:D + (c + 1) * P], mixed[:, x % 2, c * P:(c + 1) * P],
                                       core.ident[:, :])
                ins.then_inc(mix_turned, 1)

            def mix_part(n, i, x, u):
                if u == 0:
                    pe.wait_ge(mix_kept, Z + n)
                pe.wait_ge(p_lo_ready, Z + 3 * n + u + 1)
                if x % RT == 0:
                    pe.wait_ge(r_lo_ready, Z + 3 * (2 * i + x // RT) + u + 1)
                for t in range(4 * u, 4 * u + 4):
                    for m, (p, v) in enumerate(((p_hi, r_hi), (p_hi, r_lo), (p_lo, r_hi))):
                        ins = pe.matmul(ps[:, 7, 0:D], p[:, t, :], v[:, t, :],
                                        start=(t == 0 and m == 0), stop=(t == KT - 1 and m == 2))
                ins.then_inc(mix_mm, 1)

            def attention(i, last):
                for x in range(2 * RT):
                    n = i * 2 * RT + x
                    pe.wait_ge(exped, Z + n + 1)
                    for u in range(3):
                        if x > 0:
                            mix_part(n - 1, i, x - 1, u)
                            if u == 2:
                                turn_mixed(n - 1, x - 1)
                        pe.wait_ge(p_hi_ready, Z + 3 * n + u)
                        pe.wait_ge(p_lo_ready, Z + 3 * n + u)
                        for y in range(4):
                            t = 4 * u + y
                            ins = pe.transpose(ps[0:KP, 6, y * P:(y + 1) * P],
                                               prob[:, x % 2, t * KP:(t + 1) * KP], core.ident[:, :])
                        ins.then_inc(turned, 1)
                        if x < 2 * RT - 2:
                            score_part(n + 2, i, x + 2, u)
                        elif not last:
                            score_part(n + 2, i + 1, x + 2 - 2 * RT, u)
                for u in range(3):
                    mix_part(i * 2 * RT + 2 * RT - 1, i, 2 * RT - 1, u)
                turn_mixed(i * 2 * RT + 2 * RT - 1, 2 * RT - 1)

            for x in range(2):
                for k in range(3):
                    score_part(x, 0, x, k)
            with pe.Fori(0, PAIRS - 1) as i:
                attention(i, last=False)
            attention(PAIRS - 1, last=True)

            for a in range(2):
                pe.matmul(ps[:, a, :], zero[0:1, 0:P], zero[0:1, :], start=True, stop=True,
                          skip_group_check=True)
            pe.wait_ge(mix_kept, Z + B * RT)

            def value(n, i, s):
                pe.wait_ge(w_in[s], DMA * (turns + i + 1))
                pe.wait_ge(v_sb, Z + n - 1)
                for c in range(DC):
                    ins = pe.matmul(packed(ps[:, 2 + s % 2, 0:TOK]), w[:, s, c * P:(c + 1) * P],
                                    q_all[:, c, :, bass.ds(n * S, S)], start=(c == 0), stop=(c == DC - 1))
                ins.then_inc(v_mm, 1)

            def output(n, s):
                pe.wait_ge(v_sb, Z + n + 1)
                for t in range(PAIRS):
                    ins = pe.matmul(ps[:, t // 2, (t % 2) * D:(t % 2 + 1) * D],
                                    v_head[:, s % 2, t * P:(t + 1) * P], w[:, s, D:2 * D],
                                    start=False, stop=False, skip_group_check=True)
                ins.then_inc(out_mm, 1)
            with pe.Fori(0, turns) as i:
                for s in range(WS):
                    value(i * WS + s, i, s)
                    if s:
                        output(i * WS + s - 1, s - 1)
                output(i * WS + WS - 1, WS - 1)

        @block.scalar
        def _(act):
            for x in (head_sb, exped, q_hi_ready, t_hi_ready, r_hi_ready, p_hi_ready, mix_kept, v_sb):
                act.sem_inc(x, Z)

            def split_turned(b, s, c):
                act.wait_ge(raw_in, DMA * (2 * b + 1))
                act.wait_ge(score_mm, Z + RT * (b - 1))
                act.copy(t_hi[:, s, c, :], raw_t[:, c, :]).then_inc(t_hi_ready, 1)

            def split_rows(b, u):
                act.wait_ge(raw_in, DMA * (2 * b + 2))
                act.wait_ge(mix_mm, Z + 3 * (RT * b - 1) + u + 1)
                act.copy(r_hi[:, 4 * u:4 * u + 4, :], raw_r[:, 4 * u:4 * u + 4, :]).then_inc(r_hi_ready, 1)
            core.ln_scalar(act, k_ln)
            for c in range(DC):
                split_turned(0, 0, c)
            for u in range(3):
                split_rows(0, u)
            with act.Fori(0, turns) as i:
                for s in range(WS):
                    n = i * WS + s
                    act.wait_ge(head_mm, Z + n + 1)
                    act.wait_ge(fold_mm, Z + n - 1)
                    act.copy(q_head[:, s % 2, :], ps[:, 2 + s % 2, 0:TOK]).then_inc(head_sb, 1)

            def split_queries(n, x):
                act.wait_ge(q_staged, Z + n + 1)
                act.wait_ge(score_mm, Z + n - 1)
                act.copy(q_hi[:, x % 2, :, :], q_tile[:, x % 2, :, :]).then_inc(q_hi_ready, 1)

            def exp(n, x):
                act.wait_ge(maxed, Z + n + 1)
                act.wait_ge(turned, Z + 3 * (n - 1))
                act.activation(prob[:, x % 2, :].rearrange("p (k n) -> p k n", k=3),
                               ps[:, 3 * (x % 2):3 * (x % 2) + 3, 0:KN], ACT.Exp,
                               bias=neg_max[:, x % 2:x % 2 + 1],
                               accum_out=sums[:, x % 2:x % 2 + 1]).then_inc(exped, 1)

            def keep_mixed(i, x, n):
                act.wait_ge(mix_turned, Z + n + 1)
                act.copy(query_tile(i, x), ps[:, 7, D:2 * D].rearrange("p (c n) -> p c n", c=DC)) \
                    .then_inc(mix_kept, 1)

            def attention(i, last):
                for x in range(2 * RT):
                    n = i * 2 * RT + x
                    b, r = x // RT, x % RT
                    for u in range(3):
                        if u == 2 and x > 0:
                            keep_mixed(i, x - 1, n - 1)
                        act.wait_ge(turned, Z + 3 * n + u + 1)
                        act.wait_ge(mix_mm, Z + 3 * n + u - 2)
                        act.copy(p_hi[:, 4 * u:4 * u + 4, :].rearrange("p t n -> p (t n)"),
                                 ps[0:KP, 6, :]).then_inc(p_hi_ready, 1)
                        if u == 0 and not (last and x == 2 * RT - 1):
                            exp(n + 1, x + 1)
                        if u == 1 and not (last and x + 3 >= 2 * RT):
                            split_queries(n + 3, x + 3)
                        if r == 0 and x > 0:
                            split_rows(2 * i + b, u)
                    if r in (2, 3) and not (last and b == 1):
                        split_turned(2 * i + b + 1, 1 - b, r - 2)
                keep_mixed(i, 2 * RT - 1, i * 2 * RT + 2 * RT - 1)
                if not last:
                    for u in range(3):
                        split_rows(2 * i + 2, u)
            for x in range(2):
                split_queries(x, x)
            exp(0, 0)
            split_queries(2, 2)
            with act.Fori(0, PAIRS - 1) as i:
                attention(i, last=False)
            attention(PAIRS - 1, last=True)
            with act.Fori(0, turns) as i:
                for s in range(WS):
                    n = i * WS + s
                    act.wait_ge(v_mm, Z + n + 1)
                    act.wait_ge(out_mm, Z + n - 1)
                    act.copy(unpad(v_head[:, s % 2, :]), packed(ps[:, 2 + s % 2, 0:TOK])).then_inc(v_sb, 1)

        @block.vector
        def _(dve):
            link = InOrder(dve, core.dve_step, dve0)
            for x in (fold_sb, maxed, q_lo_ready, t_lo_ready, r_lo_ready, p_lo_ready, mix_sb):
                dve.sem_inc(x, Z)
            core.ln_vector(dve, link, k_ln)
            link(dve.memset(zero[:, :], 0.0))
            link(dve.memset(head_cols[:, :, :], 0.0))

            def split_turned(b, s, c):
                dve.wait_ge(t_hi_ready, Z + 2 * b + c + 1)
                dve.tensor_tensor(t_lo[:, s, c, :], raw_t[:, c, :], t_hi[:, s, c, :].bitcast(F32),
                                  ALU.subtract).then_inc(t_lo_ready, 1)

            def split_rows(b, u):
                dve.wait_ge(r_hi_ready, Z + 3 * b + u + 1)
                dve.tensor_tensor(r_lo[:, 4 * u:4 * u + 4, :], raw_r[:, 4 * u:4 * u + 4, :],
                                  r_hi[:, 4 * u:4 * u + 4, :].bitcast(F32), ALU.subtract).then_inc(r_lo_ready, 1)
            for c in range(DC):
                split_turned(0, 0, c)
            for u in range(3):
                split_rows(0, u)
            with dve.Fori(0, turns) as i:
                for s in range(WS):
                    n = i * WS + s
                    dve.wait_ge(fold_mm, Z + n + 1)
                    for c in range(DC):
                        ins = dve.tensor_scalar(q_all[:, c, :, bass.ds(n * S, S)],
                                                packed(ps[:, 4 + 2 * (s % 2) + c, 0:TOK]), scale, None, ALU.mult)
                    ins.then_inc(fold_sb, 1)

            def split_queries(n, x):
                dve.wait_ge(q_hi_ready, Z + n + 1)
                dve.tensor_tensor(q_lo[:, x % 2, :, :], q_tile[:, x % 2, :, :], q_hi[:, x % 2, :, :].bitcast(F32),
                                  ALU.subtract).then_inc(q_lo_ready, 1)

            def row_max(n, x):
                dve.wait_ge(score_mm, Z + n + 1)
                dve.wait_ge(exped, Z + n - 1)
                dve.tensor_reduce(neg_max[:, x % 2:x % 2 + 1], ps[:, 3 * (x % 2):3 * (x % 2) + 3, 0:KN],
                                  AXIS.XY, ALU.max, negate=True).then_inc(maxed, 1)

            def keep(n, x):
                dve.wait_ge(mix_mm, Z + 3 * n + 3)
                dve.tensor_scalar(mixed[:, x % 2, :], ps[:, 7, 0:D], inv[:, x % 2:x % 2 + 1], None,
                                  ALU.mult).then_inc(mix_sb, 1)

            def attention(i, last):
                for x in range(2 * RT):
                    n = i * 2 * RT + x
                    b, r = x // RT, x % RT
                    dve.wait_ge(exped, Z + n + 1)
                    link(dve.reciprocal(inv[:, x % 2:x % 2 + 1], sums[:, x % 2:x % 2 + 1]))
                    if not (last and x == 2 * RT - 1):
                        row_max(n + 1, x + 1)
                    for u in range(3):
                        if u == 2 and x > 0:
                            keep(n - 1, x - 1)
                        dve.wait_ge(p_hi_ready, Z + 3 * n + u + 1)
                        p4 = slice(4 * u, 4 * u + 4)
                        dve.tensor_tensor(p_lo[:, p4, :].rearrange("p t n -> p (t n)"), ps[0:KP, 6, :],
                                          p_hi[:, p4, :].rearrange("p t n -> p (t n)").bitcast(F32),
                                          ALU.subtract).then_inc(p_lo_ready, 1)
                        if u == 1 and not (last and x + 3 >= 2 * RT):
                            split_queries(n + 3, x + 3)
                        if r == 0 and x > 0:
                            split_rows(2 * i + b, u)
                    if r in (2, 3) and not (last and b == 1):
                        split_turned(2 * i + b + 1, 1 - b, r - 2)
                keep(i * 2 * RT + 2 * RT - 1, 2 * RT - 1)
                if not last:
                    for u in range(3):
                        split_rows(2 * i + 2, u)
            for x in range(2):
                split_queries(x, x)
            row_max(0, 0)
            split_queries(2, 2)
            first = link.n
            with dve.Fori(0, PAIRS - 1) as i:
                link.loop(i, first, 2 * RT)
                attention(i, last=False)
            link.end(first, 2 * RT, PAIRS - 1)
            attention(PAIRS - 1, last=True)
            dve.wait_ge(out_mm, Z + H)
            for a in range(2):
                rows = core.x_rows[:, 2 * a:2 * a + 2, :].rearrange("p i d -> p (i d)")
                link(dve.tensor_tensor(rows, rows, ps[:, a, :], ALU.add))
            core.dve_n = link.n


PACK = 4 * P + D + P
SLOTS = 4


def moe(core, tag, experts, top_k, tiles, shared_gate, per_owner):
    nc, dram, ps = core.nc, core.dram, core.psum
    k_ln = core.new_norm()
    dve0 = core.dve_n
    ne = experts + 1
    nl = experts + int(shared_gate)
    ctx = ExitStack()
    with ctx:
        def sb(name, shape, dt=F32):
            return ctx.enter_context(nc.sbuf_tensor(tag + name, shape, dt))
        w_gate = sb("gate", [P, DC, nl])
        w = sb("w", [P, SLOTS, PACK])
        before = sb("before", [P, experts, experts])
        zero = sb("zero", [1, 512])
        gate_silu = sb("gate_silu", [P, 2, TOK])
        prod = sb("prod", [P, 2, TOK])
        hid = sb("hid", [P, 2, T])
        x_hi = sb("x_hi", [P, DC, T], F32R)
        x_lo = sb("x_lo", [P, DC, T], F32R)
        w_hi = sb("w_hi", [P, SLOTS, PACK], F32R)
        w_lo = sb("w_lo", [P, SLOTS, 4 * P + D], F32R)
        hid_hi = sb("hid_hi", [P, 2, T], F32R)
        hid_lo = sb("hid_lo", [P, 2, T], F32R)
        comb_hi = sb("comb_hi", [ne, T], F32R)
        comb_lo = sb("comb_lo", [ne, T], F32R)
        top = sb("top", [P, PAIRS])
        logit = sb("logit", [P, PAIRS, nl])
        prob = sb("prob", [P, PAIRS, experts])
        sig = sb("sig", [P, PAIRS])
        gt = sb("gt", [P, PAIRS, experts * experts])
        eq = sb("eq", [P, PAIRS, experts * experts])
        rank = sb("rank", [P, PAIRS, experts])
        total = sb("total", [P, PAIRS])
        combine = sb("combine", [P, PAIRS, ne])
        sem = core.sem
        gate_in = sem(tag + "gate_in")
        w_in = [sem(f"{tag}w_in{s}") for s in range(SLOTS)]
        (gate_mm, maxed, exped, combined, comb_turned, comb_hi_ready, comb_lo_ready, x_hi_ready, x_lo_ready,
         w_hi_ready, w_lo_ready, up_mm, silued, product, scaled, hid_hi_ready, hid_lo_ready, owner_mm,
         down_mm, cleared) = (sem(tag + n) for n in (
            "gate_mm", "maxed", "exped", "combined", "comb_turned", "comb_hi_ready", "comb_lo_ready",
            "x_hi_ready", "x_lo_ready", "w_hi_ready", "w_lo_ready", "up_mm", "silued", "product", "scaled",
            "hid_hi_ready", "hid_lo_ready", "owner_mm", "down_mm", "cleared"))

        def tok(x, c):
            return unpad(x[:, c, :])

        def split(x, y):
            (x_h, x_l), (y_h, y_l) = x, y
            return (x_h, y_h), (x_h, y_l), (x_l, y_h)
        turns = tiles // SLOTS
        block = ctx.enter_context(nc.Block())

        @block.sync
        def _(sp):
            sp.dma_start(w_gate[:, :, :], dram[tag + "gate"]).then_inc(gate_in, DMA)
            sp.dma_start(before[:, :, :], dram[tag + "before"]).then_inc(gate_in, DMA)
            for s in range(SLOTS):
                sp.dma_start(w[:, s, :], dram[tag + "pack"][s]).then_inc(w_in[s], DMA)
            with sp.Fori(1, turns) as i:
                for s in range(SLOTS):
                    sp.wait_ge(w_hi_ready, (i - 1) * SLOTS + s + 1)
                    sp.wait_ge(w_lo_ready, (i - 1) * SLOTS + s + 1)
                    sp.dma_start(w[:, s, :], dram[tag + "pack"][i * SLOTS + s]).then_inc(w_in[s], DMA)

        @block.gpsimd
        def _(pool):
            core.ln_pool(pool, k_ln)

        @block.tensor
        def _(pe):
            core.ln_tensor(pe, k_ln)
            pe.wait_ge(core.ln_cols, core.cols_ready(k_ln))
            pe.wait_ge(gate_in, 2 * DMA)
            for t in range(PAIRS):
                for c in range(DC):
                    ins = pe.matmul(ps[:, 7, t * nl:(t + 1) * nl], core.xn_cols[:, c, t * P:(t + 1) * P],
                                    w_gate[:, c, :], start=(c == 0), stop=(c == DC - 1))
            ins.then_inc(gate_mm, 1)

            def up(n, s, first=False):
                pe.wait_ge(w_lo_ready, n + 1)
                if not first:
                    pe.wait_ge(silued, n - 1)
                    pe.wait_ge(product, n - 1)
                for k in range(2):
                    for c in range(DC):
                        at = slice((2 * k + c) * P, (2 * k + c + 1) * P)
                        for m, (wt, xt) in enumerate(split((w_hi, w_lo), (x_hi, x_lo))):
                            ins = pe.matmul(packed(ps[:, 2 + 2 * k + s % 2, 0:TOK]), wt[:, s, at], tok(xt, c),
                                            start=(c == 0 and m == 0), stop=(c == DC - 1 and m == 2))
                ins.then_inc(up_mm, 1)

            def owner(n, s, first=False):
                if not first:
                    pe.wait_ge(scaled, n)
                for m, part in enumerate((comb_hi, comb_lo)):
                    ins = pe.matmul(packed(ps[:, 6, 0:TOK]), w_hi[0:ne, s, 4 * P + D:], unpad(part[:, :]),
                                    start=(m == 0), stop=(m == 1))
                ins.then_inc(owner_mm, 1)

            def down(n, s):
                pe.wait_ge(hid_lo_ready, n + 1)
                for t in range(PAIRS):
                    for h, wt in split((hid_hi, hid_lo), (w_hi, w_lo)):
                        ins = pe.matmul(ps[:, t // 2, (t % 2) * D:(t % 2 + 1) * D],
                                        h[:, s % 2, t * P:(t + 1) * P], wt[:, s, 4 * P:4 * P + D],
                                        start=False, stop=False, skip_group_check=True)
                ins.then_inc(down_mm, 1)

            pe.wait_ge(x_lo_ready, DC)
            up(0, 0, first=True)
            up(1, 1, first=True)
            pe.wait_ge(cleared, 1)
            for a in range(2):
                pe.matmul(ps[:, a, :], zero[0:1, 0:P], zero[0:1, :], start=True, stop=True,
                          skip_group_check=True)
            pe.wait_ge(combined, 1)
            for t in range(PAIRS):
                ins = pe.transpose(ps[0:ne, 7, t * P:(t + 1) * P], combine[:, t, :], core.ident[:, :])
            ins.then_inc(comb_turned, 1)
            pe.wait_ge(comb_lo_ready, 1)
            owner(0, 0, first=True)
            for n in range(1, SLOTS):
                if n >= 2:
                    up(n, n)
                if n % per_owner == 0:
                    owner(n, n)
                down(n - 1, n - 1)
            with pe.Fori(1, turns) as i:
                for s in range(SLOTS):
                    n = i * SLOTS + s
                    up(n, s)
                    if s % per_owner == 0:
                        owner(n, s)
                    down(n - 1, (s - 1) % SLOTS)
            down(tiles - 1, SLOTS - 1)

        @block.scalar
        def _(act):
            core.ln_scalar(act, k_ln)
            for c in range(DC):
                act.wait_ge(core.ln_cols, core.cols_ready(k_ln) - DC + c + 1)
                act.copy(x_hi[:, c, :], core.xn_cols[:, c, :]).then_inc(x_hi_ready, 1)

            def split_weights(n, i, s):
                act.wait_ge(w_in[s], DMA * (i + 1))
                if not (isinstance(n, int) and n < SLOTS):
                    act.wait_ge(down_mm, n - SLOTS + 1)
                act.copy(w_hi[:, s, :], w[:, s, :]).then_inc(w_hi_ready, 1)
            split_weights(0, 0, 0)
            split_weights(1, 0, 1)
            act.wait_ge(maxed, 1)
            act.activation(prob[:, :, :], prob[:, :, :], ACT.Exp).then_inc(exped, 1)
            if shared_gate:
                act.activation(sig[:, :], logit[:, :, experts], ACT.Sigmoid).then_inc(exped, 1)
            act.wait_ge(comb_turned, 1)
            act.copy(comb_hi[:, :], ps[0:ne, 7, :]).then_inc(comb_hi_ready, 1)

            def silu(n, s, first=False):
                act.wait_ge(up_mm, n + 1)
                if not first:
                    act.wait_ge(product, n - 1)
                act.activation(gate_silu[:, s % 2, :], ps[:, 2 + s % 2, 0:TOK], ACT.Silu).then_inc(silued, 1)

            def hidden(n, s, first=False):
                act.wait_ge(scaled, n + 1)
                if not first:
                    act.wait_ge(down_mm, n - 1)
                act.copy(hid_hi[:, s % 2, :], hid[:, s % 2, :]).then_inc(hid_hi_ready, 1)
            for n in range(SLOTS):
                silu(n, n, first=(n < 2))
                split_weights(n + 2, (n + 2) // SLOTS, (n + 2) % SLOTS)
                hidden(n, n, first=(n < 2))
            with act.Fori(1, turns - 1) as i:
                for s in range(SLOTS):
                    n = i * SLOTS + s
                    silu(n, s)
                    split_weights(n + 2, i + (s + 2) // SLOTS, (s + 2) % SLOTS)
                    hidden(n, s)
            for n in range(tiles - SLOTS, tiles):
                silu(n, n % SLOTS)
                if n + 2 < tiles:
                    split_weights(n + 2, (n + 2) // SLOTS, (n + 2) % SLOTS)
                hidden(n, n % SLOTS)

        @block.vector
        def _(dve):
            link = InOrder(dve, core.dve_step, dve0)
            dve.memset(zero[:, :], 0.0).then_inc(cleared, 1)
            link(dve.memset(hid[:, :, :], 0.0))
            core.ln_vector(dve, link, k_ln)

            def split_weights(n, s):
                dve.wait_ge(w_hi_ready, n + 1)
                dve.tensor_tensor(w_lo[:, s, :], w[:, s, 0:4 * P + D], w_hi[:, s, 0:4 * P + D].bitcast(F32),
                                  ALU.subtract).then_inc(w_lo_ready, 1)
            for c in range(DC):
                dve.wait_ge(x_hi_ready, c + 1)
                dve.tensor_tensor(x_lo[:, c, :], core.xn_cols[:, c, :], x_hi[:, c, :].bitcast(F32),
                                  ALU.subtract).then_inc(x_lo_ready, 1)
            split_weights(0, 0)
            split_weights(1, 1)
            dve.wait_ge(gate_mm, 1)
            link(dve.tensor_copy(logit[:, :, :].rearrange("p t e -> p (t e)"), ps[:, 7, 0:PAIRS * nl]))
            link(dve.tensor_reduce(top[:, :], logit[:, :, 0:experts], AXIS.X, ALU.max))
            dve.tensor_tensor(prob[:, :, :], logit[:, :, 0:experts],
                              top[:, :].unsqueeze(2).to_broadcast([P, PAIRS, experts]),
                              ALU.subtract).then_inc(maxed, 1)
            dve.wait_ge(exped, 1 + int(shared_gate))
            mine = prob[:, :, :].unsqueeze(3).to_broadcast([P, PAIRS, experts, experts])
            other = prob[:, :, :].unsqueeze(2).to_broadcast([P, PAIRS, experts, experts])
            first_of_two = before[:, :, :].unsqueeze(1).to_broadcast([P, PAIRS, experts, experts])
            g4 = gt[:, :, :].rearrange("p t (a b) -> p t a b", b=experts)
            e4 = eq[:, :, :].rearrange("p t (a b) -> p t a b", b=experts)
            link(dve.tensor_tensor(g4, other, mine, ALU.is_gt))
            link(dve.tensor_tensor(e4, other, mine, ALU.is_equal))
            link(dve.tensor_tensor(e4, e4, first_of_two, ALU.mult))
            link(dve.tensor_tensor(g4, g4, e4, ALU.add))
            link(dve.tensor_reduce(rank[:, :, :], g4, AXIS.X, ALU.add))
            link(dve.tensor_scalar(rank[:, :, :], rank[:, :, :], float(top_k), None, ALU.is_lt))
            link(dve.tensor_tensor(prob[:, :, :], prob[:, :, :], rank[:, :, :], ALU.mult))
            link(dve.tensor_reduce(total[:, :], prob[:, :, :], AXIS.X, ALU.add))
            link(dve.reciprocal(total[:, :], total[:, :]))
            if shared_gate:
                link(dve.tensor_copy(combine[:, :, experts], sig[:, :]))
            else:
                link(dve.memset(combine[:, :, experts], 1.0))
            dve.tensor_tensor(combine[:, :, 0:experts], prob[:, :, :],
                              total[:, :].unsqueeze(2).to_broadcast([P, PAIRS, experts]),
                              ALU.mult).then_inc(combined, 1)
            dve.wait_ge(comb_hi_ready, 1)
            dve.tensor_tensor(comb_lo[:, :], ps[0:ne, 7, :], comb_hi[:, :].bitcast(F32),
                              ALU.subtract).then_inc(comb_lo_ready, 1)

            def gated(n, i, s, more=True):
                dve.wait_ge(silued, n + 1)
                dve.tensor_tensor(prod[:, s % 2, :], gate_silu[:, s % 2, :], ps[:, 4 + s % 2, 0:TOK],
                                  ALU.mult).then_inc(product, 1)
                dve.wait_ge(product, n + 1)
                dve.wait_ge(owner_mm, n + 1 if per_owner == 1 else i + 1)
                dve.tensor_tensor(unpad(hid[:, s % 2, :]), packed(prod[:, s % 2, :]), packed(ps[:, 6, 0:TOK]),
                                  ALU.mult).then_inc(scaled, 1)
                if more:
                    split_weights(n + 2, (s + 2) % SLOTS)
                dve.wait_ge(hid_hi_ready, n + 1)
                dve.tensor_tensor(hid_lo[:, s % 2, :], hid[:, s % 2, :], hid_hi[:, s % 2, :].bitcast(F32),
                                  ALU.subtract).then_inc(hid_lo_ready, 1)
            for n in range(SLOTS):
                gated(n, 0, n)
            with dve.Fori(1, turns - 1) as i:
                for s in range(SLOTS):
                    gated(i * SLOTS + s, i, s)
            for n in range(tiles - SLOTS, tiles):
                gated(n, n // SLOTS, n % SLOTS, more=(n + 2 < tiles))
            dve.wait_ge(down_mm, tiles)
            for a in range(2):
                rows = core.x_rows[:, 2 * a:2 * a + 2, :].rearrange("p i d -> p (i d)")
                link(dve.tensor_tensor(rows, rows, ps[:, a, :], ALU.add))
            core.dve_n = link.n


E1, K1, I1, SI1 = 16, 4, 176, 704
TILES1 = -(-(E1 * I1 + SI1) // P)
E3, K3, I3 = 8, 2, 512
TILES3 = (E3 + 1) * I3 // P


def moe_1(core):
    moe(core, "m1_", E1, K1, TILES1, shared_gate=True, per_owner=1)


def moe_3(core):
    moe(core, "m3_", E3, K3, TILES3, shared_gate=False, per_owner=SLOTS)


def chunks(w, p=P):
    return w.reshape(w.shape[0] // p, p, w.shape[1]).transpose(1, 0, 2)


def rope_tables(length):
    half = R // 2
    freq = (1.0 / 10000.0 ** (np.arange(half, dtype=np.float32) / np.float32(half))).astype(np.float32)
    ang = np.arange(length, dtype=np.float32)[:, None] * freq
    cos, sin = np.cos(ang), np.sin(ang)
    return (np.concatenate([cos, cos], 1).astype(np.float32),
            np.concatenate([-sin, sin], 1).astype(np.float32))


def layouts(a):
    out = {"x": a["x"], "c_ident": np.eye(P, dtype=np.float32)}
    seg = a["itok_BxS_0_1023"].reshape(B, GROUPS, GQ)
    out["seg_k"] = np.repeat(seg.transpose(2, 0, 1).reshape(GQ, B * GROUPS), WIN, axis=0)
    out["seg_r"] = np.tile(seg.transpose(2, 0, 1).reshape(GQ, B * GROUPS), (HH, 1))
    win = np.arange(WIN, dtype=np.float32) - (WIN - 1)
    out["c_win_k"] = np.tile(win, GQ)[:, None]
    out["c_seq_row"] = np.tile(np.repeat(np.arange(B, dtype=np.float32) * LK, GROUPS), (GR, 1))
    out["c_win_r"] = np.tile(win, (ROW0, 1))
    own = np.tile(np.arange(GQ), HH)[:, None] == np.repeat(np.arange(GQ), WIN)[None, :]
    out["c_diag"] = np.where(own, 0.0, NEG).astype(np.float32)
    cos, sin = rope_tables(LK)
    ctx = a["ctx_2048"]
    table = np.broadcast_to(np.concatenate([sin, cos], 1)[None], (B, LK, 2 * R))
    out["ctx_rope"] = np.concatenate([ctx, table], 2).reshape(B * LK, D + 2 * R)
    out["c_rope_q"] = np.tile(np.stack([cos[:S].T, sin[:S].T], 1), (2, 1, 1))

    def swap(w):
        w = w.reshape(w.shape[0], -1, 2, R // 2)
        return w[:, :, ::-1, :].reshape(w.shape[0], -1)
    out["w_kvc"] = chunks(a["L0_xattn_W_kvc"])
    out["w_kvc_t"] = a["L0_xattn_W_kvc"].T
    out["w_kr2"] = np.concatenate([a["L0_xattn_W_kr"], swap(a["L0_xattn_W_kr"])], 1)
    out["w_dq"] = chunks(a["L0_xattn_W_dq"])
    out["w_uq_t"] = a["L0_xattn_W_uq"].reshape(QC, H, HD).transpose(2, 1, 0)
    out["w_uk_t"] = a["L0_xattn_W_uk"].reshape(KVC, H, HD).transpose(2, 1, 0)
    out["w_uv_t"] = a["L0_xattn_W_uv"].reshape(KVC, H, HD).transpose(2, 1, 0)
    out["w_qr"] = np.stack([a["L0_xattn_W_qr"], swap(a["L0_xattn_W_qr"])], 1)
    out["w_o"] = a["L0_xattn_W_o"].reshape(H, HD, D).transpose(1, 0, 2)
    out["f_w1"] = chunks(a["L0_ffn_W1"].T)
    out["f_w2"] = chunks(a["L0_ffn_W2"].T)
    out["ctx_r"] = ctx.reshape(B, KP, KT, D)
    out["ctx_t"] = ctx.reshape(B, KP, KT, DC, P).transpose(0, 4, 3, 2, 1).reshape(B, P, DC, LK)
    out["c_mask"] = a["mask_BxS2_bk0"].reshape(B, KP, KT).transpose(0, 2, 1).reshape(B, LK).view(np.int32)
    out["c_mask2"] = a["mask_BxS2_ff1"].reshape(B, KP, KT).transpose(1, 0, 2)
    out["c_w_k"] = chunks(a["L2_xattn_Wk"].T)
    out["c_w_v"] = chunks(a["L2_xattn_Wv"].T)
    out["c_b_k"] = a["L2_xattn_bk"].reshape(2, P).T

    def block_diagonal(w):
        out = np.zeros((8, HD2, 8, FD2), np.float32)
        out[np.arange(8), :, np.arange(8), :] = w.T
        return out.reshape(P, FG)
    out["c_w_kf"] = block_diagonal(a["L2_xattn_Wkf"])
    out["l_w_q"] = chunks(a["L2_xattn_Wq"].T)
    out["l_w_o"] = chunks(a["L2_xattn_Wo"].T)
    out["l_w_qf"] = block_diagonal(a["L2_xattn_Wqf"])
    out["l_b_q"] = a["L2_xattn_bq"].reshape(2, P).T
    out["l_b_v"] = a["L2_xattn_bv"]
    out["l_b_o"] = a["L2_xattn_bo"]
    order = np.pad(a["L2_ffn_down_reorder_index"], (0, FT2 * P - FF2))
    out["q_order"] = order.reshape(FT2, P).T
    out["q_w_gate"] = a["L2_ffn_w_gate"]
    out["q_w_up"] = a["L2_ffn_w_up"]
    out["q_w_down"] = a["L2_ffn_w_down"].reshape(DC, P, FF2).transpose(1, 0, 2)
    wq = a["L3_xattn_Wq"].reshape(DC, P, H, HD).transpose(2, 1, 0, 3).reshape(H, P, D)
    wk = a["L3_xattn_Wk"].reshape(D, H, HD).transpose(1, 2, 0)
    wv = a["L3_xattn_Wv"].reshape(DC, P, H, HD).transpose(2, 1, 0, 3).reshape(H, P, D)
    wo = a["L3_xattn_Wo"].reshape(H, HD, D)
    out["a_w"] = np.concatenate([np.concatenate([wq, wk], 2), np.concatenate([wv, wo], 2)])

    def pack(gate, up, down, owner, tiles, experts):
        pad = tiles * P - len(gate)
        gate, up, down = (np.pad(w, ((0, pad), (0, 0))) for w in (gate, up, down))
        one = np.zeros((P, tiles * P), np.float32)
        one[owner, np.arange(len(owner))] = 1.0
        up_in = np.stack([gate, up]).reshape(2, tiles, P, DC, P).transpose(1, 4, 0, 3, 2)
        return np.concatenate([up_in.reshape(tiles, P, 4 * P), down.reshape(tiles, P, D),
                               one.reshape(P, tiles, P).transpose(1, 0, 2)], 2)

    def before(n):
        return np.tile((np.arange(n)[None, :] < np.arange(n)[:, None]).astype(np.float32), (P, 1, 1))
    gu, dn = a["L1_ffn_expert_gate_up"], a["L1_ffn_expert_down"]
    sgu, sdn = a["L1_ffn_shared_gate_up"], a["L1_ffn_shared_down"]
    out["m1_pack"] = pack(np.concatenate([gu[:, :I1].reshape(-1, D), sgu[:SI1]]),
                          np.concatenate([gu[:, I1:].reshape(-1, D), sgu[SI1:]]),
                          np.concatenate([dn.transpose(0, 2, 1).reshape(-1, D), sdn.T]),
                          np.concatenate([np.repeat(np.arange(E1), I1), np.full(SI1, E1)]), TILES1, E1)
    out["m1_gate"] = chunks(np.concatenate([a["L1_ffn_gate_w"], a["L1_ffn_shared_gate_vec"]]).T)
    out["m1_before"] = before(E1)
    gu, dn = a["L3_ffn_w_gate_up"].transpose(0, 2, 1), a["L3_ffn_w_down"]
    sgu, sdn = a["L3_ffn_shared_gate_up"].T, a["L3_ffn_shared_down"]
    out["m3_pack"] = pack(np.concatenate([gu[:, :I3].reshape(-1, D), sgu[:I3]]),
                          np.concatenate([gu[:, I3:].reshape(-1, D), sgu[I3:]]),
                          np.concatenate([dn.reshape(-1, D), sdn]),
                          np.repeat(np.arange(E3 + 1), I3), TILES3, E3)
    out["m3_gate"] = chunks(a["L3_ffn_gate_w"])
    out["m3_before"] = before(E3)
    return {k: np.ascontiguousarray(v) for k, v in out.items()}


def program(nc, dram):
    with ExitStack() as ctx:
        core = Core(nc, ctx, dram)
        setup(core)
        with ExitStack() as sums:
            core.open_kv_sums(sums)
            for stage in STAGES_A:
                stage(core)
                if stage is moe_1:
                    core.retire_sems()
        for stage in STAGES_B:
            stage(core)
        store(core)


STAGES_A = [window_attention, lookup_ffn, memory_attention_and_features, moe_1, linear_attention]
STAGES_B = [quantised_ffn, full_attention, moe_3]


def kernel(**inputs):
    import numpy as _np
    import concourse.bacc as _bacc
    from concourse import mybir as _mybir
    from concourse.bass_utils import run_bass_kernel_spmd as _run

    nc = _bacc.Bacc("TRN2", target_bir_lowering=False, num_devices=1)
    arrays, dram = {}, {}
    for name, a in layouts({k: _np.asarray(v) for k, v in inputs.items()}).items():
        arrays[f"in_{name}"] = a
        dram[name] = nc.dram_tensor(f"in_{name}", a.shape, _mybir.dt.from_np(a.dtype),
                                    kind="ExternalInput").ap()
    dram["out"] = nc.dram_tensor("out_0", (B, S, D), _mybir.dt.float32, kind="ExternalOutput").ap()
    program(nc, dram)
    r = _run(nc, [arrays], core_ids=[0])
    return r.results[0]["out_0"]
```

```python
from contextlib import ExitStack

import numpy as np

import concourse.bass as bass
from concourse import mybir

F32 = mybir.dt.float32
BF16 = mybir.dt.bfloat16
I32 = mybir.dt.int32
U32 = mybir.dt.uint32
U8 = mybir.dt.uint8
ACT = mybir.ActivationFunctionType
ALU = mybir.AluOpType
AXIS = mybir.AxisListType
REDUCE = bass.bass_isa.ReduceOp

P = 128
B, S, D = 8, 56, 256
SP = 64
PAIRS = B // 2
T = B * SP
TOK = B * S
DC = D // P
LK = 1500
KT, KP = 12, 125
KN = 500
EPS = 1e-5
NEG = -1e30
AHEAD = 8
DMA = 16


class InOrder:

    def __init__(self, eng, sem, n=0):
        self.eng, self.sem, self.n, self.base = eng, sem, n, 0

    def __call__(self, ins):
        ins.then_inc(self.sem, 1)
        self.n += 1
        self.eng.wait_ge(self.sem, self.base + self.n)

    def loop(self, i, first, per_turn):
        self.base, self.n = first + i * per_turn, 0

    def end(self, first, per_turn, turns):
        assert self.n == per_turn, (self.n, per_turn)
        self.base, self.n = 0, first + per_turn * turns


class Core:

    def __init__(self, nc, ctx, dram):
        self.nc, self.dram = nc, dram

        def sb(name, shape, dt=F32):
            return ctx.enter_context(nc.sbuf_tensor(name, shape, dt))

        self.x_rows = sb("x_rows", [P, PAIRS, D])
        self.xn_rows = sb("xn_rows", [P, PAIRS, D])
        self.xn_cols = sb("xn_cols", [P, DC, T])
        self.ident = sb("ident", [P, P])
        self.bn = sb("bn", [P, PAIRS, 6])
        self.mean_var = sb("mean_var", [P, PAIRS, 2])
        self.var_eps = sb("var_eps", [P, PAIRS])
        self.rstd = sb("rstd", [P, PAIRS])
        self.minus_half = sb("minus_half", [P, PAIRS])
        self.psum = ctx.enter_context(nc.psum_tensor("psum", [P, 8, 512], F32))

        self.stage_sems = []
        self.const_ready = self.sem("const_ready")
        self.dve_step = self.sem("dve_step")
        self.act_step = self.sem("act_step")
        self.pool_step = self.sem("pool_step")
        self.ln_stats = self.sem("ln_stats")
        self.ln_rstd = self.sem("ln_rstd")
        self.ln_rows = self.sem("ln_rows")
        self.ln_turned = self.sem("ln_turned")
        self.ln_cols = self.sem("ln_cols")
        self.fp8_order_in = self.sem("fp8_order_in")
        self.fp8_down_in = self.sem("fp8_down_in")
        self.fp8_rows_in = self.sem("fp8_rows_in")
        self.fp8_exponents = self.sem("fp8_exponents")
        self.fp8_rounded = self.sem("fp8_rounded")
        self.keep_sems()
        self.norms = 0
        self.turn_of = {}
        self.dve_n = self.act_n = self.pool_n = 0

    def sem(self, name):
        self.stage_sems.append(self.nc.alloc_semaphore(name=name))
        return self.stage_sems[-1]

    def keep_sems(self):
        self.stage_sems = []

    def retire_sems(self):
        self.nc.clear_and_free_semaphores(self.stage_sems)
        self.nc.all_engine_barrier()
        self.stage_sems = []

    def open_kv_sums(self, ctx):
        self.kv_sums = ctx.enter_context(self.nc.sbuf_tensor("kv_sums", [P, B, 8, 34], F32))

    def open_fp8_weights(self, ctx):
        self.fp8_weights = Fp8Weights(self, ctx)

    def new_norm(self, turned=True):
        k = self.norms
        self.norms += 1
        if turned:
            self.turn_of[k] = len(self.turn_of)
        return k

    def cols_ready(self, k):
        return DC * (self.turn_of[k] + 1)

    def ln_vector(self, dve, link, k):
        for i in range(PAIRS):
            ins = dve.bn_stats(self.bn[:, i, :], self.x_rows[:, i, :])
        link(ins)
        for i in range(PAIRS):
            ins = dve.bn_aggr(self.mean_var[:, i, :], self.bn[:, i, :])
        link(ins)
        dve.tensor_scalar(self.var_eps[:, :], self.mean_var[:, :, 1], EPS, None,
                          ALU.add).then_inc(self.ln_stats, 1)
        dve.wait_ge(self.ln_rstd, k + 1)
        for i in range(PAIRS):
            dve.tensor_scalar(self.xn_rows[:, i, :], self.x_rows[:, i, :], self.mean_var[:, i, 0:1],
                              self.rstd[:, i:i + 1], ALU.subtract, ALU.mult).then_inc(self.ln_rows, 1)

    def ln_pool(self, pool, k):
        pool.wait_ge(self.ln_stats, k + 1)
        pool.tensor_tensor(self.rstd[:, :], self.var_eps[:, :], self.minus_half[:, :],
                           ALU.pow).then_inc(self.ln_rstd, 1)

    def ln_tensor(self, pe, k):
        for i in range(PAIRS):
            pe.wait_ge(self.ln_rows, PAIRS * k + i + 1)
            for c in range(DC):
                ins = pe.transpose(self.psum[:, c, i * P:(i + 1) * P],
                                   self.xn_rows[:, i, c * P:(c + 1) * P], self.ident[:, :])
        ins.then_inc(self.ln_turned, 1)

    def ln_scalar(self, act, k):
        act.wait_ge(self.ln_turned, self.turn_of[k] + 1)
        for c in range(DC):
            act.copy(self.xn_cols[:, c, :], self.psum[:, c, :]).then_inc(self.ln_cols, 1)

    def tok(self, c):
        return self.xn_cols[:, c, :].rearrange("p (b s) -> p b s", b=B)[:, :, 0:S]


def unpad(cols):
    return cols.rearrange("p (b s) -> p b s", b=B)[:, :, 0:S]


def packed(cols):
    return cols.rearrange("p (b s) -> p b s", b=B)


def setup(core):
    nc, dram = core.nc, core.dram
    x_loaded, zeroed = core.sem("x_loaded"), core.sem("zeroed")
    core.x_loaded = x_loaded
    with nc.Block() as block:
        @block.vector
        def _(dve):
            dve.memset(core.x_rows[:, :, :], 0.0).then_inc(zeroed, 1)
            dve.memset(core.minus_half[:, :], -0.5).then_inc(zeroed, 1)

        def load(eng, k):
            eng.wait_ge(zeroed, 1)
            for b in range(k, B, 2):
                eng.dma_start(core.x_rows[k * SP:k * SP + S, b // 2, :], dram["x"][b]).then_inc(x_loaded, DMA)

        @block.scalar
        def _(act):
            load(act, 0)

        @block.sync
        def _(sp):
            load(sp, 1)
            sp.dma_start(core.ident[:, :], dram["c_ident"]).then_inc(core.const_ready, DMA)
            sp.wait_ge(x_loaded, DMA * B)
            sp.wait_ge(core.const_ready, DMA)


def store(core):
    dram = core.dram
    stored = core.sem("stored")
    with core.nc.Block() as block:
        def write(eng, k):
            for b in range(k, B, 2):
                eng.dma_start(dram["out"][b], core.x_rows[k * SP:k * SP + S, b // 2, :]).then_inc(stored, DMA)

        @block.scalar
        def _(act):
            write(act, 0)

        @block.sync
        def _(sp):
            write(sp, 1)
            sp.wait_ge(stored, DMA * B)


H, HD = 16, 128
KVC, QC, R = 64, 96, 64
WIN = 9
GQ = 14
GROUPS = S // GQ
GR = GQ * WIN
HH = H // 2
ROW0 = GQ * HH


def window_attention(core):
    nc, dram, ps = core.nc, core.dram, core.psum
    k_ln = core.new_norm()
    dve0, Z = core.dve_n, AHEAD
    scale = 1.0 / float(np.sqrt(np.float32(HD + R)))
    ctx = ExitStack()
    with ctx:
        def sb(name, shape, dt=F32):
            return ctx.enter_context(nc.sbuf_tensor(name, shape, dt))
        w_dq = sb("w_dq", [P, DC, QC])
        w_kvc_t = sb("w_kvc_t", [KVC, D])
        w_kr2 = sb("w_kr2", [KVC, 2 * R])
        w_key = sb("w_key", [P, DC, P])
        w_key_sw = sb("w_key_sw", [P, DC, R])
        w_uq_t = sb("w_uq_t", [P, H, QC])
        w_uk_t = sb("w_uk_t", [P, H, KVC])
        w_qr = sb("w_qr", [QC, 2, H * R])
        w_abs = sb("w_abs", [QC, H * KVC])
        w_uv_t = sb("w_uv_t", [P, H, KVC])
        w_o = sb("w_o", [P, H, D])
        w_vo = sb("w_vo", [P, HH, D])
        q_lat = sb("q_lat", [QC, T])
        rope_q = sb("rope_q", [P, 2, S])
        rope_a = sb("rope_a", [P, TOK])
        rope_b = sb("rope_b", [P, TOK])
        q_cat = sb("q_cat", [P, B * GROUPS, H, GQ])
        q_now = sb("q_now", [P, 2, GROUPS, H, GQ])
        seg_k = sb("seg_k", [GR, B * GROUPS], I32)
        seg_r = sb("seg_r", [ROW0, B * GROUPS], I32)
        win_k = sb("win_k", [GR, 1])
        seq_row = sb("seq_row", [GR, B * GROUPS])
        win_r = sb("win_r", [ROW0, WIN])
        diag = sb("diag", [ROW0, GR])
        row_f = sb("row_f", [GR, B * GROUPS])
        row_c = sb("row_c", [GR, B * GROUPS])
        rows_at = sb("rows_at", [GR, B * GROUPS], I32)
        kid = sb("kid", [ROW0, B * GROUPS, WIN])
        kid_c = sb("kid_c", [ROW0, B * GROUPS, WIN])
        outside = sb("outside", [ROW0, B * GROUPS, WIN])
        mask = sb("mask", [ROW0, B * GROUPS, GR])
        got = sb("got", [GR, 2, GROUPS, 3 * P])
        got_t = sb("got_t", [P, 3, GROUPS * GR])
        key_sin = sb("key_sin", [P, GROUPS * GR])
        keys = sb("keys", [P, 2, GROUPS * GR])
        vals = sb("vals", [GR, 2, GROUPS, KVC])
        scores = sb("scores", [ROW0, 2, GROUPS * GR])
        neg_max = sb("neg_max", [ROW0, 2, GROUPS])
        sums = sb("sums", [ROW0, 2, GROUPS])
        inv = sb("inv", [ROW0, 2, GROUPS])
        prob = sb("prob", [ROW0, 2, GROUPS * GR])
        prob_t = sb("prob_t", [GR, 2, GROUPS * ROW0])
        lat = sb("lat", [P, HH, T])

        sem = core.sem
        idx_in = sem("w_idx_in")
        fold_in = sem("w_fold_in")
        query_in = sem("w_query_in")
        out_in = sem("w_out_in")
        rows_known = sem("w_rows_known")
        got_in = [sem("w_got_in0"), sem("w_got_in1")]
        got_turned = sem("w_got_turned")
        got_t_ready = sem("w_got_t_ready")
        key_mm = sem("w_key_mm")
        key_latent = sem("w_key_latent")
        key_ready = sem("w_key_ready")
        val_mm = sem("w_val_mm")
        val_ready = sem("w_val_ready")
        comp_mm = sem("w_comp_mm")
        comp_ready = sem("w_comp_ready")
        q_mm = sem("w_q_mm")
        q_rot = sem("w_q_rot")
        q_abs = sem("w_q_abs")
        q_staged = sem("w_q_staged")
        score_mm = sem("w_score_mm")
        score_sb = sem("w_score_sb")
        maxed = sem("w_maxed")
        exped = sem("w_exped")
        normed = sem("w_normed")
        prob_turned = sem("w_prob_turned")
        prob_t_ready = sem("w_prob_t_ready")
        lat_mm = sem("w_lat_mm")
        lat_ready = sem("w_lat_ready")
        out_mm = sem("w_out_mm")

        gt = GROUPS * GR
        block = ctx.enter_context(nc.Block())

        @block.sync
        def _(sp):
            for dst, src in ((seg_k, "seg_k"), (win_k, "c_win_k"), (seq_row, "c_seq_row"),
                             (seg_r, "seg_r"), (win_r, "c_win_r"), (diag, "c_diag")):
                sp.dma_start(dst[:, :], dram[src]).then_inc(idx_in, DMA)
            sp.dma_start(w_kvc_t[:, :], dram["w_kvc_t"]).then_inc(fold_in, DMA)
            sp.dma_start(w_kr2[:, :], dram["w_kr2"]).then_inc(fold_in, DMA)
            sp.dma_start(w_key[:, :, 0:KVC], dram["w_kvc"]).then_inc(fold_in, DMA)
            sp.dma_start(w_dq[:, :, :], dram["w_dq"]).then_inc(fold_in, DMA)
            for dst, src in ((w_uq_t, "w_uq_t"), (w_uk_t, "w_uk_t"), (w_qr, "w_qr"), (rope_q, "c_rope_q")):
                sp.dma_start(dst[:, :, :], dram[src]).then_inc(query_in, DMA)
            for dst, src in ((w_uv_t, "w_uv_t"), (w_o, "w_o")):
                sp.dma_start(dst[:, :, :], dram[src]).then_inc(out_in, DMA)

        @block.gpsimd
        def _(pool):
            core.ln_pool(pool, k_ln)
            pool.sem_inc(q_staged, Z)
            pool.wait_ge(rows_known, 1)

            def gather(b):
                for g in range(GROUPS):
                    n = b * GROUPS + g
                    pool.indirect_dma_start(
                        got[:, b % 2, g, :], None, dram["ctx_rope"],
                        bass.IndirectOffsetOnAxis(ap=rows_at[:, n:n + 1], axis=0),
                    ).then_inc(got_in[b % 2], DMA)
            gather(0)
            gather(1)
            pool.wait_ge(q_rot, 2 * HH)
            pool.wait_ge(q_abs, 1 + 2 * HH)
            for b in range(B):
                pool.wait_ge(score_mm, Z + b - 1)
                pool.tensor_copy(q_now[:, b % 2, :, :, :], q_cat[:, b * GROUPS:(b + 1) * GROUPS, :, :]) \
                    .then_inc(q_staged, 1)
                if b + 2 < B:
                    pool.wait_ge(got_turned, Z + b + 1)
                    gather(b + 2)

        @block.tensor
        def _(pe):
            for x in (got_turned, key_mm, val_mm, score_mm, prob_turned, lat_mm):
                pe.sem_inc(x, Z)
            pe.wait_ge(fold_in, DMA * 4)
            for c in range(DC):
                ins = pe.matmul(ps[:, 2, c * P:(c + 1) * P], w_kvc_t[:, c * P:(c + 1) * P], w_kr2[:, :],
                                start=True, stop=True)
            ins.then_inc(comp_mm, 1)
            core.ln_tensor(pe, k_ln)
            pe.wait_ge(core.ln_cols, core.cols_ready(k_ln))
            for c in range(DC):
                ins = pe.matmul(ps[0:QC, 7, :], w_dq[:, c, :], core.xn_cols[:, c, :],
                                start=(c == 0), stop=(c == DC - 1))
            ins.then_inc(q_mm, 1)
            pe.wait_ge(query_in, DMA * 4)
            for h in range(H):
                ins = pe.matmul(ps[0:QC, 3 + h // 8, (h % 8) * KVC:(h % 8 + 1) * KVC],
                                w_uq_t[:, h, :], w_uk_t[:, h, :], start=True, stop=True)
            ins.then_inc(comp_mm, 1)
            pe.wait_ge(q_abs, 1)
            pe.wait_ge(comp_ready, 3)
            lq = unpad(q_lat[:, :])
            for j in range(HH):
                if j >= 2:
                    pe.wait_ge(q_rot, 2 * (j - 1))
                    pe.wait_ge(q_abs, 1 + 2 * (j - 1))
                bank = 3 * (j % 2)
                pe.matmul(packed(ps[:, bank, 0:TOK]), w_abs[:, j * P:(j + 1) * P], lq, start=True, stop=True)
                for k in range(2):
                    ins = pe.matmul(packed(ps[:, bank + 1 + k, 0:TOK]), w_qr[:, k, j * P:(j + 1) * P], lq,
                                    start=True, stop=True)
                ins.then_inc(q_mm, 1)

            pe.wait_ge(out_in, DMA * 2)
            for j in range(HH):
                if j == 4:
                    pe.wait_ge(comp_ready, 4)
                for k in range(2):
                    ins = pe.matmul(ps[k * KVC:(k + 1) * KVC, 6 + j // 2 % 2, (j % 2) * D:(j % 2 + 1) * D],
                                    w_uv_t[:, j + k * HH, :], w_o[:, j + k * HH, :], start=True, stop=True)
                if j % 4 == 3:
                    ins.then_inc(comp_mm, 1)
            pe.wait_ge(q_rot, 2 * HH)
            pe.wait_ge(q_abs, 1 + 2 * HH)

            def turn_rows(b, i, s):
                pe.wait_ge(got_in[s], DMA * GROUPS * (i + 1))
                pe.wait_ge(prob_t_ready, Z + 2 * (b - 1))
                for c in range(3):
                    for g in range(GROUPS):
                        ins = pe.transpose(ps[:, c, g * GR:(g + 1) * GR], got[:, s, g, c * P:(c + 1) * P],
                                           core.ident[0:GR, 0:GR])
                ins.then_inc(got_turned, 1)

            def project(b):
                pe.wait_ge(got_t_ready, Z + 3 * (b + 1))
                for c in range(DC):
                    pe.matmul(ps[:, 3, 0:gt], w_key[:, c, :], got_t[:, c, :],
                              start=(c == 0), stop=(c == DC - 1))
                for c in range(DC):
                    ins = pe.matmul(ps[0:R, 4, 0:gt], w_key_sw[:, c, :], got_t[:, c, :],
                                    start=(c == 0), stop=(c == DC - 1))
                ins.then_inc(key_mm, 1)

            def turn_keys(b, s):
                pe.wait_ge(key_ready, Z + b + 1)
                for g in range(GROUPS):
                    ins = pe.transpose(ps[0:GR, 4, g * P:(g + 1) * P], keys[:, s, g * GR:(g + 1) * GR],
                                       core.ident[:, :])
                ins.then_inc(val_mm, 1)

            def score(b, s):
                pe.wait_ge(q_staged, Z + b + 1)
                pe.wait_ge(score_sb, Z + b)
                for k in range(2):
                    for g in range(GROUPS):
                        ins = pe.matmul(ps[0:ROW0, 5 + k, g * GR:(g + 1) * GR],
                                        q_now[:, s, g, k * HH:(k + 1) * HH, :].rearrange("p h q -> p (h q)"),
                                        keys[:, s, g * GR:(g + 1) * GR], start=True, stop=True)
                ins.then_inc(score_mm, 1)

            def turn_probs(b):
                pe.wait_ge(normed, Z + b + 1)
                for k in range(2):
                    for g in range(GROUPS):
                        ins = pe.transpose(ps[0:GR, k, g * ROW0:(g + 1) * ROW0], prob[:, k, g * GR:(g + 1) * GR],
                                           core.ident[0:ROW0, 0:ROW0])
                    ins.then_inc(prob_turned, 1)

            def mix(b, s):
                pe.wait_ge(val_ready, Z + b + 1)
                pe.wait_ge(lat_ready, Z + b)
                for k in range(2):
                    pe.wait_ge(prob_t_ready, Z + 2 * b + k + 1)
                    for g in range(GROUPS):
                        at = slice(g * ROW0, (g + 1) * ROW0)
                        ins = pe.matmul(ps[k * KVC:(k + 1) * KVC, 7, at], vals[:, s, g, :], prob_t[:, k, at],
                                        start=True, stop=True)
                ins.then_inc(lat_mm, 1)

            def step(i, s, more=True):
                b, after = 2 * i + s, (i + s, 1 - s)
                if more:
                    turn_rows(b + 1, *after)
                    project(b + 1)
                turn_probs(b)
                if more:
                    turn_keys(b + 1, 1 - s)
                    score(b + 1, 1 - s)
                mix(b, s)
            turn_rows(0, 0, 0)
            project(0)
            turn_keys(0, 0)
            score(0, 0)
            with pe.Fori(0, PAIRS - 1) as i:
                for s in range(2):
                    step(i, s)
            for s in range(2):
                step(PAIRS - 1, s, more=(s == 0))
            pe.wait_ge(lat_ready, Z + B)
            pe.wait_ge(comp_ready, 5)
            for i in range(PAIRS):
                for j in range(HH):
                    ins = pe.matmul(ps[:, i // 2, (i % 2) * D:(i % 2 + 1) * D], lat[:, j, i * P:(i + 1) * P],
                                    w_vo[:, j, :], start=(j == 0), stop=(j == HH - 1))
                if i % 2:
                    ins.then_inc(out_mm, 1)

        @block.scalar
        def _(act):
            for x in (got_t_ready, key_latent, val_ready, exped, prob_t_ready):
                act.sem_inc(x, Z)
            act.wait_ge(comp_mm, 1)
            act.copy(w_key[:, :, KVC:P], ps[:, 2, 0:2 * P].rearrange("p (c k) -> p c k", c=2)[:, :, 0:R]) \
                .then_inc(comp_ready, 1)
            act.copy(w_key_sw[:, :, :], ps[:, 2, 0:2 * P].rearrange("p (c k) -> p c k", c=2)[:, :, R:P]) \
                .then_inc(comp_ready, 1)
            core.ln_scalar(act, k_ln)
            act.wait_ge(q_mm, 1)
            act.copy(q_lat[:, :], ps[0:QC, 7, :]).then_inc(q_abs, 1)
            act.wait_ge(comp_mm, 2)
            act.copy(w_abs[:, :], ps[0:QC, 3:5, :].rearrange("p a n -> p (a n)")).then_inc(comp_ready, 1)
            for j in range(HH):
                act.wait_ge(q_mm, 2 + j)
                for k in range(2):
                    act.copy(q_cat[0:KVC, :, 2 * j + k, :],
                             ps[k * KVC:(k + 1) * KVC, 3 * (j % 2), 0:TOK]
                             .rearrange("p (n q) -> p n q", q=GQ)).then_inc(q_abs, 1)

            for a in range(2):
                act.wait_ge(comp_mm, 3 + a)
                act.copy(w_vo[:, 4 * a:4 * a + 4, :].rearrange("p j n -> p (j n)"),
                         ps[:, 6:8, :].rearrange("p a n -> p (a n)")).then_inc(comp_ready, 1)

            def turned_rows(b):
                act.wait_ge(got_turned, Z + b + 1)
                act.wait_ge(key_ready, Z + b)
                for c in range(2):
                    act.copy(got_t[:, c, :], ps[:, c, 0:gt]).then_inc(got_t_ready, 1)

            def latent_keys(b, s):
                act.wait_ge(key_mm, Z + b + 1)
                act.wait_ge(score_mm, Z + b - 1)
                act.copy(keys[0:KVC, s, :], ps[0:KVC, 3, 0:gt]).then_inc(key_latent, 1)

            def values(b, s):
                act.wait_ge(val_mm, Z + b + 1)
                act.copy(vals[:, s, :, :], ps[0:GR, 4, :].rearrange("p (g k) -> p g k", g=GROUPS)[:, :, 0:KVC]) \
                    .then_inc(val_ready, 1)

            def exps(b):
                act.wait_ge(maxed, Z + b + 1)
                act.wait_ge(prob_turned, Z + 2 * b)
                for k in range(2):
                    for g in range(GROUPS):
                        at = slice(g * GR, (g + 1) * GR)
                        act.activation(prob[:, k, at], scores[:, k, at], ACT.Exp, bias=neg_max[:, k, g:g + 1],
                                       accum_out=sums[:, k, g:g + 1]).then_inc(exped, 1)

            def turned_probs(b):
                for k in range(2):
                    act.wait_ge(prob_turned, Z + 2 * b + k + 1)
                    act.wait_ge(lat_mm, Z + b)
                    act.copy(prob_t[:, k, :], ps[0:GR, k, 0:GROUPS * ROW0]).then_inc(prob_t_ready, 1)

            def step(i, s, more=True):
                b = 2 * i + s
                if more:
                    turned_rows(b + 1)
                exps(b)
                if more:
                    latent_keys(b + 1, 1 - s)
                turned_probs(b)
                if more:
                    values(b + 1, 1 - s)
            turned_rows(0)
            latent_keys(0, 0)
            values(0, 0)
            with act.Fori(0, PAIRS - 1) as i:
                for s in range(2):
                    step(i, s)
            for s in range(2):
                step(PAIRS - 1, s, more=(s == 0))

        @block.vector
        def _(dve):
            link = InOrder(dve, core.dve_step, dve0)
            for x in (key_ready, score_sb, maxed, normed, lat_ready):
                dve.sem_inc(x, Z)
            core.ln_vector(dve, link, k_ln)
            dve.wait_ge(idx_in, DMA * 6)
            link(dve.tensor_scalar(row_f[:, :], seg_k[:, :], win_k[:, 0:1], 0.0, ALU.add, ALU.max))
            link(dve.tensor_scalar(row_c[:, :], row_f[:, :], float(LK - 1), None, ALU.min))
            dve.tensor_tensor(rows_at[:, :], row_c[:, :], seq_row[:, :], ALU.add).then_inc(rows_known, 1)
            n_g = B * GROUPS
            link(dve.tensor_tensor(kid[:, :, :], seg_r[:, :].unsqueeze(2).to_broadcast([ROW0, n_g, WIN]),
                                   win_r[:, :].unsqueeze(1).to_broadcast([ROW0, n_g, WIN]), ALU.add))
            link(dve.tensor_scalar(kid_c[:, :, :], kid[:, :, :], 0.0, float(LK - 1), ALU.max, ALU.min))
            link(dve.tensor_tensor(outside[:, :, :], kid[:, :, :], kid_c[:, :, :], ALU.not_equal))
            link(dve.tensor_scalar(outside[:, :, :], outside[:, :, :], NEG, None, ALU.mult))
            link(dve.tensor_tensor(mask[:, :, :].rearrange("p n (q w) -> p n q w", w=WIN),
                                   diag[:, :].rearrange("p (q w) -> p q w", w=WIN).unsqueeze(1)
                                   .to_broadcast([ROW0, n_g, GQ, WIN]),
                                   outside[:, :, :].unsqueeze(2).to_broadcast([ROW0, n_g, GQ, WIN]), ALU.add))
            dve.wait_ge(query_in, DMA * 4)
            for j in range(HH):
                bank = 3 * (j % 2)
                dve.wait_ge(q_mm, 2 + j)
                link(dve.tensor_tensor(packed(rope_a[:, :]), packed(ps[:, bank + 1, 0:TOK]),
                                       rope_q[:, 0:1, :].to_broadcast([P, B, S]), ALU.mult))
                link(dve.tensor_tensor(packed(rope_b[:, :]), packed(ps[:, bank + 2, 0:TOK]),
                                       rope_q[:, 1:2, :].to_broadcast([P, B, S]), ALU.mult))
                for k in range(2):
                    r = slice(k * R, (k + 1) * R)
                    dve.tensor_tensor(q_cat[KVC:P, :, 2 * j + k, :],
                                      rope_a[r, :].rearrange("p (n q) -> p n q", q=GQ),
                                      rope_b[r, :].rearrange("p (n q) -> p n q", q=GQ), ALU.add) \
                        .then_inc(q_rot, 1)
                    dve.wait_ge(q_rot, 2 * j + k + 1)

            link(dve.memset(lat[:, :, :], 0.0))

            def turned_table(b):
                dve.wait_ge(got_turned, Z + b + 1)
                dve.wait_ge(key_ready, Z + b)
                dve.tensor_copy(got_t[:, 2, :], ps[:, 2, 0:gt]).then_inc(got_t_ready, 1)
                dve.wait_ge(got_t_ready, Z + 3 * (b + 1))

            def rotary_keys(b, s):
                dve.wait_ge(key_mm, Z + b + 1)
                link(dve.tensor_tensor(key_sin[KVC:P, :], ps[0:R, 4, 0:gt], got_t[0:R, 2, :], ALU.mult))
                dve.wait_ge(score_mm, Z + b - 1)
                dve.wait_ge(key_latent, Z + b + 1)
                link(dve.tensor_tensor(keys[KVC:P, s, :], ps[KVC:P, 3, 0:gt], got_t[KVC:P, 2, :], ALU.mult))
                dve.tensor_tensor(keys[KVC:P, s, :], keys[KVC:P, s, :], key_sin[KVC:P, :], ALU.add) \
                    .then_inc(key_ready, 1)

            def scored(b):
                dve.wait_ge(score_mm, Z + b + 1)
                dve.wait_ge(exped, Z + 2 * GROUPS * b)
                dve.scalar_tensor_tensor(scores[:, :, :], ps[0:ROW0, 5:7, 0:gt], scale,
                                         mask[:, bass.ds(b * GROUPS, GROUPS), :].rearrange("p g r -> p (g r)")
                                         .unsqueeze(1).to_broadcast([ROW0, 2, gt]),
                                         ALU.mult, ALU.add).then_inc(score_sb, 1)
                dve.wait_ge(score_sb, Z + b + 1)
                dve.tensor_reduce(neg_max[:, :, :], scores[:, :, :].rearrange("p k (g r) -> p k g r", g=GROUPS),
                                  AXIS.X, ALU.max, negate=True).then_inc(maxed, 1)

            def normalise(b):
                dve.wait_ge(exped, Z + 2 * GROUPS * (b + 1))
                link(dve.reciprocal(inv[:, :, :], sums[:, :, :]))
                probs = prob[:, :, :].rearrange("p k (g r) -> p k g r", g=GROUPS)
                dve.tensor_tensor(probs, probs, inv[:, :, :].unsqueeze(3).to_broadcast([ROW0, 2, GROUPS, GR]),
                                  ALU.mult).then_inc(normed, 1)

            def mixed(b):
                dve.wait_ge(lat_mm, Z + b + 1)
                dst = lat[:, :, bass.ds(b * SP, SP)][:, :, 0:S].rearrange("p j (g q) -> p g j q", g=GROUPS)
                dve.tensor_copy(dst, ps[:, 7, 0:GROUPS * ROW0].rearrange("p (g j q) -> p g j q", g=GROUPS, q=GQ)) \
                    .then_inc(lat_ready, 1)

            def step(i, s, more=True):
                b = 2 * i + s
                if more:
                    turned_table(b + 1)
                normalise(b)
                if more:
                    rotary_keys(b + 1, 1 - s)
                    scored(b + 1)
                mixed(b)
            turned_table(0)
            rotary_keys(0, 0)
            scored(0)
            first, per_step = link.n, 3
            with dve.Fori(0, PAIRS - 1) as i:
                link.loop(i, first, 2 * per_step)
                for s in range(2):
                    step(i, s)
            link.end(first, 2 * per_step, PAIRS - 1)
            for s in range(2):
                step(PAIRS - 1, s, more=(s == 0))
            for a in range(2):
                dve.wait_ge(out_mm, a + 1)
                link(dve.tensor_tensor(core.x_rows[:, 2 * a:2 * a + 2, :].rearrange("p i d -> p (i d)"),
                                       core.x_rows[:, 2 * a:2 * a + 2, :].rearrange("p i d -> p (i d)"),
                                       ps[:, a, :], ALU.add))
            core.dve_n = link.n


FF0 = 1024
FT0 = FF0 // P
STEP = 0.1
QMIN, QMAX = -32768.0, 32767.0
ROUND = 1.5 * 2.0 ** 23


def lookup_ffn(core):
    nc, dram, ps = core.nc, core.dram, core.psum
    k_ln = core.new_norm()
    dve0 = core.dve_n
    ctx = ExitStack()
    with ctx:
        def sb(name, shape, dt=F32):
            return ctx.enter_context(nc.sbuf_tensor(name, shape, dt))
        w1 = sb("f_w1", [P, DC, FF0])
        w2 = sb("f_w2", [P, FT0, D])
        tenths = sb("f_tenths", [P, 2, TOK])
        act_t = sb("f_act_t", [P, FT0, T])
        sem = core.sem
        w_in, up_mm, rounded, acted, out_mm = (sem("f_" + n) for n in
                                               ("weights_in", "up_mm", "rounded", "acted", "out_mm"))
        block = ctx.enter_context(nc.Block())

        @block.sync
        def _(sp):
            sp.dma_start(w1[:, :, :], dram["f_w1"]).then_inc(w_in, DMA)
            sp.dma_start(w2[:, :, :], dram["f_w2"]).then_inc(w_in, DMA)

        @block.gpsimd
        def _(pool):
            core.ln_pool(pool, k_ln)

        @block.tensor
        def _(pe):
            core.ln_tensor(pe, k_ln)
            pe.wait_ge(core.ln_cols, core.cols_ready(k_ln))
            pe.wait_ge(w_in, 2 * DMA)
            for f in range(FT0):
                if f >= 4:
                    pe.wait_ge(rounded, f - 3)
                for c in range(DC):
                    ins = pe.matmul(packed(ps[:, 2 + f % 4, 0:TOK]), w1[:, c, f * P:(f + 1) * P], core.tok(c),
                                    start=(c == 0), stop=(c == DC - 1))
                ins.then_inc(up_mm, 1)
            pe.wait_ge(acted, FT0)
            for i in range(PAIRS):
                for f in range(FT0):
                    ins = pe.matmul(ps[:, 6 + i // 2, (i % 2) * D:(i % 2 + 1) * D],
                                    act_t[:, f, i * P:(i + 1) * P], w2[:, f, :],
                                    start=(f == 0), stop=(f == FT0 - 1))
                if i % 2:
                    ins.then_inc(out_mm, 1)

        @block.scalar
        def _(act):
            core.ln_scalar(act, k_ln)
            for f in range(FT0):
                act.wait_ge(rounded, f + 1)
                act.activation(unpad(act_t[:, f, :]), packed(tenths[:, f % 2, :]), ACT.Gelu_apprx_tanh,
                               scale=STEP).then_inc(acted, 1)

        @block.vector
        def _(dve):
            link = InOrder(dve, core.dve_step, dve0)
            core.ln_vector(dve, link, k_ln)
            link(dve.memset(act_t[:, :, :], 0.0))
            for f in range(FT0):
                dve.wait_ge(up_mm, f + 1)
                if f >= 2:
                    dve.wait_ge(acted, f - 1)
                t = tenths[:, f % 2, :]
                link(dve.tensor_scalar(t, ps[:, 2 + f % 4, 0:TOK], 1.0 / STEP, QMIN, ALU.mult, ALU.max))
                link(dve.tensor_scalar(t, t, QMAX, ROUND, ALU.min, ALU.add))
                dve.tensor_scalar(t, t, ROUND, None, ALU.subtract).then_inc(rounded, 1)
            for a in range(2):
                dve.wait_ge(out_mm, a + 1)
                rows = core.x_rows[:, 2 * a:2 * a + 2, :].rearrange("p i d -> p (i d)")
                link(dve.tensor_tensor(rows, rows, ps[:, 6 + a, :], ALU.add))
            core.dve_n = link.n


NH2, HD2, FD2 = 16, 16, 64
HP = NH2 // 2
VW = 2 * HD2 + 1
BW = 2 * HD2 + 2
FG = 512
F32R = mybir.dt.float32r


def split(x, y):
    (x_hi, x_lo), (y_hi, y_lo) = x, y
    return (x_hi, y_hi), (x_hi, y_lo), (x_lo, y_hi)


def memory_attention_and_features(core):
    nc, dram, ps = core.nc, core.dram, core.psum
    k_ln = core.new_norm()
    dve0, Z = core.dve_n, AHEAD
    ctx = ExitStack()
    with ctx:
        def sb(name, shape, dt=F32):
            return ctx.enter_context(nc.sbuf_tensor("c_" + name, shape, dt))

        def parts(name, shape):
            return sb(name + "_hi", shape, F32R), sb(name + "_lo", shape, F32R)
        ctx_t = sb("ctx_t", [P, 2, DC, LK])
        ctx_r = sb("ctx_r", [KP, 2, KT, D])
        t_hi, t_lo = t_parts = parts("t", [P, DC, LK])
        w_k = sb("w_k", [P, DC, D])
        w_v = sb("w_v", [P, DC, D])
        w_kf = sb("w_kf", [P, FG])
        wk_hi, wk_lo = wk_parts = parts("wk", [P, DC, D])
        wv_hi, wv_lo = wv_parts = parts("wv", [P, DC, D])
        wf_hi, wf_lo = wf_parts = parts("wf", [P, FG])
        b_k = sb("b_k", [P, 2])
        mask2 = sb("mask2", [KP, B, KT])
        mask_now = sb("mask_now", [KP, KT])
        zero = sb("zero", [1, 512])
        q_pair = sb("q_pair", [P, DC, P])
        mask_u8 = sb("mask_u8", [P, LK // 4], I32)
        mask_add = sb("mask_add", [P, LK])
        any_key = sb("any_key", [P, 1])
        prob = sb("prob", [P, LK])
        neg_max = sb("neg_max", [P, 1])
        sums = sb("sums", [P, 1])
        inv = sb("inv", [P, 1])
        prob_t = sb("prob_t", [KP, KT, P])
        k_hi, k_lo = k_parts = parts("k", [P, 2, LK])
        feat = sb("feat", [KP, 2, 2, FG])
        v_aug = sb("v_aug", [KP, 2, 2, HP, VW])
        sums_sb = sb("sums_sb", [P, 512])
        sem = core.sem
        w_in = sem("c_weights_in")
        t_in = [sem("c_t_in0"), sem("c_t_in1")]
        names = ("r_in", "mask_in", "w_hi_ready", "w_lo_ready", "t_hi_ready", "t_lo_ready", "q_staged",
                 "score_mm", "maxed", "mask_read", "exped", "turned", "turned_sb", "out_mm", "added",
                 "kt_mm", "k_hi_ready", "k_lo_ready", "v_mm", "v_sb",
                 "feat_mm", "feat_act", "feat_dve", "sum_mm", "sum_sb", "sum_turned", "sum_kept")
        (r_in, mask_in, w_hi_ready, w_lo_ready, t_hi_ready, t_lo_ready, q_staged,
         score_mm, maxed, mask_read, exped, turned, turned_sb, out_mm, added,
         kt_mm, k_hi_ready, k_lo_ready, v_mm, v_sb,
         feat_mm, feat_act, feat_dve, sum_mm, sum_sb, sum_turned, sum_kept) = (
            sem("c_" + n) for n in names)
        weights = ((w_k[:, :, :], "c_w_k"), (w_v[:, :, :], "c_w_v"), (w_kf[:, :], "c_w_kf"))
        w_splits = ((w_k[:, :, :], wk_hi[:, :, :], wk_lo[:, :, :]), (w_v[:, :, :], wv_hi[:, :, :], wv_lo[:, :, :]),
                    (w_kf[:, :], wf_hi[:, :], wf_lo[:, :]))
        n_in = DMA * (len(weights) + 2)
        KT2 = KT // 2
        kv_sums = core.kv_sums
        block = ctx.enter_context(nc.Block())

        @block.sync
        def _(sp):
            sp.dma_start(ctx_t[:, 0, :, :], dram["ctx_t"][0]).then_inc(t_in[0], DMA)
            for dst, src in weights + ((b_k[:, :], "c_b_k"), (mask2[:, :, :], "c_mask2")):
                sp.dma_start(dst, dram[src]).then_inc(w_in, DMA)
            sp.dma_start(ctx_t[:, 1, :, :], dram["ctx_t"][1]).then_inc(t_in[1], DMA)
            for k in range(2):
                sp.dma_start(mask_u8[k * SP:(k + 1) * SP, :],
                             dram["c_mask"][k].partition_broadcast(SP)).then_inc(mask_in, DMA)
            for k in range(2):
                sp.dma_start(ctx_r[:, k, :, :], dram["ctx_r"][k]).then_inc(r_in, DMA)
            with sp.Fori(1, PAIRS) as n:
                sp.wait_ge(mask_read, Z + n)
                for k in range(2):
                    sp.dma_start(mask_u8[k * SP:(k + 1) * SP, :],
                                 dram["c_mask"][2 * n + k].partition_broadcast(SP)).then_inc(mask_in, DMA)
                sp.wait_ge(score_mm, Z + n)
                for k in range(2):
                    sp.wait_ge(t_hi_ready, Z + DC * (2 * n - 1 + k))
                    sp.wait_ge(t_lo_ready, Z + DC * (2 * n - 1 + k))
                    sp.dma_start(ctx_t[:, k, :, :], dram["ctx_t"][2 * n + k]).then_inc(t_in[k], DMA)
                sp.wait_ge(out_mm, Z + n)
                for k in range(2):
                    sp.dma_start(ctx_r[:, k, :, :], dram["ctx_r"][2 * n + k]).then_inc(r_in, DMA)

        @block.gpsimd
        def _(pool):
            core.ln_pool(pool, k_ln)
            pool.sem_inc(q_staged, Z)
            pool.wait_ge(core.ln_cols, core.cols_ready(k_ln))
            with pool.Fori(0, PAIRS) as n:
                pool.wait_ge(score_mm, Z + n)
                pool.tensor_copy(q_pair[:, :, :], core.xn_cols[:, :, bass.ds(n * P, P)]).then_inc(q_staged, 1)

        @block.tensor
        def _(pe):
            for s in (score_mm, turned, out_mm, kt_mm, v_mm, feat_mm, sum_mm, sum_turned):
                pe.sem_inc(s, Z)
            core.ln_tensor(pe, k_ln)

            def scores(n):
                pe.wait_ge(q_staged, Z + n + 1)
                pe.wait_ge(added, Z + n)
                for k in range(2):
                    pe.wait_ge(t_in[k], DMA * (n + 1))
                    for m in range(3):
                        for c in range(DC):
                            ins = pe.matmul(ps[k * SP:(k + 1) * SP, m, 0:KN], q_pair[:, c, k * SP:(k + 1) * SP],
                                            ctx_t[:, k, c, m * KN:(m + 1) * KN],
                                            start=(c == 0), stop=(c == DC - 1))
                ins.then_inc(score_mm, 1)

            def attend(n):
                pe.wait_ge(exped, Z + n + 1)
                for u in range(3):
                    if u == 2:
                        pe.wait_ge(turned_sb, Z + 3 * n + 1)
                    for x in range(4):
                        t = 4 * u + x
                        ins = pe.transpose(ps[0:KP, u % 2, x * P:(x + 1) * P], prob[:, t * KP:(t + 1) * KP],
                                           core.ident[:, :])
                    ins.then_inc(turned, 1)
                turn_sums(2 * n)
                pe.wait_ge(turned_sb, Z + 3 * n + 3)
                pe.wait_ge(r_in, 2 * DMA * (n + 1))
                for k in range(2):
                    for t in range(KT):
                        ins = pe.matmul(ps[k * SP:(k + 1) * SP, 2, 0:D], prob_t[:, t, k * SP:(k + 1) * SP],
                                        ctx_r[:, k, t, :], start=(t == 0), stop=(t == KT - 1))
                ins.then_inc(out_mm, 1)

            def keys(b):
                pe.wait_ge(w_lo_ready, len(weights))
                pe.wait_ge(t_lo_ready, Z + DC * (b + 1))
                pe.wait_ge(feat_act, Z + KT * b)
                pe.wait_ge(feat_dve, Z + KT * b)
                for e in range(6):
                    g, m = e // 3, e % 3
                    if e >= 3:
                        pe.wait_ge(k_lo_ready, Z + 6 * b + e - 2)
                    for c in range(DC):
                        for y, (wt, x) in enumerate(split(wk_parts, t_parts)):
                            ins = pe.matmul(ps[:, 4 + m, 0:KN], wt[:, c, g * P:(g + 1) * P],
                                            x[:, c, m * KN:(m + 1) * KN],
                                            start=(c == 0 and y == 0), stop=(c == DC - 1 and y == 2))
                    ins.then_inc(kt_mm, 1)

            def values(b, t):
                if t == 0:
                    pe.wait_ge(sum_kept, Z + b)
                pe.wait_ge(v_sb, Z + 2 * (KT2 * b + t // 2))
                for x in range(2):
                    for c in range(DC):
                        for y, (xt, wt) in enumerate(split(t_parts, wv_parts)):
                            ins = pe.matmul(ps[0:KP, 3, x * D:(x + 1) * D],
                                            xt[:, c, (t + x) * KP:(t + x + 1) * KP], wt[:, c, :],
                                            start=(c == 0 and y == 0), stop=(c == DC - 1 and y == 2))
                ins.then_inc(v_mm, 1)

            def features(b, t):
                for g in range(2):
                    m = 2 * t + g
                    if m < 3:
                        pe.wait_ge(k_lo_ready, Z + 6 * (b + 1))
                    else:
                        pe.wait_ge(feat_dve if m % 2 == 0 else feat_act, Z + KT * b + (m - 3) // 2 + 1)
                    for y, (k, wt) in enumerate(split(k_parts, wf_parts)):
                        ins = pe.matmul(ps[0:KP, 4 + m % 3, :], k[:, g, t * KP:(t + 1) * KP], wt[:, :],
                                        start=(y == 0), stop=(y == 2))
                    ins.then_inc(feat_mm, 1)

            def add_sums(b, t):
                pe.wait_ge(feat_act, Z + KT * b + t + 1)
                pe.wait_ge(feat_dve, Z + KT * b + t + 1)
                pe.wait_ge(v_sb, Z + 2 * (KT2 * b + t // 2 + 1))
                for p in range(HP):
                    r = (p % 2) * SP
                    ins = pe.matmul(ps[r:r + VW, 7, (p // 2) * P:(p // 2 + 1) * P], v_aug[:, t // 2 % 2, t % 2, p, :],
                                    feat[:, t % 2, p // 4, (p % 4) * P:(p % 4 + 1) * P],
                                    start=False, stop=False, skip_group_check=True)
                ins.then_inc(sum_mm, 1)

            def turn_sums(b):
                pe.wait_ge(sum_sb, Z + b + 1)
                for q in range(HP // 2):
                    ins = pe.transpose(ps[:, 3, q * P:(q + 1) * P], sums_sb[:, q * P:(q + 1) * P],
                                       core.ident[:, :])
                ins.then_inc(sum_turned, 1)

            def sequence(b):
                keys(b)
                pe.wait_ge(sum_sb, Z + b)
                pe.matmul(ps[:, 7, :], zero[0:1, 0:P], zero[0:1, :], start=True, stop=True,
                          skip_group_check=True)
                for t in range(KT + 1):
                    if t < KT:
                        if t % 2 == 0:
                            values(b, t)
                        features(b, t)
                    if t >= 1:
                        add_sums(b, t - 1)

            with pe.Fori(0, PAIRS) as n:
                scores(n)
                sequence(2 * n)
                attend(n)
                sequence(2 * n + 1)
                turn_sums(2 * n + 1)

        @block.scalar
        def _(act):
            for s in (exped, turned_sb, t_hi_ready, k_hi_ready, feat_act, sum_sb):
                act.sem_inc(s, Z)

            def split_context(b, n, k):
                act.wait_ge(v_mm, Z + KT2 * b)
                act.wait_ge(t_in[k], DMA * (n + 1))
                for c in range(DC):
                    act.copy(t_hi[:, c, :], ctx_t[:, k, c, :]).then_inc(t_hi_ready, 1)
            core.ln_scalar(act, k_ln)
            split_context(0, 0, 0)
            act.wait_ge(w_in, n_in)
            for full, hi, _lo in w_splits:
                act.copy(hi, full).then_inc(w_hi_ready, 1)

            def exp(n):
                act.wait_ge(maxed, Z + n + 1)
                act.activation(prob[:, :], prob[:, :], ACT.Exp, bias=neg_max[:, 0:1],
                               accum_out=sums[:, 0:1]).then_inc(exped, 1)

            def sequence(b, after_keys=None):
                for e in range(6):
                    act.wait_ge(kt_mm, Z + 6 * b + e + 1)
                    act.activation(k_hi[:, e // 3, (e % 3) * KN:(e % 3 + 1) * KN], ps[:, 4 + e % 3, 0:KN],
                                   ACT.Identity, bias=b_k[:, e // 3:e // 3 + 1]).then_inc(k_hi_ready, 1)
                if after_keys:
                    after_keys()
                for t in range(KT):
                    act.wait_ge(sum_mm, Z + KT * b + t - 1)
                    act.wait_ge(feat_mm, Z + 2 * (KT * b + t) + 1)
                    act.activation(feat[:, t % 2, 0, :], ps[0:KP, 4 + (2 * t) % 3, :], ACT.Relu) \
                        .then_inc(feat_act, 1)
                act.wait_ge(sum_mm, Z + KT * (b + 1))
                act.wait_ge(sum_turned, Z + b)
                act.copy(sums_sb[:, :], ps[:, 7, :]).then_inc(sum_sb, 1)

            def pair(n, last):
                sequence(2 * n, after_keys=lambda: exp(n))
                for u in range(3):
                    act.wait_ge(turned, Z + 3 * n + u + 1)
                    act.copy(prob_t[:, 4 * u:4 * u + 4, :].rearrange("p t q -> p (t q)"),
                             ps[0:KP, u % 2, :]).then_inc(turned_sb, 1)
                split_context(2 * n + 1, n, 1)
                sequence(2 * n + 1)
                if not last:
                    split_context(2 * n + 2, n + 1, 0)
            with act.Fori(0, PAIRS - 1) as n:
                pair(n, last=False)
            pair(PAIRS - 1, last=True)

        @block.vector
        def _(dve):
            link = InOrder(dve, core.dve_step, dve0)
            for s in (maxed, mask_read, added, t_lo_ready, k_lo_ready, v_sb, feat_dve, sum_kept):
                dve.sem_inc(s, Z)
            core.ln_vector(dve, link, k_ln)
            link(dve.memset(zero[:, :], 0.0))
            link(dve.memset(kv_sums[:, :, :, :], 0.0))

            def split_context(b, k):
                for c in range(DC):
                    dve.wait_ge(t_hi_ready, Z + DC * b + c + 1)
                    dve.tensor_tensor(t_lo[:, c, :], ctx_t[:, k, c, :], t_hi[:, c, :].bitcast(F32),
                                      ALU.subtract).then_inc(t_lo_ready, 1)
            split_context(0, 0)
            for y, (full, hi, lo) in enumerate(w_splits):
                dve.wait_ge(w_hi_ready, y + 1)
                dve.tensor_tensor(lo, full, hi.bitcast(F32), ALU.subtract).then_inc(w_lo_ready, 1)

            def mask_scores(n):
                dve.wait_ge(mask_in, 2 * DMA * (n + 1))
                dve.tensor_scalar(mask_add[:, :], mask_u8[:, :].bitcast(U8), 1.0, -NEG, ALU.subtract, ALU.mult) \
                    .then_inc(mask_read, 1)
                dve.wait_ge(mask_read, Z + n + 1)
                link(dve.tensor_reduce(any_key[:, :], mask_add[:, :], AXIS.X, ALU.max))
                link(dve.tensor_scalar(any_key[:, :], any_key[:, :], 0.0, None, ALU.is_equal))
                dve.wait_ge(score_mm, Z + n + 1)
                dve.wait_ge(turned, Z + 3 * n)
                link(dve.scalar_tensor_tensor(prob[:, :].rearrange("p (m n) -> p m n", m=3), ps[:, 0:3, 0:KN],
                                              1.0 / 16.0, mask_add[:, :].rearrange("p (m n) -> p m n", m=3),
                                              ALU.mult, ALU.add))

            def row_max():
                dve.tensor_reduce(neg_max[:, :], prob[:, :], AXIS.X, ALU.max, negate=True).then_inc(maxed, 1)

            def add_out(n):
                dve.wait_ge(exped, Z + n + 1)
                link(dve.reciprocal(inv[:, :], sums[:, :]))
                link(dve.tensor_tensor(inv[:, :], inv[:, :], any_key[:, :], ALU.mult))
                dve.wait_ge(out_mm, Z + n + 1)
                row = core.x_rows[:, bass.ds(n, 1), :].rearrange("p a d -> p (a d)")
                dve.scalar_tensor_tensor(row, ps[:, 2, 0:D], inv[:, 0:1], row,
                                         ALU.mult, ALU.add).then_inc(added, 1)

            def sequence(b, after_three_keys=None):
                dve.wait_ge(v_sb, Z + 2 * KT2 * b)
                link(dve.tensor_copy(mask_now[:, :], mask2[:, bass.ds(b, 1), :].rearrange("p a t -> p (a t)")))
                for e in range(6):
                    dve.wait_ge(k_hi_ready, Z + 6 * b + e + 1)
                    at = slice((e % 3) * KN, (e % 3 + 1) * KN)
                    dve.scalar_tensor_tensor(k_lo[:, e // 3, at], ps[:, 4 + e % 3, 0:KN],
                                             b_k[:, e // 3:e // 3 + 1], k_hi[:, e // 3, at].bitcast(F32),
                                             ALU.add, ALU.subtract).then_inc(k_lo_ready, 1)
                    if e == 2 and after_three_keys:
                        after_three_keys()
                for t in range(KT):
                    slot = t // 2 % 2
                    dve.wait_ge(sum_mm, Z + KT * b + t - 1)
                    if t % 2 == 0:
                        dve.wait_ge(v_mm, Z + KT2 * b + t // 2 + 1)
                        dve.tensor_tensor(v_aug[:, slot, :, :, 0:2 * HD2],
                                          ps[0:KP, 3, :].rearrange("p (x h e) -> p x h e", x=2, h=HP),
                                          mask_now[:, t:t + 2].unsqueeze(2).unsqueeze(3)
                                          .to_broadcast([KP, 2, HP, 2 * HD2]), ALU.mult).then_inc(v_sb, 1)
                        dve.tensor_copy(v_aug[:, slot, :, :, 2 * HD2],
                                        mask_now[:, t:t + 2].unsqueeze(2).to_broadcast([KP, 2, HP])) \
                            .then_inc(v_sb, 1)
                    dve.wait_ge(feat_mm, Z + 2 * (KT * b + t) + 2)
                    dve.tensor_scalar(feat[:, t % 2, 1, :], ps[0:KP, 4 + (2 * t + 1) % 3, :], 0.0, None,
                                      ALU.max).then_inc(feat_dve, 1)
                dve.wait_ge(sum_turned, Z + b + 1)
                turned_sums = ps[:, 3, :].rearrange("p (h w) -> p h w", w=SP)
                dst = kv_sums[:, bass.ds(b, 1), :, :].rearrange("p a h w -> p (a h) w")
                lo, hi = slice(0, FD2), slice(FD2, P)
                link(dve.tensor_copy(dst[lo, :, 0:HD2], turned_sums[lo, :, 0:HD2]))
                link(dve.tensor_copy(dst[hi, :, HD2:2 * HD2], turned_sums[hi, :, HD2:2 * HD2]))
                link(dve.tensor_copy(dst[lo, :, 2 * HD2], turned_sums[lo, :, 2 * HD2]))
                dve.tensor_copy(dst[hi, :, 2 * HD2 + 1], turned_sums[hi, :, 2 * HD2]).then_inc(sum_kept, 1)

            def pair(n, last):
                mask_scores(n)
                sequence(2 * n, after_three_keys=row_max)
                split_context(2 * n + 1, 1)
                add_out(n)
                sequence(2 * n + 1)
                if not last:
                    split_context(2 * n + 2, 0)
            first, per_pair = link.n, 3 + 2 + 2 * (1 + 3)
            with dve.Fori(0, PAIRS - 1) as n:
                link.loop(n, first, per_pair)
                pair(n, last=False)
            link.end(first, per_pair, PAIRS - 1)
            pair(PAIRS - 1, last=True)
            core.dve_n = link.n


def linear_attention(core):
    nc, dram, ps = core.nc, core.dram, core.psum
    k_ln = core.new_norm()
    dve0 = core.dve_n
    ctx = ExitStack()
    with ctx:
        def sb(name, shape, dt=F32):
            return ctx.enter_context(nc.sbuf_tensor("l_" + name, shape, dt))
        w_q = sb("w_q", [P, DC, D])
        w_o = sb("w_o", [P, DC, D])
        w_qf = sb("w_qf", [P, FG])
        b_q = sb("b_q", [P, 2])
        b_v = sb("b_v", [P, D])
        b_o = sb("b_o", [P, D])
        q_t = sb("q_t", [P, 2, T])
        feat_t = sb("feat_t", [P, HP, T])
        den = sb("den", [P, PAIRS, NH2])
        vals = sb("vals", [P, PAIRS, D])
        bias = sb("bias", [P, PAIRS, D])
        vals_t = sb("vals_t", [P, DC, T])
        sem = core.sem
        w_in, q_mm, q_sb, feat_mm, feat_sb, att_mm, divided, turned, turned_sb, out_mm = (sem("l_" + n) for n in (
            "weights_in", "q_mm", "q_sb", "feat_mm", "feat_sb", "att_mm", "divided", "turned", "turned_sb",
            "out_mm"))
        loads = ((w_q[:, :, :], "l_w_q"), (w_o[:, :, :], "l_w_o"), (w_qf[:, :], "l_w_qf"), (b_q[:, :], "l_b_q"))
        block = ctx.enter_context(nc.Block())

        @block.sync
        def _(sp):
            for dst, src in loads:
                sp.dma_start(dst, dram[src]).then_inc(w_in, DMA)
            sp.dma_start(b_v[:, :], dram["l_b_v"].partition_broadcast(P)).then_inc(w_in, DMA)
            sp.dma_start(b_o[:, :], dram["l_b_o"].partition_broadcast(P)).then_inc(w_in, DMA)
        n_in = DMA * (len(loads) + 2)

        @block.gpsimd
        def _(pool):
            core.ln_pool(pool, k_ln)

        @block.tensor
        def _(pe):
            core.ln_tensor(pe, k_ln)
            pe.wait_ge(core.ln_cols, core.cols_ready(k_ln))
            pe.wait_ge(w_in, n_in)
            for g in range(2):
                for c in range(DC):
                    ins = pe.matmul(ps[:, 2 + g, :], w_q[:, c, g * P:(g + 1) * P], core.xn_cols[:, c, :],
                                    start=(c == 0), stop=(c == DC - 1))
                ins.then_inc(q_mm, 1)
            for p in range(HP):
                if p % 4 == 0:
                    pe.wait_ge(q_sb, p // 4 + 1)
                if p >= 4:
                    pe.wait_ge(feat_sb, p - 3)
                pe.matmul(ps[:, 4 + p % 4, :], w_qf[:, (p % 4) * P:(p % 4 + 1) * P], q_t[:, p // 4, :],
                          start=True, stop=True).then_inc(feat_mm, 1)
            pe.wait_ge(feat_sb, HP)
            for b in range(B):
                for p in range(HP):
                    ins = pe.matmul(ps[(b % 2) * SP:(b % 2 + 1) * SP, b // 2, p * BW:(p + 1) * BW],
                                    feat_t[:, p, b * SP:(b + 1) * SP], core.kv_sums[:, b, p, :],
                                    start=True, stop=True)
                if b % 2:
                    ins.then_inc(att_mm, 1)
            for i in range(PAIRS):
                pe.wait_ge(divided, i + 1)
                for c in range(DC):
                    ins = pe.transpose(ps[:, 4 + c, i * P:(i + 1) * P], vals[:, i, c * P:(c + 1) * P],
                                       core.ident[:, :])
            ins.then_inc(turned, 1)
            pe.wait_ge(turned_sb, DC)
            for i in range(PAIRS):
                for c in range(DC):
                    ins = pe.matmul(ps[:, 6 + i // 2, (i % 2) * D:(i % 2 + 1) * D],
                                    vals_t[:, c, i * P:(i + 1) * P], w_o[:, c, :],
                                    start=(c == 0), stop=(c == DC - 1))
                if i % 2:
                    ins.then_inc(out_mm, 1)

        @block.scalar
        def _(act):
            core.ln_scalar(act, k_ln)
            act.wait_ge(w_in, n_in)
            for g in range(2):
                act.wait_ge(q_mm, g + 1)
                act.activation(q_t[:, g, :], ps[:, 2 + g, :], ACT.Identity, bias=b_q[:, g:g + 1]) \
                    .then_inc(q_sb, 1)
            for p in range(HP):
                act.wait_ge(feat_mm, p + 1)
                act.activation(feat_t[:, p, :], ps[:, 4 + p % 4, :], ACT.Relu).then_inc(feat_sb, 1)
            act.wait_ge(turned, 1)
            for c in range(DC):
                act.copy(vals_t[:, c, :], ps[:, 4 + c, :]).then_inc(turned_sb, 1)

        @block.vector
        def _(dve):
            link = InOrder(dve, core.dve_step, dve0)
            core.ln_vector(dve, link, k_ln)
            dve.wait_ge(w_in, n_in)
            for i in range(PAIRS):
                dve.wait_ge(att_mm, i + 1)
                got = ps[:, i, 0:HP * BW].rearrange("p (h w) -> p h w", w=BW)
                row = vals[:, i, :].rearrange("p (h e) -> p h e", e=HD2)
                bias_row = bias[:, i, :].rearrange("p (h e) -> p h e", e=HD2)
                each = den[:, i, :].rearrange("p (h k) -> p h k", k=2)
                link(dve.tensor_copy(each, got[:, :, 2 * HD2:BW]))
                link(dve.tensor_tensor(bias_row, b_v[:, :].rearrange("p (h e) -> p h e", e=HD2),
                                       den[:, i, :].unsqueeze(2).to_broadcast([P, NH2, HD2]), ALU.mult))
                link(dve.tensor_tensor(vals[:, i, :].rearrange("p (h e) -> p h e", h=HP),
                                       bias[:, i, :].rearrange("p (h e) -> p h e", h=HP),
                                       got[:, :, 0:2 * HD2], ALU.add))
                link(dve.tensor_scalar(den[:, i, :], den[:, i, :], 1e-8, None, ALU.add))
                link(dve.reciprocal(den[:, i, :], den[:, i, :]))
                dve.tensor_tensor(row, row, den[:, i, :].unsqueeze(2).to_broadcast([P, NH2, HD2]),
                                  ALU.mult).then_inc(divided, 1)
            for i in range(PAIRS):
                link(dve.tensor_tensor(core.x_rows[:, i, :], core.x_rows[:, i, :], b_o[:, :], ALU.add))
            for a in range(2):
                dve.wait_ge(out_mm, a + 1)
                rows = core.x_rows[:, 2 * a:2 * a + 2, :].rearrange("p i d -> p (i d)")
                link(dve.tensor_tensor(rows, rows, ps[:, 6 + a, :], ALU.add))
            core.dve_n = link.n


FF2 = 704
FT2 = -(-FF2 // P)
FP8_MAX = 448.0
GLOBAL_DIV = 448.0 * 6.0
EXPONENT = 0x7F800000
FP8_LEAST = 2.0 ** -6
FP8_ROUND = 1.5 * 2.0 ** 20


FP8_TILES = 2 * FT2 + DC


def fp8_scales(eng, link, peak, scale, inv):
    link(eng.tensor_scalar(scale, peak, 1.0 / FP8_MAX, 1e-30, ALU.mult, ALU.max))
    link(eng.reciprocal(inv, scale))


class Fp8Weights:

    def __init__(self, core, ctx):
        def sb(name, shape, dt=F32):
            return ctx.enter_context(core.nc.sbuf_tensor("q_" + name, shape, dt))
        self.core = core
        self.order = sb("order", [P, FT2], I32)
        self.rows = sb("w_rows", [P, 2, FT2, D])
        self.down = sb("wd_rows", [P, DC, FF2])
        self.peak = sb("peak", [P, FP8_TILES])
        self.scale = sb("w_scale", [P, FP8_TILES])
        self.inv = sb("w_inv", [P, FP8_TILES])
        self.rows_unit = sb("w_rows_unit", [P, 2, FT2, D])
        self.down_unit = sb("wd_rows_unit", [P, DC, FF2])
        self.rows_hi = sb("w_rows_hi", [P, 2, FT2, D], F32R)
        self.down_hi = sb("wd_rows_hi", [P, DC, FF2], F32R)
        self.groups = ((self.rows[:, :, :, :].rearrange("p k f d -> p (k f) d"),
                        self.rows_unit[:, :, :, :].rearrange("p k f d -> p (k f) d"),
                        self.rows_hi[:, :, :, :].rearrange("p k f d -> p (k f) d"), slice(0, 2 * FT2)),
                       (self.down[:, :, :], self.down_unit[:, :, :], self.down_hi[:, :, :],
                        slice(2 * FT2, FP8_TILES)))

    def load(self, sp):
        core = self.core
        sp.dma_start(self.order[:, :], core.dram["q_order"]).then_inc(core.fp8_order_in, DMA)
        sp.dma_start(self.down[:, :, :], core.dram["q_w_down"]).then_inc(core.fp8_down_in, DMA)

    def gather(self, pool):
        core = self.core
        pool.wait_ge(core.fp8_order_in, DMA)
        for k, src in enumerate(("q_w_gate", "q_w_up")):
            for f in range(FT2):
                pool.indirect_dma_start(self.rows[:, k, f, :], None, core.dram[src],
                                        bass.IndirectOffsetOnAxis(ap=self.order[:, f:f + 1], axis=0)) \
                    .then_inc(core.fp8_rows_in, DMA)

    def find_scales(self, dve, link):
        core = self.core
        dve.wait_ge(core.fp8_rows_in, DMA * 2 * FT2)
        dve.wait_ge(core.fp8_down_in, DMA)
        for w, _unit, _hi, which in self.groups:
            link(dve.tensor_reduce(self.peak[:, which], w, AXIS.X, ALU.max, apply_absolute_value=True))
        fp8_scales(dve, link, self.peak[:, :], self.scale[:, :], self.inv[:, :])

    def scale_tile(self, dve, link, tile):
        w, unit, _hi, _which = self.groups[0]
        one = bass.ds(tile, 1)
        link(dve.tensor_tensor(w[:, one, :], w[:, one, :],
                               self.inv[:, one].unsqueeze(2).to_broadcast([P, 1, D]), ALU.mult))
        dve.tensor_scalar(unit[:, one, :].bitcast(U32), w[:, one, :].bitcast(U32), EXPONENT, None,
                          ALU.bitwise_and).then_inc(self.core.fp8_exponents, 1)

    def divide(self, dve, link, group):
        w, _unit, _hi, which = self.groups[group]
        link(dve.tensor_tensor(w, w, self.inv[:, which].unsqueeze(2).to_broadcast(list(w.shape)), ALU.mult))

    def find_exponents(self, dve, group):
        w, unit, _hi, _which = self.groups[group]
        dve.tensor_scalar(unit.bitcast(U32), w.bitcast(U32), EXPONENT, None, ALU.bitwise_and) \
            .then_inc(self.core.fp8_exponents, 1)

    def round(self, pool, link):
        core = self.core
        for g, (w, unit, hi, which) in ((1, self.groups[1]), (0, self.groups[0])):
            pool.wait_ge(core.fp8_exponents, 1 if g == 1 else 1 + 2 * FT2)
            link(pool.tensor_scalar(unit, unit, FP8_LEAST, FP8_ROUND, ALU.max, ALU.mult))
            link(pool.tensor_tensor(w, w, unit, ALU.add))
            link(pool.tensor_tensor(w, w, unit, ALU.subtract))
            link(pool.tensor_tensor(w, w, self.scale[:, which].unsqueeze(2).to_broadcast(list(w.shape)), ALU.mult))
            link(pool.tensor_copy(hi, w))
            pool.tensor_tensor(unit, w, hi.bitcast(F32), ALU.subtract).then_inc(core.fp8_rounded, 1)


def quantised_ffn(core):
    nc, dram, ps = core.nc, core.dram, core.psum
    k_ln = core.new_norm(turned=False)
    dve0, pool0 = core.dve_n, core.pool_n
    ctx = ExitStack()
    with ctx:
        def sb(name, shape, dt=F32):
            return ctx.enter_context(nc.sbuf_tensor("q_" + name, shape, dt))
        fp8 = core.fp8_weights
        w_parts = (fp8.rows_hi[:, :, :, :].bitcast(F32), fp8.rows_unit[:, :, :, :])
        wd_parts = (fp8.down_hi[:, :, :].bitcast(F32), fp8.down_unit[:, :, :])
        w_cols = sb("w_cols", [P, 2, 2, DC, FT2 * P], F32R)
        wd_cols = sb("wd_cols", [P, 2, FT2, D], F32R)
        x_unit = sb("x_unit", [P, PAIRS, D])
        unit = sb("unit", [P, FF2])
        row_peak = sb("row_peak", [P, PAIRS])
        all_peak = sb("all_peak", [P, 4])
        row_scale = sb("row_scale", [P, PAIRS])
        row_inv = sb("row_inv", [P, PAIRS])
        x_scale = sb("x_scale", [P, PAIRS])
        hid_scale = sb("hid_scale", [P, PAIRS])
        row_peak2 = sb("row_peak2", [P, PAIRS])
        all_peak2 = sb("all_peak2", [P, 4])
        row_scale2 = sb("row_scale2", [P, PAIRS])
        row_inv2 = sb("row_inv2", [P, PAIRS])
        xq = sb("xq", [P, PAIRS, D])
        xq_cols = sb("xq_cols", [P, DC, T], F32R)
        silu = sb("silu", [P, 2, FF2])
        hid = sb("hid", [P, PAIRS, FF2])
        hid_cols = sb("hid_cols", [P, 2, FT2, P], F32R)
        sem = core.sem
        (w_turned, w_cols_ready, peak_known, peak_all, x_quant, x_turned,
         x_cols_ready, up_mm, silued, hid_ready, peak2_known, peak2_all, hid_quant, hid_turned, hid_cols_ready,
         out_mm, row_scales) = (sem("q_" + n) for n in (
            "w_turned", "w_cols_ready", "peak_known", "peak_all",
            "x_quant", "x_turned", "x_cols_ready", "up_mm", "silued", "hid_ready", "peak2_known", "peak2_all",
            "hid_quant", "hid_turned", "hid_cols_ready", "out_mm", "row_scales"))
        block = ctx.enter_context(nc.Block())
        half = FF2 // 2

        @block.gpsimd
        def _(pool):
            core.ln_pool(pool, k_ln)
            pool.wait_ge(peak_known, 1)
            pool.partition_all_reduce(all_peak[:, 1:2], all_peak[:, 0:1], P, REDUCE.max).then_inc(peak_all, 1)
            pool.wait_ge(peak2_known, 1)
            pool.partition_all_reduce(all_peak2[:, 1:2], all_peak2[:, 0:1], P, REDUCE.max).then_inc(peak2_all, 1)

        @block.tensor
        def _(pe):
            n = 0
            pe.wait_ge(core.fp8_rounded, 2)
            for k in range(2):
                for f in range(FT2):
                    if n >= 6:
                        pe.wait_ge(w_cols_ready, n - 5)
                    for m, part in enumerate(w_parts):
                        for c in range(DC):
                            ins = pe.transpose(ps[:, 2 + n % 6, m * D + c * P:m * D + (c + 1) * P],
                                               part[:, k, f, c * P:(c + 1) * P], core.ident[:, :])
                    ins.then_inc(w_turned, 1)
                    n += 1
            for f in range(FT2):
                w = min(P, FF2 - f * P)
                pe.wait_ge(w_cols_ready, n - 5)
                for m, part in enumerate(wd_parts):
                    for c in range(DC):
                        ins = pe.transpose(ps[0:w, 2 + n % 6, m * D + c * P:m * D + (c + 1) * P],
                                           part[:, c, f * P:f * P + w], core.ident[:, :])
                ins.then_inc(w_turned, 1)
                n += 1
            for i in range(PAIRS):
                pe.wait_ge(x_quant, i + 1)
                for c in range(DC):
                    ins = pe.transpose(ps[:, c, i * P:(i + 1) * P], xq[:, i, c * P:(c + 1) * P], core.ident[:, :])
            ins.then_inc(x_turned, 1)
            pe.wait_ge(x_cols_ready, DC)
            pe.wait_ge(w_cols_ready, 3 * FT2)
            for i in range(PAIRS):
                if i >= 2:
                    pe.wait_ge(hid_ready, i - 1)
                for k in range(2):
                    for a in range(2):
                        for c in range(DC):
                            for m in range(2):
                                ins = pe.matmul(ps[:, 4 * (i % 2) + 2 * k + a, 0:half],
                                                xq_cols[:, c, i * P:(i + 1) * P],
                                                w_cols[:, m, k, c, a * half:(a + 1) * half],
                                                start=(c == 0 and m == 0), stop=(c == DC - 1 and m == 1))
                ins.then_inc(up_mm, 1)
            pe.wait_ge(hid_ready, PAIRS)
            for i in range(PAIRS):
                pe.wait_ge(hid_quant, i + 1)
                if i >= 2:
                    pe.wait_ge(hid_cols_ready, 2 * (i - 1))
                for f in range(FT2):
                    w = min(P, FF2 - f * P)
                    ins = pe.transpose(ps[0:w, 2 * (i % 2) + f // 4, (f % 4) * P:(f % 4 + 1) * P],
                                       hid[:, i, f * P:f * P + w], core.ident[:, :])
                ins.then_inc(hid_turned, 1)
                pe.wait_ge(hid_cols_ready, 2 * (i + 1))
                for f in range(FT2):
                    w = min(P, FF2 - f * P)
                    for m in range(2):
                        ins = pe.matmul(ps[:, 6 + i // 2, (i % 2) * D:(i % 2 + 1) * D], hid_cols[0:w, i % 2, f, :],
                                        wd_cols[0:w, m, f, :], start=(f == 0 and m == 0),
                                        stop=(f == FT2 - 1 and m == 1))
                if i % 2:
                    ins.then_inc(out_mm, 1)

        @block.scalar
        def _(act):
            n = 0
            for k in range(2):
                for f in range(FT2):
                    act.wait_ge(w_turned, n + 1)
                    act.copy(w_cols[:, :, k, :, f * P:(f + 1) * P],
                             ps[:, 2 + n % 6, :].rearrange("p (m c d) -> p m c d", m=2, c=DC)) \
                        .then_inc(w_cols_ready, 1)
                    n += 1
            for f in range(FT2):
                w = min(P, FF2 - f * P)
                act.wait_ge(w_turned, n + 1)
                act.copy(wd_cols[0:w, :, f, :], ps[0:w, 2 + n % 6, :].rearrange("p (m d) -> p m d", m=2)) \
                    .then_inc(w_cols_ready, 1)
                n += 1
            act.wait_ge(x_turned, 1)
            for c in range(DC):
                act.copy(xq_cols[:, c, :], ps[:, c, :]).then_inc(x_cols_ready, 1)
            act.wait_ge(row_scales, 1)
            for i in range(PAIRS):
                act.wait_ge(up_mm, i + 1)
                if i >= 2:
                    act.wait_ge(hid_ready, i - 1)
                act.activation(silu[:, i % 2, :].rearrange("p (a n) -> p a n", a=2),
                               ps[:, 4 * (i % 2):4 * (i % 2) + 2, 0:half], ACT.Silu,
                               scale=x_scale[:, i:i + 1]).then_inc(silued, 1)
            for i in range(PAIRS):
                act.wait_ge(hid_turned, i + 1)
                b = 2 * (i % 2)
                act.copy(hid_cols[:, i % 2, 0:4, :].rearrange("p f n -> p (f n)"), ps[:, b, :]) \
                    .then_inc(hid_cols_ready, 1)
                act.copy(hid_cols[:, i % 2, 4, :], ps[:, b + 1, 0:P]).then_inc(core.act_step, 1)
                act.copy(hid_cols[0:FF2 % P, i % 2, 5, :], ps[0:FF2 % P, b + 1, P:2 * P]) \
                    .then_inc(hid_cols_ready, 1)

        @block.vector
        def _(dve):
            link = InOrder(dve, core.dve_step, dve0)

            core.ln_vector(dve, link, k_ln)
            dve.wait_ge(core.ln_rows, PAIRS * (k_ln + 1))

            def exponents(v, e):
                link(dve.tensor_scalar(e.bitcast(U32), v.bitcast(U32), EXPONENT, None, ALU.bitwise_and))
                link(dve.tensor_scalar(e, e, FP8_LEAST, FP8_ROUND, ALU.max, ALU.mult))

            def global_scale(rows_peak, g, known, reduced):
                link(dve.tensor_reduce(g[:, 0:1], rows_peak[:, :], AXIS.X, ALU.max))
                known_ins = dve.tensor_copy(g[:, 3:4], g[:, 0:1])
                known_ins.then_inc(known, 1)
                dve.wait_ge(reduced, 1)
                link(dve.tensor_scalar(g[:, 2:3], g[:, 1:2], 1.0 / GLOBAL_DIV, 1e-30, ALU.mult, ALU.max))
                link(dve.reciprocal(g[:, 3:4], g[:, 2:3]))
                link(dve.tensor_scalar(rows_peak[:, :], rows_peak[:, :], g[:, 3:4], None, ALU.mult))

            link(dve.tensor_reduce(row_peak[:, :], core.xn_rows[:, :, :], AXIS.X, ALU.max,
                                   apply_absolute_value=True))
            global_scale(row_peak, all_peak, peak_known, peak_all)
            fp8_scales(dve, link, row_peak[:, :], row_scale[:, :], row_inv[:, :])
            for i in range(PAIRS):
                ins = dve.tensor_scalar(xq[:, i, :], core.xn_rows[:, i, :], all_peak[:, 3:4], row_inv[:, i:i + 1],
                                        ALU.mult, ALU.mult)
            link(ins)
            exponents(xq[:, :, :], x_unit[:, :, :])
            link(dve.tensor_tensor(xq[:, :, :], xq[:, :, :], x_unit[:, :, :], ALU.add))
            for i in range(PAIRS):
                dve.tensor_tensor(xq[:, i, :], xq[:, i, :], x_unit[:, i, :], ALU.subtract).then_inc(x_quant, 1)
            dve.tensor_scalar(x_scale[:, :], row_scale[:, :], all_peak[:, 2:3], None, ALU.mult) \
                .then_inc(row_scales, 1)
            dve.wait_ge(row_scales, 1)
            for i in range(PAIRS):
                dve.wait_ge(silued, i + 1)
                dve.scalar_tensor_tensor(hid[:, i, :].rearrange("p (a n) -> p a n", a=2),
                                         ps[:, 4 * (i % 2) + 2:4 * (i % 2) + 4, 0:half], x_scale[:, i:i + 1],
                                         silu[:, i % 2, :].rearrange("p (a n) -> p a n", a=2),
                                         ALU.mult, ALU.mult).then_inc(hid_ready, 1)
                dve.wait_ge(hid_ready, i + 1)
                link(dve.tensor_reduce(row_peak2[:, i:i + 1], hid[:, i, :], AXIS.X, ALU.max,
                                       apply_absolute_value=True))
            global_scale(row_peak2, all_peak2, peak2_known, peak2_all)
            fp8_scales(dve, link, row_peak2[:, :], row_scale2[:, :], row_inv2[:, :])
            for i in range(PAIRS):
                link(dve.tensor_scalar(hid[:, i, :], hid[:, i, :], all_peak2[:, 3:4], row_inv2[:, i:i + 1],
                                       ALU.mult, ALU.mult))
                exponents(hid[:, i, :], unit[:, :])
                link(dve.tensor_tensor(hid[:, i, :], hid[:, i, :], unit[:, :], ALU.add))
                dve.tensor_tensor(hid[:, i, :], hid[:, i, :], unit[:, :], ALU.subtract).then_inc(hid_quant, 1)
                dve.wait_ge(hid_quant, i + 1)
            link(dve.tensor_scalar(hid_scale[:, :], row_scale2[:, :], all_peak2[:, 2:3], None, ALU.mult))
            for i in range(PAIRS):
                dve.wait_ge(out_mm, i // 2 + 1)
                row = core.x_rows[:, i, :]
                ins = dve.scalar_tensor_tensor(row, ps[:, 6 + i // 2, (i % 2) * D:(i % 2 + 1) * D],
                                               hid_scale[:, i:i + 1], row, ALU.mult, ALU.add)
            link(ins)
            core.dve_n = link.n


RT = H * S // P
WS = 4


def full_attention(core):
    nc, dram, ps = core.nc, core.dram, core.psum
    k_ln = core.new_norm()
    dve0, Z = core.dve_n, AHEAD
    ctx = ExitStack()
    with ctx:
        def sb(name, shape, dt=F32):
            return ctx.enter_context(nc.sbuf_tensor("a_" + name, shape, dt))
        w = sb("w", [P, WS, 2 * D])
        head_hi = sb("head_hi", [P, 2, T], F32R)
        head_lo = sb("head_lo", [P, 2, T], F32R)
        q_all = sb("q_all", [P, DC, B, H * S])
        q_tile = sb("q_tile", [P, 2, DC, P])
        q_hi = sb("q_hi", [P, 2, DC, P], F32R)
        q_lo = sb("q_lo", [P, 2, DC, P], F32R)
        raw = sb("raw", [P, KT * D])
        t_hi = sb("t_hi", [P, 2, DC, LK], F32R)
        t_lo = sb("t_lo", [P, 2, DC, LK], F32R)
        r_hi = sb("r_hi", [KP, KT, D], F32R)
        r_lo = sb("r_lo", [KP, KT, D], F32R)
        neg_max = sb("neg_max", [P, 2])
        sums = sb("sums", [P, 2])
        inv = sb("inv", [P, 2])
        prob = sb("prob", [P, 2, LK])
        p_store = sb("p_store", [P, 2, KT * P], F32R)
        mixed = sb("mixed", [P, 2, D])
        zero = sb("zero", [1, 512])
        p_hi, p_lo = (p_store[0:KP, k, :].rearrange("p (t n) -> p t n", t=KT) for k in range(2))
        x_parts = x_hi, x_lo = tuple(p_store[:, k, 0:DC * T].rearrange("p (c n) -> p c n", c=DC) for k in range(2))
        w_parts = w_hi, w_lo = tuple(
            t[:, 1, :, :].rearrange("p c k -> p (c k)")[:, 0:WS * 2 * D].rearrange("p (s n) -> p s n", s=WS)
            for t in (t_hi, t_lo))
        head_parts = (head_hi, head_lo)
        sem = core.sem
        w_in = [sem(f"a_w_in{s}") for s in range(WS)]
        names = ("raw_in", "t_hi_ready", "t_lo_ready", "r_hi_ready", "r_lo_ready", "head_mm",
                 "x_lo_ready", "w_hi_ready", "w_lo_ready", "head_hi_ready", "head_lo_ready",
                 "fold_mm", "fold_sb", "q_staged", "q_hi_ready", "q_lo_ready", "score_mm", "maxed", "exped", "turned",
                 "p_hi_ready", "p_lo_ready", "mix_mm", "mix_sb", "mix_turned", "mix_kept", "v_mm", "v_hi_ready", "v_lo_ready",
                 "out_mm",
                 "cleared")
        (raw_in, t_hi_ready, t_lo_ready, r_hi_ready, r_lo_ready, head_mm,
         x_lo_ready, w_hi_ready, w_lo_ready, head_hi_ready, head_lo_ready,
         fold_mm, fold_sb, q_staged, q_hi_ready, q_lo_ready, score_mm, maxed, exped, turned,
         p_hi_ready, p_lo_ready, mix_mm, mix_sb, mix_turned, mix_kept, v_mm, v_hi_ready, v_lo_ready,
         out_mm,
         cleared) = (
            sem("a_" + n) for n in names)
        turns = H // WS
        scale = 1.0 / float(np.sqrt(HD))
        raw_t = raw[:, 0:DC * LK].rearrange("p (c k) -> p c k", c=DC)
        raw_r = raw[0:KP, :].rearrange("p (t d) -> p t d", t=KT)

        def query_tile(i, x):
            return q_all[:, :, bass.ds(2 * i + x // RT, 1), x % RT * P:(x % RT + 1) * P] \
                .rearrange("p c b n -> p c (b n)")
        block = ctx.enter_context(nc.Block())

        @block.sync
        def _(sp):
            def weights(n, s):
                sp.dma_start(w[:, s, :], dram["a_w"][n]).then_inc(w_in[s], DMA)

            def context_turned(b):
                sp.wait_ge(r_hi_ready, Z + 3 * b)
                sp.wait_ge(r_lo_ready, Z + 3 * b)
                sp.dma_start(raw_t, dram["ctx_t"][b]).then_inc(raw_in, DMA)

            def context_rows(b):
                sp.wait_ge(t_hi_ready, Z + 2 * (b + 1))
                sp.wait_ge(t_lo_ready, Z + 2 * (b + 1))
                sp.dma_start(raw_r, dram["ctx_r"][b]).then_inc(raw_in, DMA)
            for s in range(WS):
                weights(s, s)
            context_turned(0)

            def next_weights(i):
                for s in range(WS):
                    sp.wait_ge(w_lo_ready, Z + (i - 1) * WS + s + 1)
                    weights(i * WS + s, s)
            next_weights(1)
            context_rows(0)
            with sp.Fori(2, turns) as i:
                next_weights(i)
            with sp.Fori(1, B) as b:
                context_turned(b)
                context_rows(b)
            sp.wait_ge(w_lo_ready, Z + H)
            for s in range(WS):
                weights(H + s, s)
            with sp.Fori(1, turns) as i:
                for s in range(WS):
                    sp.wait_ge(out_mm, Z + (i - 1) * WS + s + 1)
                    weights((turns + i) * WS + s, s)

        @block.gpsimd
        def _(pool):
            core.ln_pool(pool, k_ln)
            pool.sem_inc(q_staged, Z)
            pool.wait_ge(fold_sb, Z + H)
            with pool.Fori(0, PAIRS) as i:
                for x in range(2 * RT):
                    n = i * 2 * RT + x
                    pool.wait_ge(q_lo_ready, Z + n - 1)
                    pool.tensor_copy(q_tile[:, x % 2, :, :], query_tile(i, x)).then_inc(q_staged, 1)

        @block.tensor
        def _(pe):
            for x in (head_mm, fold_mm, score_mm, turned, mix_mm, mix_turned, v_mm, out_mm):
                pe.sem_inc(x, Z)
            core.ln_tensor(pe, k_ln)
            pe.wait_ge(x_lo_ready, Z + DC)

            def head(n, s):
                pe.wait_ge(w_lo_ready, Z + n + 1)
                pe.wait_ge(head_lo_ready, Z + n - 1)
                for c in range(DC):
                    for m, (wt, x) in enumerate(split(w_parts, x_parts)):
                        ins = pe.matmul(packed(ps[:, 2 + s % 2, 0:TOK]), wt[:, s, c * P:(c + 1) * P],
                                        unpad(x[:, c, :]), start=(c == 0 and m == 0), stop=(c == DC - 1 and m == 2))
                ins.then_inc(head_mm, 1)

            def fold(n, s):
                pe.wait_ge(head_lo_ready, Z + n + 1)
                pe.wait_ge(fold_sb, Z + n - 1)
                for c in range(DC):
                    for m, (wt, q) in enumerate(split(w_parts, head_parts)):
                        ins = pe.matmul(ps[:, 4 + 2 * (s % 2) + c, 0:TOK], wt[:, s, D + c * P:D + (c + 1) * P],
                                        q[:, s % 2, 0:TOK], start=(m == 0), stop=(m == 2))
                ins.then_inc(fold_mm, 1)
            head(0, 0)
            for s in range(1, WS):
                head(s, s)
                fold(s - 1, s - 1)
            with pe.Fori(1, turns) as i:
                for s in range(WS):
                    head(i * WS + s, s)
                    fold(i * WS + s - 1, (s - 1) % WS)
            fold(H - 1, WS - 1)

            def score_part(n, turn, x, k, between=None):
                b = x // RT
                if k == 0:
                    pe.wait_ge(exped, Z + n - 1)
                    pe.wait_ge(q_lo_ready, Z + n + 1)
                    if x % RT == 0:
                        pe.wait_ge(t_lo_ready, Z + 2 * (2 * turn + b + 1))
                products = [(q, t, c) for q, t in ((q_hi, t_hi), (q_hi, t_lo), (q_lo, t_hi)) for c in range(DC)]
                for m, (q, t, c) in enumerate(products):
                    if between and m == 1:
                        between()
                    ins = pe.matmul(ps[:, 3 * (x % 2) + k, 0:KN], q[:, x % 2, c, :],
                                    t[:, b, c, k * KN:(k + 1) * KN],
                                    start=(m == 0), stop=(m == len(products) - 1))
                if k == 2:
                    ins.then_inc(score_mm, 1)

            def turn_mixed(n, x):
                pe.wait_ge(mix_sb, Z + n + 1)
                for c in range(DC):
                    ins = pe.transpose(ps[:, 7, D + c * P:D + (c + 1) * P], mixed[:, x % 2, c * P:(c + 1) * P],
                                       core.ident[:, :])
                ins.then_inc(mix_turned, 1)

            def mix_part(n, i, x, u):
                if u == 0:
                    pe.wait_ge(mix_kept, Z + n)
                pe.wait_ge(p_lo_ready, Z + 3 * n + u + 1)
                if x % RT == 0:
                    pe.wait_ge(r_lo_ready, Z + 3 * (2 * i + x // RT) + u + 1)
                for t in range(4 * u, 4 * u + 4):
                    for m, (p, v) in enumerate(((p_hi, r_hi), (p_hi, r_lo), (p_lo, r_hi))):
                        ins = pe.matmul(ps[:, 7, 0:D], p[:, t, :], v[:, t, :],
                                        start=(t == 0 and m == 0), stop=(t == KT - 1 and m == 2))
                ins.then_inc(mix_mm, 1)

            def attention(i, first=False, last=False):
                for x in range(2 * RT):
                    n = i * 2 * RT + x
                    pe.wait_ge(exped, Z + n + 1)
                    for u in range(3):
                        if not (first and x == 0):
                            mix_part(n - 1, i, x - 1, u)
                        pe.wait_ge(p_hi_ready, Z + 3 * n + u)
                        pe.wait_ge(p_lo_ready, Z + 3 * n + u)
                        for y in range(4):
                            t = 4 * u + y
                            ins = pe.transpose(ps[0:KP, 6, y * P:(y + 1) * P],
                                               prob[:, x % 2, t * KP:(t + 1) * KP], core.ident[:, :])
                        ins.then_inc(turned, 1)
                        turn = None
                        if u == 2 and not (first and x == 0):
                            def turn(n=n, x=x):
                                turn_mixed(n - 1, x - 1)
                        if x < 2 * RT - 2:
                            score_part(n + 2, i, x + 2, u, between=turn)
                        elif not last:
                            score_part(n + 2, i + 1, x + 2 - 2 * RT, u, between=turn)
                        elif turn:
                            turn()
                if last:
                    for u in range(3):
                        mix_part(n, i, x, u)
                    turn_mixed(n, x)

            for x in range(2):
                for k in range(3):
                    score_part(x, 0, x, k)
            attention(0, first=True)
            with pe.Fori(1, PAIRS - 1) as i:
                attention(i)
            attention(PAIRS - 1, last=True)

            for a in range(2):
                pe.matmul(ps[:, a, :], zero[0:1, 0:P], zero[0:1, :], start=True, stop=True,
                          skip_group_check=True)
            pe.wait_ge(mix_kept, Z + B * RT)

            def value(n, i, s):
                pe.wait_ge(w_in[s], DMA * (turns + i + 1))
                pe.wait_ge(v_lo_ready, Z + n - 1)
                for c in range(DC):
                    ins = pe.matmul(packed(ps[:, 2 + s % 2, 0:TOK]), w[:, s, c * P:(c + 1) * P],
                                    q_all[:, c, :, bass.ds(n * S, S)], start=(c == 0), stop=(c == DC - 1))
                ins.then_inc(v_mm, 1)

            def output(n, s):
                pe.wait_ge(v_lo_ready, Z + n + 1)
                pe.wait_ge(w_lo_ready, Z + H + n + 1)
                for t in range(PAIRS):
                    for v, wt in split(head_parts, w_parts):
                        ins = pe.matmul(ps[:, t // 2, (t % 2) * D:(t % 2 + 1) * D],
                                        v[:, s % 2, t * P:(t + 1) * P], wt[:, s, D:2 * D],
                                        start=False, stop=False, skip_group_check=True)
                ins.then_inc(out_mm, 1)
            with pe.Fori(0, turns) as i:
                for s in range(WS):
                    value(i * WS + s, i, s)
                    if s:
                        output(i * WS + s - 1, s - 1)
                output(i * WS + WS - 1, WS - 1)

        @block.scalar
        def _(act):
            for x in (w_hi_ready, head_hi_ready, v_hi_ready, exped, q_hi_ready, t_hi_ready, r_hi_ready, p_hi_ready,
                      mix_kept):
                act.sem_inc(x, Z)

            def split_turned(b, s, c):
                act.wait_ge(raw_in, DMA * (2 * b + 1))
                act.wait_ge(score_mm, Z + RT * (b - 1))
                act.copy(t_hi[:, s, c, :], raw_t[:, c, :]).then_inc(t_hi_ready, 1)

            def split_rows(b, u):
                act.wait_ge(raw_in, DMA * (2 * b + 2))
                act.wait_ge(mix_mm, Z + 3 * (RT * b - 1) + u + 1)
                act.copy(r_hi[:, 4 * u:4 * u + 4, :], raw_r[:, 4 * u:4 * u + 4, :]).then_inc(r_hi_ready, 1)

            def split_weights(n, i, s):
                act.wait_ge(w_in[s], DMA * (i + 1))
                act.wait_ge(fold_mm, Z + n - WS + 1)
                act.copy(w_hi[:, s, :], w[:, s, :]).then_inc(w_hi_ready, 1)
            split_weights(0, 0, 0)
            act.wait_ge(core.ln_turned, core.turn_of[k_ln] + 1)
            for c in range(DC):
                act.copy(x_hi[:, c, :], ps[:, c, :]).then_inc(core.ln_cols, 1)

            def queries(n, s):
                act.wait_ge(head_mm, Z + n + 1)
                act.wait_ge(fold_mm, Z + n - 1)
                act.copy(head_hi[:, s % 2, 0:TOK], ps[:, 2 + s % 2, 0:TOK]).then_inc(head_hi_ready, 1)

            def turn(i, first=False, last=False):
                for s in range(WS):
                    n = i * WS + s
                    if not (last and s + 2 >= WS):
                        split_weights(n + 2, i + (s + 2) // WS, (s + 2) % WS)
                    queries(n, s)
                    if first and s < DC:
                        split_turned(0, 0, s)
                    if last and s < 3:
                        split_rows(0, s)
            split_weights(1, 0, 1)
            act.wait_ge(cleared, 2)
            turn(0, first=True)
            with act.Fori(1, turns - 1) as i:
                turn(i)
            turn(turns - 1, last=True)

            def split_queries(n, x):
                act.wait_ge(q_staged, Z + n + 1)
                act.wait_ge(score_mm, Z + n - 1)
                act.copy(q_hi[:, x % 2, :, :], q_tile[:, x % 2, :, :]).then_inc(q_hi_ready, 1)

            def exp(n, x):
                act.wait_ge(maxed, Z + n + 1)
                act.wait_ge(turned, Z + 3 * (n - 1))
                act.activation(prob[:, x % 2, :].rearrange("p (k n) -> p k n", k=3),
                               ps[:, 3 * (x % 2):3 * (x % 2) + 3, 0:KN], ACT.Exp,
                               bias=neg_max[:, x % 2:x % 2 + 1],
                               accum_out=sums[:, x % 2:x % 2 + 1]).then_inc(exped, 1)

            def keep_mixed(i, x, n):
                act.wait_ge(mix_turned, Z + n + 1)
                act.copy(query_tile(i, x), ps[:, 7, D:2 * D].rearrange("p (c n) -> p c n", c=DC)) \
                    .then_inc(mix_kept, 1)

            def attention(i, first=False, last=False):
                for x in range(2 * RT):
                    n = i * 2 * RT + x
                    b, r = x // RT, x % RT
                    for u in range(3):
                        act.wait_ge(turned, Z + 3 * n + u + 1)
                        act.wait_ge(mix_mm, Z + 3 * n + u - 2)
                        act.copy(p_hi[:, 4 * u:4 * u + 4, :].rearrange("p t n -> p (t n)"),
                                 ps[0:KP, 6, :]).then_inc(p_hi_ready, 1)
                        if u == 2 and not (first and x == 0):
                            keep_mixed(i, x - 1, n - 1)
                        if u == 0 and not (last and x == 2 * RT - 1):
                            exp(n + 1, x + 1)
                        if u == 1 and not (last and x + 3 >= 2 * RT):
                            split_queries(n + 3, x + 3)
                        if r == 0 and not (first and x == 0):
                            split_rows(2 * i + b, u)
                    if r in (2, 3) and not (last and b == 1):
                        split_turned(2 * i + b + 1, 1 - b, r - 2)
                if last:
                    keep_mixed(i, x, n)
            for x in range(2):
                split_queries(x, x)
            exp(0, 0)
            split_queries(2, 2)
            attention(0, first=True)
            with act.Fori(1, PAIRS - 1) as i:
                attention(i)
            attention(PAIRS - 1, last=True)
            with act.Fori(0, turns) as i:
                for s in range(WS):
                    n = i * WS + s
                    act.wait_ge(w_in[s], DMA * (turns + i + 1))
                    act.wait_ge(out_mm, Z + n - WS + 1)
                    act.copy(w_hi[:, s, D:2 * D], w[:, s, D:2 * D]).then_inc(w_hi_ready, 1)
                    act.wait_ge(v_mm, Z + n + 1)
                    act.wait_ge(out_mm, Z + n - 1)
                    act.copy(unpad(head_hi[:, s % 2, :]), packed(ps[:, 2 + s % 2, 0:TOK])) \
                        .then_inc(v_hi_ready, 1)

        @block.vector
        def _(dve):
            link = InOrder(dve, core.dve_step, dve0)
            for x in (x_lo_ready, w_lo_ready, head_lo_ready, v_lo_ready, fold_sb, maxed, q_lo_ready, t_lo_ready,
                      r_lo_ready, p_lo_ready, mix_sb):
                dve.sem_inc(x, Z)
            core.ln_vector(dve, link, k_ln)

            def split_weights(n, s):
                dve.wait_ge(w_hi_ready, Z + n + 1)
                dve.tensor_tensor(w_lo[:, s, :], w[:, s, :], w_hi[:, s, :].bitcast(F32),
                                  ALU.subtract).then_inc(w_lo_ready, 1)

            def queries(n, s):
                dve.wait_ge(head_hi_ready, Z + n + 1)
                dve.tensor_tensor(head_lo[:, s % 2, 0:TOK], ps[:, 2 + s % 2, 0:TOK],
                                  head_hi[:, s % 2, 0:TOK].bitcast(F32), ALU.subtract).then_inc(head_lo_ready, 1)
            split_weights(0, 0)
            link(dve.memset(zero[:, :], 0.0))
            for part in head_parts:
                dve.memset(part[:, :, :].bitcast(F32), 0.0).then_inc(cleared, 1)
            for c in range(DC):
                dve.wait_ge(core.ln_cols, core.cols_ready(k_ln) - DC + c + 1)
                dve.tensor_tensor(x_lo[:, c, :], ps[:, c, :], x_hi[:, c, :].bitcast(F32),
                                  ALU.subtract).then_inc(x_lo_ready, 1)
            split_weights(1, 1)

            def split_turned(b, s, c):
                dve.wait_ge(t_hi_ready, Z + 2 * b + c + 1)
                dve.tensor_tensor(t_lo[:, s, c, :], raw_t[:, c, :], t_hi[:, s, c, :].bitcast(F32),
                                  ALU.subtract).then_inc(t_lo_ready, 1)

            def split_rows(b, u):
                dve.wait_ge(r_hi_ready, Z + 3 * b + u + 1)
                dve.tensor_tensor(r_lo[:, 4 * u:4 * u + 4, :], raw_r[:, 4 * u:4 * u + 4, :],
                                  r_hi[:, 4 * u:4 * u + 4, :].bitcast(F32), ALU.subtract).then_inc(r_lo_ready, 1)

            def folded(n, s):
                dve.wait_ge(fold_mm, Z + n + 1)
                for c in range(DC):
                    ins = dve.tensor_scalar(q_all[:, c, :, bass.ds(n * S, S)],
                                            packed(ps[:, 4 + 2 * (s % 2) + c, 0:TOK]), scale, None, ALU.mult)
                ins.then_inc(fold_sb, 1)

            def turn(i, first=False, last=False):
                for s in range(WS):
                    n = i * WS + s
                    queries(n, s)
                    if not (first and s == 0):
                        folded(n - 1, (s - 1) % WS)
                    if not (last and s + 2 >= WS):
                        split_weights(n + 2, (s + 2) % WS)
                    if first and s < DC:
                        split_turned(0, 0, s)
                    if last and s < 3:
                        split_rows(0, s)
            turn(0, first=True)
            with dve.Fori(1, turns - 1) as i:
                turn(i)
            turn(turns - 1, last=True)
            folded(H - 1, WS - 1)

            def split_queries(n, x):
                dve.wait_ge(q_hi_ready, Z + n + 1)
                dve.tensor_tensor(q_lo[:, x % 2, :, :], q_tile[:, x % 2, :, :], q_hi[:, x % 2, :, :].bitcast(F32),
                                  ALU.subtract).then_inc(q_lo_ready, 1)

            def row_max(n, x):
                dve.wait_ge(score_mm, Z + n + 1)
                dve.wait_ge(exped, Z + n - 1)
                dve.tensor_reduce(neg_max[:, x % 2:x % 2 + 1], ps[:, 3 * (x % 2):3 * (x % 2) + 3, 0:KN],
                                  AXIS.XY, ALU.max, negate=True).then_inc(maxed, 1)

            def keep(n, x):
                dve.wait_ge(mix_mm, Z + 3 * n + 3)
                dve.tensor_scalar(mixed[:, x % 2, :], ps[:, 7, 0:D], inv[:, x % 2:x % 2 + 1], None,
                                  ALU.mult).then_inc(mix_sb, 1)

            def attention(i, first=False, last=False):
                for x in range(2 * RT):
                    n = i * 2 * RT + x
                    b, r = x // RT, x % RT
                    dve.wait_ge(exped, Z + n + 1)
                    dve.wait_ge(mix_sb, Z + n - 1)
                    link(dve.reciprocal(inv[:, x % 2:x % 2 + 1], sums[:, x % 2:x % 2 + 1]))
                    if not (last and x == 2 * RT - 1):
                        row_max(n + 1, x + 1)
                    for u in range(3):
                        if u == 2 and not (first and x == 0):
                            keep(n - 1, x - 1)
                        dve.wait_ge(p_hi_ready, Z + 3 * n + u + 1)
                        p4 = slice(4 * u, 4 * u + 4)
                        dve.tensor_tensor(p_lo[:, p4, :].rearrange("p t n -> p (t n)"), ps[0:KP, 6, :],
                                          p_hi[:, p4, :].rearrange("p t n -> p (t n)").bitcast(F32),
                                          ALU.subtract).then_inc(p_lo_ready, 1)
                        if u == 1 and not (last and x + 3 >= 2 * RT):
                            split_queries(n + 3, x + 3)
                        if r == 0 and u < 2 and not (first and x == 0):
                            split_rows(2 * i + b, u)
                        if r == 1 and u == 0 and not (first and x == 1):
                            split_rows(2 * i + b, 2)
                        if r in (3, 4) and u == 0 and not (last and b == 1):
                            split_turned(2 * i + b + 1, 1 - b, r - 3)
                if last:
                    keep(n, x)
            for x in range(2):
                split_queries(x, x)
            row_max(0, 0)
            split_queries(2, 2)
            before = link.n
            attention(0, first=True)
            with dve.Fori(1, PAIRS - 1) as i:
                link.loop(i, before, 2 * RT)
                attention(i)
            link.end(before, 2 * RT, PAIRS - 1)
            attention(PAIRS - 1, last=True)
            with dve.Fori(0, turns) as i:
                for s in range(WS):
                    n = i * WS + s
                    dve.wait_ge(w_hi_ready, Z + H + n + 1)
                    dve.tensor_tensor(w_lo[:, s, D:2 * D], w[:, s, D:2 * D], w_hi[:, s, D:2 * D].bitcast(F32),
                                      ALU.subtract).then_inc(w_lo_ready, 1)
                    dve.wait_ge(v_hi_ready, Z + n + 1)
                    dve.tensor_tensor(unpad(head_lo[:, s % 2, :]), packed(ps[:, 2 + s % 2, 0:TOK]),
                                      unpad(head_hi[:, s % 2, :]).bitcast(F32), ALU.subtract) \
                        .then_inc(v_lo_ready, 1)
            dve.wait_ge(out_mm, Z + H)
            for a in range(2):
                rows = core.x_rows[:, 2 * a:2 * a + 2, :].rearrange("p i d -> p (i d)")
                link(dve.tensor_tensor(rows, rows, ps[:, a, :], ALU.add))
            core.dve_n = link.n


PACK = 4 * P + D + P
SLOTS = 4


def moe(core, tag, experts, top_k, tiles, shared_gate, per_owner, fp8=None):
    nc, dram, ps = core.nc, core.dram, core.psum
    k_ln = core.new_norm()
    dve0, pool0 = core.dve_n, core.pool_n
    ne = experts + 1
    nl = experts + int(shared_gate)
    ctx = ExitStack()
    with ctx:
        def sb(name, shape, dt=F32):
            return ctx.enter_context(nc.sbuf_tensor(tag + name, shape, dt))
        w_gate = sb("gate", [P, DC, nl])
        w = sb("w", [P, SLOTS, PACK])
        before = sb("before", [P, experts, experts])
        zero = sb("zero", [1, 512])
        gate_silu = sb("gate_silu", [P, 2, TOK])
        prod = sb("prod", [P, 2, TOK])
        hid = sb("hid", [P, 2, T])
        x_hi = sb("x_hi", [P, DC, T], F32R)
        x_lo = sb("x_lo", [P, DC, T], F32R)
        w_hi = sb("w_hi", [P, SLOTS, PACK], F32R)
        w_lo = sb("w_lo", [P, SLOTS, 4 * P + D], F32R)
        hid_hi = sb("hid_hi", [P, 2, T], F32R)
        hid_lo = sb("hid_lo", [P, 2, T], F32R)
        comb_hi = sb("comb_hi", [ne, T], F32R)
        comb_lo = sb("comb_lo", [ne, T], F32R)
        top = sb("top", [P, PAIRS])
        logit = sb("logit", [P, PAIRS, nl])
        prob = sb("prob", [P, PAIRS, experts])
        sig = sb("sig", [P, PAIRS])
        gt = sb("gt", [P, PAIRS, experts * experts])
        eq = sb("eq", [P, PAIRS, experts * experts])
        rank = sb("rank", [P, PAIRS, experts])
        total = sb("total", [P, PAIRS])
        combine = sb("combine", [P, PAIRS, ne])
        sem = core.sem
        gate_in = sem(tag + "gate_in")
        w_in = [sem(f"{tag}w_in{s}") for s in range(SLOTS)]
        (gate_mm, maxed, exped, combined, comb_turned, comb_hi_ready, comb_lo_ready, x_hi_ready, x_lo_ready,
         w_hi_ready, w_lo_ready, up_mm, silued, product, scaled, hid_hi_ready, hid_lo_ready, owner_mm,
         down_mm, cleared) = (sem(tag + n) for n in (
            "gate_mm", "maxed", "exped", "combined", "comb_turned", "comb_hi_ready", "comb_lo_ready",
            "x_hi_ready", "x_lo_ready", "w_hi_ready", "w_lo_ready", "up_mm", "silued", "product", "scaled",
            "hid_hi_ready", "hid_lo_ready", "owner_mm", "down_mm", "cleared"))

        def tok(x, c):
            return unpad(x[:, c, :])

        def split(x, y):
            (x_h, x_l), (y_h, y_l) = x, y
            return (x_h, y_h), (x_h, y_l), (x_l, y_h)
        turns = tiles // SLOTS
        block = ctx.enter_context(nc.Block())

        @block.sync
        def _(sp):
            sp.dma_start(w_gate[:, :, :], dram[tag + "gate"]).then_inc(gate_in, DMA)
            sp.dma_start(before[:, :, :], dram[tag + "before"]).then_inc(gate_in, DMA)
            for s in range(SLOTS):
                sp.dma_start(w[:, s, :], dram[tag + "pack"][s]).then_inc(w_in[s], DMA)
            if fp8:
                fp8.load(sp)
            with sp.Fori(1, turns) as i:
                for s in range(SLOTS):
                    sp.wait_ge(w_hi_ready, (i - 1) * SLOTS + s + 1)
                    sp.wait_ge(w_lo_ready, (i - 1) * SLOTS + s + 1)
                    sp.dma_start(w[:, s, :], dram[tag + "pack"][i * SLOTS + s]).then_inc(w_in[s], DMA)

        @block.gpsimd
        def _(pool):
            core.ln_pool(pool, k_ln)
            if fp8:
                link = InOrder(pool, core.pool_step, pool0)
                fp8.gather(pool)
                fp8.round(pool, link)
                core.pool_n = link.n

        @block.tensor
        def _(pe):
            core.ln_tensor(pe, k_ln)
            pe.wait_ge(core.ln_cols, core.cols_ready(k_ln))
            pe.wait_ge(gate_in, 2 * DMA)
            for t in range(PAIRS):
                for c in range(DC):
                    ins = pe.matmul(ps[:, 7, t * nl:(t + 1) * nl], core.xn_cols[:, c, t * P:(t + 1) * P],
                                    w_gate[:, c, :], start=(c == 0), stop=(c == DC - 1))
            ins.then_inc(gate_mm, 1)

            def up(n, s, first=False):
                pe.wait_ge(w_lo_ready, n + 1)
                if not first:
                    pe.wait_ge(silued, n - 1)
                    pe.wait_ge(product, n - 1)
                for k in range(2):
                    for c in range(DC):
                        at = slice((2 * k + c) * P, (2 * k + c + 1) * P)
                        for m, (wt, xt) in enumerate(split((w_hi, w_lo), (x_hi, x_lo))):
                            ins = pe.matmul(packed(ps[:, 2 + 2 * k + s % 2, 0:TOK]), wt[:, s, at], tok(xt, c),
                                            start=(c == 0 and m == 0), stop=(c == DC - 1 and m == 2))
                ins.then_inc(up_mm, 1)

            def owner(n, s, first=False):
                if not first:
                    pe.wait_ge(scaled, n)
                for m, part in enumerate((comb_hi, comb_lo)):
                    ins = pe.matmul(packed(ps[:, 6, 0:TOK]), w_hi[0:ne, s, 4 * P + D:], unpad(part[:, :]),
                                    start=(m == 0), stop=(m == 1))
                ins.then_inc(owner_mm, 1)

            def down(n, s):
                pe.wait_ge(hid_lo_ready, n + 1)
                for t in range(PAIRS):
                    for h, wt in split((hid_hi, hid_lo), (w_hi, w_lo)):
                        ins = pe.matmul(ps[:, t // 2, (t % 2) * D:(t % 2 + 1) * D],
                                        h[:, s % 2, t * P:(t + 1) * P], wt[:, s, 4 * P:4 * P + D],
                                        start=False, stop=False, skip_group_check=True)
                ins.then_inc(down_mm, 1)

            pe.wait_ge(x_lo_ready, DC)
            up(0, 0, first=True)
            up(1, 1, first=True)
            pe.wait_ge(cleared, 1)
            for a in range(2):
                pe.matmul(ps[:, a, :], zero[0:1, 0:P], zero[0:1, :], start=True, stop=True,
                          skip_group_check=True)
            up(2, 2)
            pe.wait_ge(combined, 1)
            for t in range(PAIRS):
                ins = pe.transpose(ps[0:ne, 7, t * P:(t + 1) * P], combine[:, t, :], core.ident[:, :])
            ins.then_inc(comb_turned, 1)
            up(3, 3)
            pe.wait_ge(comb_lo_ready, 1)
            owner(0, 0, first=True)
            for n in range(1, SLOTS):
                if n % per_owner == 0:
                    owner(n, n)
                down(n - 1, n - 1)
            with pe.Fori(1, turns) as i:
                for s in range(SLOTS):
                    n = i * SLOTS + s
                    up(n, s)
                    if s % per_owner == 0:
                        owner(n, s)
                    down(n - 1, (s - 1) % SLOTS)
            down(tiles - 1, SLOTS - 1)

        @block.scalar
        def _(act):
            core.ln_scalar(act, k_ln)
            for c in range(DC):
                act.wait_ge(core.ln_cols, core.cols_ready(k_ln) - DC + c + 1)
                act.copy(x_hi[:, c, :], core.xn_cols[:, c, :]).then_inc(x_hi_ready, 1)

            def split_weights(n, i, s):
                act.wait_ge(w_in[s], DMA * (i + 1))
                if not (isinstance(n, int) and n < SLOTS):
                    act.wait_ge(down_mm, n - SLOTS + 1)
                act.copy(w_hi[:, s, :], w[:, s, :]).then_inc(w_hi_ready, 1)
            split_weights(0, 0, 0)
            split_weights(1, 0, 1)
            split_weights(2, 0, 2)
            act.wait_ge(maxed, 1)
            act.activation(prob[:, :, :], prob[:, :, :], ACT.Exp).then_inc(exped, 1)
            if shared_gate:
                act.activation(sig[:, :], logit[:, :, experts], ACT.Sigmoid).then_inc(exped, 1)

            def silu(n, s, first=False):
                act.wait_ge(up_mm, n + 1)
                if not first:
                    act.wait_ge(product, n - 1)
                act.activation(gate_silu[:, s % 2, :], ps[:, 2 + s % 2, 0:TOK], ACT.Silu).then_inc(silued, 1)

            def hidden(n, s, first=False):
                act.wait_ge(scaled, n + 1)
                if not first:
                    act.wait_ge(down_mm, n - 1)
                act.copy(hid_hi[:, s % 2, :], hid[:, s % 2, :]).then_inc(hid_hi_ready, 1)
            silu(0, 0, first=True)
            silu(1, 1, first=True)
            split_weights(3, 0, 3)
            act.wait_ge(comb_turned, 1)
            act.copy(comb_hi[:, :], ps[0:ne, 7, :]).then_inc(comb_hi_ready, 1)
            for n in range(SLOTS):
                if n >= 2:
                    silu(n, n)
                    split_weights(n + 2, 1, (n + 2) % SLOTS)
                hidden(n, n, first=(n < 2))
            with act.Fori(1, turns - 1) as i:
                for s in range(SLOTS):
                    n = i * SLOTS + s
                    silu(n, s)
                    split_weights(n + 2, i + (s + 2) // SLOTS, (s + 2) % SLOTS)
                    hidden(n, s)
            for n in range(tiles - SLOTS, tiles):
                silu(n, n % SLOTS)
                if n + 2 < tiles:
                    split_weights(n + 2, (n + 2) // SLOTS, (n + 2) % SLOTS)
                hidden(n, n % SLOTS)

        @block.vector
        def _(dve):
            link = InOrder(dve, core.dve_step, dve0)
            dve.memset(zero[:, :], 0.0).then_inc(cleared, 1)
            core.ln_vector(dve, link, k_ln)
            link(dve.memset(hid[:, :, :], 0.0))

            def split_weights(n, s):
                dve.wait_ge(w_hi_ready, n + 1)
                dve.tensor_tensor(w_lo[:, s, :], w[:, s, 0:4 * P + D], w_hi[:, s, 0:4 * P + D].bitcast(F32),
                                  ALU.subtract).then_inc(w_lo_ready, 1)

            def product_of(n, s):
                dve.wait_ge(silued, n + 1)
                dve.tensor_tensor(prod[:, s % 2, :], gate_silu[:, s % 2, :], ps[:, 4 + s % 2, 0:TOK],
                                  ALU.mult).then_inc(product, 1)
            for c in range(DC):
                dve.wait_ge(x_hi_ready, c + 1)
                dve.tensor_tensor(x_lo[:, c, :], core.xn_cols[:, c, :], x_hi[:, c, :].bitcast(F32),
                                  ALU.subtract).then_inc(x_lo_ready, 1)
            split_weights(0, 0)
            split_weights(1, 1)
            dve.wait_ge(gate_mm, 1)
            link(dve.tensor_copy(logit[:, :, :].rearrange("p t e -> p (t e)"), ps[:, 7, 0:PAIRS * nl]))
            link(dve.tensor_reduce(top[:, :], logit[:, :, 0:experts], AXIS.X, ALU.max))
            dve.tensor_tensor(prob[:, :, :], logit[:, :, 0:experts],
                              top[:, :].unsqueeze(2).to_broadcast([P, PAIRS, experts]),
                              ALU.subtract).then_inc(maxed, 1)
            split_weights(2, 2)
            dve.wait_ge(exped, 1)
            mine = prob[:, :, :].unsqueeze(3).to_broadcast([P, PAIRS, experts, experts])
            other = prob[:, :, :].unsqueeze(2).to_broadcast([P, PAIRS, experts, experts])
            first_of_two = before[:, :, :].unsqueeze(1).to_broadcast([P, PAIRS, experts, experts])
            g4 = gt[:, :, :].rearrange("p t (a b) -> p t a b", b=experts)
            e4 = eq[:, :, :].rearrange("p t (a b) -> p t a b", b=experts)
            link(dve.tensor_tensor(g4, other, mine, ALU.is_gt))
            link(dve.tensor_tensor(e4, other, mine, ALU.is_equal))
            link(dve.tensor_tensor(e4, e4, first_of_two, ALU.mult))
            link(dve.tensor_tensor(g4, g4, e4, ALU.add))
            link(dve.tensor_reduce(rank[:, :, :], g4, AXIS.X, ALU.add))
            for n in range(2):
                product_of(n, n)
            link(dve.tensor_scalar(rank[:, :, :], rank[:, :, :], float(top_k), None, ALU.is_lt))
            link(dve.tensor_tensor(prob[:, :, :], prob[:, :, :], rank[:, :, :], ALU.mult))
            link(dve.tensor_reduce(total[:, :], prob[:, :, :], AXIS.X, ALU.add))
            link(dve.reciprocal(total[:, :], total[:, :]))
            if shared_gate:
                dve.wait_ge(exped, 2)
                link(dve.tensor_copy(combine[:, :, experts], sig[:, :]))
            else:
                link(dve.memset(combine[:, :, experts], 1.0))
            dve.tensor_tensor(combine[:, :, 0:experts], prob[:, :, :],
                              total[:, :].unsqueeze(2).to_broadcast([P, PAIRS, experts]),
                              ALU.mult).then_inc(combined, 1)
            split_weights(3, 3)
            dve.wait_ge(comb_hi_ready, 1)
            dve.tensor_tensor(comb_lo[:, :], ps[0:ne, 7, :], comb_hi[:, :].bitcast(F32),
                              ALU.subtract).then_inc(comb_lo_ready, 1)

            def gated(n, i, s, more=True, early=False):
                if not early:
                    product_of(n, s)
                dve.wait_ge(product, n + 1)
                dve.wait_ge(owner_mm, n + 1 if per_owner == 1 else i + 1)
                dve.tensor_tensor(unpad(hid[:, s % 2, :]), packed(prod[:, s % 2, :]), packed(ps[:, 6, 0:TOK]),
                                  ALU.mult).then_inc(scaled, 1)
                if more:
                    split_weights(n + 2, (s + 2) % SLOTS)
                dve.wait_ge(hid_hi_ready, n + 1)
                dve.tensor_tensor(hid_lo[:, s % 2, :], hid[:, s % 2, :], hid_hi[:, s % 2, :].bitcast(F32),
                                  ALU.subtract).then_inc(hid_lo_ready, 1)
            for n in range(SLOTS):
                gated(n, 0, n, more=(n >= 2), early=(n < 2))
                if fp8 and n == 0:
                    fp8.find_scales(dve, link)
                if fp8 and n == 2:
                    fp8.divide(dve, link, 1)
                    fp8.find_exponents(dve, 1)
            split_turns = 1 + (2 * FT2 // SLOTS if fp8 else 0)
            if fp8:
                before_loop = link.n
                with dve.Fori(1, split_turns) as i:
                    link.loop(i - 1, before_loop, SLOTS)
                    for s in range(SLOTS):
                        gated(i * SLOTS + s, i, s)
                        fp8.scale_tile(dve, link, (i - 1) * SLOTS + s)
                link.end(before_loop, SLOTS, split_turns - 1)
            with dve.Fori(split_turns, turns - 1) as i:
                for s in range(SLOTS):
                    gated(i * SLOTS + s, i, s)
            for n in range(tiles - SLOTS, tiles):
                gated(n, n // SLOTS, n % SLOTS, more=(n + 2 < tiles))
            dve.wait_ge(down_mm, tiles)
            for a in range(2):
                rows = core.x_rows[:, 2 * a:2 * a + 2, :].rearrange("p i d -> p (i d)")
                link(dve.tensor_tensor(rows, rows, ps[:, a, :], ALU.add))
            core.dve_n = link.n


E1, K1, I1, SI1 = 16, 4, 176, 704
TILES1 = -(-(E1 * I1 + SI1) // P)
E3, K3, I3 = 8, 2, 512
TILES3 = (E3 + 1) * I3 // P


def moe_1(core):
    moe(core, "m1_", E1, K1, TILES1, shared_gate=True, per_owner=1, fp8=core.fp8_weights)


def moe_3(core):
    moe(core, "m3_", E3, K3, TILES3, shared_gate=False, per_owner=SLOTS)


def chunks(w, p=P):
    return w.reshape(w.shape[0] // p, p, w.shape[1]).transpose(1, 0, 2)


def rope_tables(length):
    half = R // 2
    freq = (1.0 / 10000.0 ** (np.arange(half, dtype=np.float32) / np.float32(half))).astype(np.float32)
    ang = np.arange(length, dtype=np.float32)[:, None] * freq
    cos, sin = np.cos(ang), np.sin(ang)
    return (np.concatenate([cos, cos], 1).astype(np.float32),
            np.concatenate([-sin, sin], 1).astype(np.float32))


def layouts(a):
    out = {"x": a["x"], "c_ident": np.eye(P, dtype=np.float32)}
    seg = a["itok_BxS_0_1023"].reshape(B, GROUPS, GQ)
    out["seg_k"] = np.repeat(seg.transpose(2, 0, 1).reshape(GQ, B * GROUPS), WIN, axis=0)
    out["seg_r"] = np.tile(seg.transpose(2, 0, 1).reshape(GQ, B * GROUPS), (HH, 1))
    win = np.arange(WIN, dtype=np.float32) - (WIN - 1)
    out["c_win_k"] = np.tile(win, GQ)[:, None]
    out["c_seq_row"] = np.tile(np.repeat(np.arange(B, dtype=np.float32) * LK, GROUPS), (GR, 1))
    out["c_win_r"] = np.tile(win, (ROW0, 1))
    own = np.tile(np.arange(GQ), HH)[:, None] == np.repeat(np.arange(GQ), WIN)[None, :]
    out["c_diag"] = np.where(own, 0.0, NEG).astype(np.float32)
    cos, sin = rope_tables(LK)
    ctx = a["ctx_2048"]
    table = np.broadcast_to(np.concatenate([sin, cos], 1)[None], (B, LK, 2 * R))
    out["ctx_rope"] = np.concatenate([ctx, table], 2).reshape(B * LK, D + 2 * R)
    out["c_rope_q"] = np.tile(np.stack([cos[:S].T, sin[:S].T], 1), (2, 1, 1))

    def swap(w):
        w = w.reshape(w.shape[0], -1, 2, R // 2)
        return w[:, :, ::-1, :].reshape(w.shape[0], -1)
    out["w_kvc"] = chunks(a["L0_xattn_W_kvc"])
    out["w_kvc_t"] = a["L0_xattn_W_kvc"].T
    out["w_kr2"] = np.concatenate([a["L0_xattn_W_kr"], swap(a["L0_xattn_W_kr"])], 1)
    out["w_dq"] = chunks(a["L0_xattn_W_dq"])
    out["w_uq_t"] = a["L0_xattn_W_uq"].reshape(QC, H, HD).transpose(2, 1, 0)
    out["w_uk_t"] = a["L0_xattn_W_uk"].reshape(KVC, H, HD).transpose(2, 1, 0)
    out["w_uv_t"] = a["L0_xattn_W_uv"].reshape(KVC, H, HD).transpose(2, 1, 0)
    out["w_qr"] = np.stack([a["L0_xattn_W_qr"], swap(a["L0_xattn_W_qr"])], 1)
    out["w_o"] = a["L0_xattn_W_o"].reshape(H, HD, D).transpose(1, 0, 2)
    out["f_w1"] = chunks(a["L0_ffn_W1"].T)
    out["f_w2"] = chunks(a["L0_ffn_W2"].T)
    out["ctx_r"] = ctx.reshape(B, KP, KT, D)
    out["ctx_t"] = ctx.reshape(B, KP, KT, DC, P).transpose(0, 4, 3, 2, 1).reshape(B, P, DC, LK)
    out["c_mask"] = a["mask_BxS2_bk0"].reshape(B, KP, KT).transpose(0, 2, 1).reshape(B, LK).view(np.int32)
    out["c_mask2"] = a["mask_BxS2_ff1"].reshape(B, KP, KT).transpose(1, 0, 2)
    out["c_w_k"] = chunks(a["L2_xattn_Wk"].T)
    out["c_w_v"] = chunks(a["L2_xattn_Wv"].T)
    out["c_b_k"] = a["L2_xattn_bk"].reshape(2, P).T

    def block_diagonal(w):
        out = np.zeros((8, HD2, 8, FD2), np.float32)
        out[np.arange(8), :, np.arange(8), :] = w.T
        return out.reshape(P, FG)
    out["c_w_kf"] = block_diagonal(a["L2_xattn_Wkf"])
    out["l_w_q"] = chunks(a["L2_xattn_Wq"].T)
    out["l_w_o"] = chunks(a["L2_xattn_Wo"].T)
    out["l_w_qf"] = block_diagonal(a["L2_xattn_Wqf"])
    out["l_b_q"] = a["L2_xattn_bq"].reshape(2, P).T
    out["l_b_v"] = a["L2_xattn_bv"]
    out["l_b_o"] = a["L2_xattn_bo"]
    order = np.pad(a["L2_ffn_down_reorder_index"], (0, FT2 * P - FF2))
    out["q_order"] = order.reshape(FT2, P).T
    out["q_w_gate"] = a["L2_ffn_w_gate"]
    out["q_w_up"] = a["L2_ffn_w_up"]
    out["q_w_down"] = a["L2_ffn_w_down"].reshape(DC, P, FF2).transpose(1, 0, 2)
    wq = a["L3_xattn_Wq"].reshape(DC, P, H, HD).transpose(2, 1, 0, 3).reshape(H, P, D)
    wk = a["L3_xattn_Wk"].reshape(D, H, HD).transpose(1, 2, 0)
    wv = a["L3_xattn_Wv"].reshape(DC, P, H, HD).transpose(2, 1, 0, 3).reshape(H, P, D)
    wo = a["L3_xattn_Wo"].reshape(H, HD, D)
    out["a_w"] = np.concatenate([np.concatenate([wq, wk], 2), np.concatenate([wv, wo], 2)])

    def pack(gate, up, down, owner, tiles, experts):
        pad = tiles * P - len(gate)
        gate, up, down = (np.pad(w, ((0, pad), (0, 0))) for w in (gate, up, down))
        one = np.zeros((P, tiles * P), np.float32)
        one[owner, np.arange(len(owner))] = 1.0
        up_in = np.stack([gate, up]).reshape(2, tiles, P, DC, P).transpose(1, 4, 0, 3, 2)
        return np.concatenate([up_in.reshape(tiles, P, 4 * P), down.reshape(tiles, P, D),
                               one.reshape(P, tiles, P).transpose(1, 0, 2)], 2)

    def before(n):
        return np.tile((np.arange(n)[None, :] < np.arange(n)[:, None]).astype(np.float32), (P, 1, 1))
    gu, dn = a["L1_ffn_expert_gate_up"], a["L1_ffn_expert_down"]
    sgu, sdn = a["L1_ffn_shared_gate_up"], a["L1_ffn_shared_down"]
    out["m1_pack"] = pack(np.concatenate([gu[:, :I1].reshape(-1, D), sgu[:SI1]]),
                          np.concatenate([gu[:, I1:].reshape(-1, D), sgu[SI1:]]),
                          np.concatenate([dn.transpose(0, 2, 1).reshape(-1, D), sdn.T]),
                          np.concatenate([np.repeat(np.arange(E1), I1), np.full(SI1, E1)]), TILES1, E1)
    out["m1_gate"] = chunks(np.concatenate([a["L1_ffn_gate_w"], a["L1_ffn_shared_gate_vec"]]).T)
    out["m1_before"] = before(E1)
    gu, dn = a["L3_ffn_w_gate_up"].transpose(0, 2, 1), a["L3_ffn_w_down"]
    sgu, sdn = a["L3_ffn_shared_gate_up"].T, a["L3_ffn_shared_down"]
    out["m3_pack"] = pack(np.concatenate([gu[:, :I3].reshape(-1, D), sgu[:I3]]),
                          np.concatenate([gu[:, I3:].reshape(-1, D), sgu[I3:]]),
                          np.concatenate([dn.reshape(-1, D), sdn]),
                          np.repeat(np.arange(E3 + 1), I3), TILES3, E3)
    out["m3_gate"] = chunks(a["L3_ffn_gate_w"])
    out["m3_before"] = before(E3)
    return {k: np.ascontiguousarray(v) for k, v in out.items()}


def program(nc, dram):
    with ExitStack() as ctx:
        core = Core(nc, ctx, dram)
        setup(core)
        with ExitStack() as early:
            for stage in STAGES_A:
                if stage is memory_attention_and_features:
                    core.open_kv_sums(early)
                if stage is moe_1:
                    core.open_fp8_weights(early)
                stage(core)
                if stage is moe_1:
                    core.retire_sems()
        for stage in STAGES_B:
            stage(core)
        store(core)


STAGES_A = [window_attention, lookup_ffn, memory_attention_and_features, moe_1, linear_attention, quantised_ffn]
STAGES_B = [full_attention, moe_3]


def kernel(**inputs):
    import numpy as _np
    import concourse.bacc as _bacc
    from concourse import mybir as _mybir
    from concourse.bass_utils import run_bass_kernel_spmd as _run

    nc = _bacc.Bacc("TRN2", target_bir_lowering=False, num_devices=1)
    arrays, dram = {}, {}
    for name, a in layouts({k: _np.asarray(v) for k, v in inputs.items()}).items():
        arrays[f"in_{name}"] = a
        dram[name] = nc.dram_tensor(f"in_{name}", a.shape, _mybir.dt.from_np(a.dtype),
                                    kind="ExternalInput").ap()
    dram["out"] = nc.dram_tensor("out_0", (B, S, D), _mybir.dt.float32, kind="ExternalOutput").ap()
    program(nc, dram)
    r = _run(nc, [arrays], core_ids=[0])
    return r.results[0]["out_0"]
```
